# Optimizing a Trainium2 kernel written in Bass

```python
import numpy as np
import jax
import jax.numpy as jnp

def _softmax(x, axis=-1):
    return jax.nn.softmax(x, axis=axis)

def _gelu(x):
    return jax.nn.gelu(x, approximate=True)

def _silu(x):
    return jax.nn.silu(x)

def _sigmoid(x):
    return jax.nn.sigmoid(x)

def _layernorm(x, axis=-1, eps=1e-05):
    m = jnp.mean(x, axis=axis, keepdims=True)
    v = jnp.var(x, axis=axis, keepdims=True)
    return (x - m) / jnp.sqrt(v + eps)

def _scatter_add(tgt, idx, src, axis=0):
    return tgt.at[idx].add(src)

def _segment_sum(src, seg, n):
    return jax.ops.segment_sum(src, seg, n)
kernel_name = 'mk_gnn_resnorm_d2_gnn_r32_50ed41'

def setup_inputs(seed: int=0):
    np.random.seed(seed)
    _w = jnp.asarray

    def _rec_inputs():
        import jax
        import jax.numpy as jnp
        _gk = jax.random.key(seed)
        x = -0.0003713 + 1 * jax.random.normal(jax.random.fold_in(_gk, 1), (3125, 128), jnp.float32)
        _s = jax.random.randint(jax.random.fold_in(_gk, 2), (25000,), 0, 3125, jnp.int32)
        _d = jax.random.randint(jax.random.fold_in(_gk, 3), (25000,), 0, 3125, jnp.int32)
        _loop = jnp.arange(3125, dtype=jnp.int32)
        src = jnp.concatenate([_s, _d, _loop])
        dst = jnp.concatenate([_d, _s, _loop])
        _o = jnp.argsort(dst, stable=True)
        src = src[_o]
        dst = dst[_o]
        edge_attr_128 = -8.513e-05 + 0.999844 * jax.random.normal(jax.random.fold_in(_gk, 13), (53125, 128), jnp.float32)
        return (x, src, dst, edge_attr_128)
    x, src, dst, edge_attr_128 = _rec_inputs()

    def _L0_gnn_setup():
        import jax, jax.numpy as jnp
        import numpy as np
        N, E, D, H = (3125, 20000, 128, 256)

        def _mlp(x, w1, b1, w2, b2, w3, b3):
            x = jax.nn.relu(x @ w1.T + b1)
            x = jax.nn.relu(x @ w2.T + b2)
            return x @ w3.T + b3

        def _gru(x, h, wih, whh, bih, bhh):
            gi = x @ wih.T + bih
            gh = h @ whh.T + bhh
            ir, iz, inn = jnp.split(gi, 3, axis=-1)
            hr, hz, hn = jnp.split(gh, 3, axis=-1)
            r = jax.nn.sigmoid(ir + hr)
            z = jax.nn.sigmoid(iz + hz)
            n = jnp.tanh(inn + r * hn)
            return (1.0 - z) * n + z * h

        def _prop_once(node_states, f_idx, t_idx, edge_features, w1, b1, w2, b2, w3, b3):
            from_states = node_states[f_idx]
            to_states = node_states[t_idx]
            edge_inputs = jnp.concatenate([from_states, to_states, edge_features], axis=1)
            edge_states = _mlp(edge_inputs, w1, b1, w2, b2, w3, b3)
            return jax.ops.segment_sum(edge_states, t_idx, num_segments=node_states.shape[0])
        key = jax.random.key(seed)
        ks = jax.random.split(key, 24)
        s = lambda *shape: 0.05
        inp = {'node_states': jax.random.normal(ks[0], (N, D), jnp.float32), 'edge_features': jax.random.normal(ks[1], (E, D), jnp.float32), 'from_idx': jax.random.randint(ks[2], (E,), 0, N, jnp.int64 if jax.config.jax_enable_x64 else jnp.int32), 'to_idx': jax.random.randint(ks[3], (E,), 0, N, jnp.int64 if jax.config.jax_enable_x64 else jnp.int32), 'graph_idx': jax.random.randint(ks[4], (N,), 0, 16, jnp.int32), 'w1': jax.random.normal(ks[5], (H, 3 * D), jnp.float32) * 0.05, 'b1': jnp.zeros((H,), jnp.float32), 'w2': jax.random.normal(ks[6], (H, H), jnp.float32) * 0.05, 'b2': jnp.zeros((H,), jnp.float32), 'w3': jax.random.normal(ks[7], (D, H), jnp.float32) * 0.05, 'b3': jnp.zeros((D,), jnp.float32)}
        for i in range(3):
            inp[f'g{i}_wih'] = jax.random.normal(ks[8 + 4 * i], (3 * D, D), jnp.float32) * 0.05
            inp[f'g{i}_whh'] = jax.random.normal(ks[9 + 4 * i], (3 * D, D), jnp.float32) * 0.05
            inp[f'g{i}_bih'] = jnp.zeros((3 * D,), jnp.float32)
            inp[f'g{i}_bhh'] = jnp.zeros((3 * D,), jnp.float32)
        return inp
    _L0_gnn_all = _L0_gnn_setup()
    _L0_gnn_in = {k: v for k, v in _L0_gnn_all.items() if k in ('w1', 'b1', 'w2', 'b2', 'w3', 'b3', 'g0_wih', 'g0_whh', 'g0_bih', 'g0_bhh', 'g1_wih', 'g1_whh', 'g1_bih', 'g1_bhh', 'g2_wih', 'g2_whh', 'g2_bih', 'g2_bhh')}
    del _L0_gnn_all

    def _L1_gnn_setup():
        import jax, jax.numpy as jnp
        import numpy as np
        N_NODES = 3125
        N_EDGES = 50000
        D = 128
        N_LAYERS = 3
        key = jax.random.key(seed)
        ks = jax.random.split(key, 8)
        X = jax.random.normal(ks[0], (N_NODES, D), dtype=jnp.float32)
        edge_index = jax.random.randint(ks[1], (2, N_EDGES), 0, N_NODES, dtype=jnp.int64)
        eps = jax.random.normal(ks[2], (N_LAYERS,), dtype=jnp.float32)
        W1 = jax.random.normal(ks[3], (N_LAYERS, D, D), dtype=jnp.float32) * (1.0 / np.sqrt(D))
        b1 = jnp.zeros((N_LAYERS, D), dtype=jnp.float32)
        W2 = jax.random.normal(ks[4], (N_LAYERS, D, D), dtype=jnp.float32) * (1.0 / np.sqrt(D))
        b2 = jnp.zeros((N_LAYERS, D), dtype=jnp.float32)
        return {'X': X, 'edge_index': edge_index, 'eps': eps, 'W1': W1, 'b1': b1, 'W2': W2, 'b2': b2}
    _L1_gnn_all = _L1_gnn_setup()
    _L1_gnn_in = {k: v for k, v in _L1_gnn_all.items() if k in ('eps', 'W1', 'b1', 'W2', 'b2')}
    del _L1_gnn_all
    return {'x': x, 'src': src, 'dst': dst, 'edge_attr_128': edge_attr_128, 'L0_gnn_w1': _L0_gnn_in['w1'], 'L0_gnn_b1': _L0_gnn_in['b1'], 'L0_gnn_w2': _L0_gnn_in['w2'], 'L0_gnn_b2': _L0_gnn_in['b2'], 'L0_gnn_w3': _L0_gnn_in['w3'], 'L0_gnn_b3': _L0_gnn_in['b3'], 'L0_gnn_g0_wih': _L0_gnn_in['g0_wih'], 'L0_gnn_g0_whh': _L0_gnn_in['g0_whh'], 'L0_gnn_g0_bih': _L0_gnn_in['g0_bih'], 'L0_gnn_g0_bhh': _L0_gnn_in['g0_bhh'], 'L0_gnn_g1_wih': _L0_gnn_in['g1_wih'], 'L0_gnn_g1_whh': _L0_gnn_in['g1_whh'], 'L0_gnn_g1_bih': _L0_gnn_in['g1_bih'], 'L0_gnn_g1_bhh': _L0_gnn_in['g1_bhh'], 'L0_gnn_g2_wih': _L0_gnn_in['g2_wih'], 'L0_gnn_g2_whh': _L0_gnn_in['g2_whh'], 'L0_gnn_g2_bih': _L0_gnn_in['g2_bih'], 'L0_gnn_g2_bhh': _L0_gnn_in['g2_bhh'], 'L1_gnn_eps': _L1_gnn_in['eps'], 'L1_gnn_W1': _L1_gnn_in['W1'], 'L1_gnn_b1': _L1_gnn_in['b1'], 'L1_gnn_W2': _L1_gnn_in['W2'], 'L1_gnn_b2': _L1_gnn_in['b2']}

def reference(x, src, dst, edge_attr_128, L0_gnn_w1, L0_gnn_b1, L0_gnn_w2, L0_gnn_b2, L0_gnn_w3, L0_gnn_b3, L0_gnn_g0_wih, L0_gnn_g0_whh, L0_gnn_g0_bih, L0_gnn_g0_bhh, L0_gnn_g1_wih, L0_gnn_g1_whh, L0_gnn_g1_bih, L0_gnn_g1_bhh, L0_gnn_g2_wih, L0_gnn_g2_whh, L0_gnn_g2_bih, L0_gnn_g2_bhh, L1_gnn_eps, L1_gnn_W1, L1_gnn_b1, L1_gnn_W2, L1_gnn_b2):
    import jax
    import jax.numpy as jnp

    def _L0_gnn_ref(node_states, edge_features, from_idx, to_idx, graph_idx, w1, b1, w2, b2, w3, b3, g0_wih, g0_whh, g0_bih, g0_bhh, g1_wih, g1_whh, g1_bih, g1_bhh, g2_wih, g2_whh, g2_bih, g2_bhh):
        import jax, jax.numpy as jnp
        import numpy as np
        N, E, D, H = (3125, 20000, 128, 256)

        def _mlp(x, w1, b1, w2, b2, w3, b3):
            x = jax.nn.relu(x @ w1.T + b1)
            x = jax.nn.relu(x @ w2.T + b2)
            return x @ w3.T + b3

        def _gru(x, h, wih, whh, bih, bhh):
            gi = x @ wih.T + bih
            gh = h @ whh.T + bhh
            ir, iz, inn = jnp.split(gi, 3, axis=-1)
            hr, hz, hn = jnp.split(gh, 3, axis=-1)
            r = jax.nn.sigmoid(ir + hr)
            z = jax.nn.sigmoid(iz + hz)
            n = jnp.tanh(inn + r * hn)
            return (1.0 - z) * n + z * h

        def _prop_once(node_states, f_idx, t_idx, edge_features, w1, b1, w2, b2, w3, b3):
            from_states = node_states[f_idx]
            to_states = node_states[t_idx]
            edge_inputs = jnp.concatenate([from_states, to_states, edge_features], axis=1)
            edge_states = _mlp(edge_inputs, w1, b1, w2, b2, w3, b3)
            return jax.ops.segment_sum(edge_states, t_idx, num_segments=node_states.shape[0])
        agg = _prop_once(node_states, from_idx, to_idx, edge_features, w1, b1, w2, b2, w3, b3)
        agg = agg + _prop_once(node_states, to_idx, from_idx, edge_features, w1, b1, w2, b2, w3, b3)
        s1 = _gru(node_states, agg, g0_wih, g0_whh, g0_bih, g0_bhh)
        s2 = _gru(agg, s1, g1_wih, g1_whh, g1_bih, g1_bhh)
        s3 = _gru(s1, s2, g2_wih, g2_whh, g2_bih, g2_bhh)
        return s3

    def _L1_gnn_ref(X, edge_index, eps, W1, b1, W2, b2):
        import jax, jax.numpy as jnp
        import numpy as np
        N_NODES = 3125
        N_EDGES = 50000
        D = 128
        N_LAYERS = 3
        src = edge_index[0]
        dst = edge_index[1]
        n = X.shape[0]
        n_layers = eps.shape[0]
        for l in range(n_layers):
            S = jax.ops.segment_sum(X[src], dst, num_segments=n)
            Z = (1.0 + eps[l]) * X + S
            H = jax.nn.relu(Z @ W1[l] + b1[l])
            X = H @ W2[l] + b2[l]
        return X
    edge_index = jnp.stack([src, dst])
    batch0 = jnp.zeros((3125,), jnp.int32)
    x = _layernorm(x + _L0_gnn_ref(x, edge_attr_128, src, dst, batch0, L0_gnn_w1, L0_gnn_b1, L0_gnn_w2, L0_gnn_b2, L0_gnn_w3, L0_gnn_b3, L0_gnn_g0_wih, L0_gnn_g0_whh, L0_gnn_g0_bih, L0_gnn_g0_bhh, L0_gnn_g1_wih, L0_gnn_g1_whh, L0_gnn_g1_bih, L0_gnn_g1_bhh, L0_gnn_g2_wih, L0_gnn_g2_whh, L0_gnn_g2_bih, L0_gnn_g2_bhh), axis=-1)
    x = _layernorm(x + _L1_gnn_ref(x, edge_index, L1_gnn_eps, L1_gnn_W1, L1_gnn_b1, L1_gnn_W2, L1_gnn_b2), axis=-1)
    return x

_drawn_inputs = setup_inputs


def setup_inputs(seed=0):
    import zlib

    import numpy as np

    out = dict(_drawn_inputs(seed))
    spreads = {'L0_gnn_b1': (0.0, 0.1),
     'L0_gnn_b2': (0.0, 0.1),
     'L0_gnn_b3': (0.0, 0.1),
     'L0_gnn_g0_bih': (0.0, 0.645),
     'L0_gnn_g0_bhh': (0.0, 0.467),
     'L0_gnn_g1_bih': (0.0, 0.8),
     'L0_gnn_g1_bhh': (0.0, 0.8),
     'L0_gnn_g2_bih': (0.0, 1.025),
     'L0_gnn_g2_bhh': (0.0, 0.606),
     'L1_gnn_b1': (0.0, 2.0),
     'L1_gnn_b2': (0.0, 2.0)}
    factors = {'edge_attr_128': 4.016, 'L0_gnn_g0_wih': 4.643, 'L1_gnn_eps': 41.706}
    for name, (base, spread) in spreads.items():
        noise = np.random.default_rng([zlib.crc32(name.encode()), seed]).standard_normal(out[name].shape)
        drawn = base * np.exp(spread * noise) if base else spread * noise
        out[name] = jnp.asarray(drawn.astype(out[name].dtype))
    for name, factor in factors.items():
        out[name] = (out[name] * factor).astype(out[name].dtype)
    return out
```

```python
import numpy as np
import concourse.bass as bass
from concourse import mybir
from contextlib import ExitStack

fp32 = mybir.dt.float32
f32r = mybir.dt.float32r
i32 = mybir.dt.int32
ALU = mybir.AluOpType
ACT = mybir.ActivationFunctionType
AX = mybir.AxisListType

P = 128
D = 128
H = 256
HB = H // P
N = 3125
E = 53125
K = 4
GE = K * P
G = (E + GE - 1) // GE
LAST = E - (G - 1) * GE
PAD = N
AW = 3136
DUMMY = PAD + 1
AROWS = 3328
NR = 3200
ADUMMY = NR * AW
ZW = AROWS * D // P
AZ = -(-(ADUMMY + P) // (P * ZW))
ASIZE = AZ * P * ZW
NP = 125
NB = N // NP
CH = 448
CHUNKS = [(c, min(CH, N - c)) for c in range(0, N, CH)]
LAYERS = 3
EPS = 1e-5


def edge_stage(nc, a, adj_flat, tables):
    ctx = ExitStack()
    with ctx:
        def sb(name, shape, dt=fp32):
            return ctx.enter_context(nc.sbuf_tensor(name, shape, dt))

        def sem(name):
            return ctx.enter_context(nc.semaphore(name))

        ident = sb("ident", [P, P])
        lower = sb("lower", [P, P])
        w1n = sb("w1n", [P, HB, 3 * D])
        w2n = sb("w2n", [P, HB, H])
        w3n = sb("w3n", [P, H])
        whalf = sb("whalf", [P, HB, 2, D])
        wfirst = sb("wfirst", [P, HB, 3, P])
        w2t = sb("w2t", [P, HB, HB, P])
        w3t = sb("w3t", [P, HB, P])
        b1c = sb("b1c", [P, HB])
        b2c = sb("b2c", [P, HB])
        b3r = sb("b3r", [P, D])
        zero = sb("zero", [P, ZW])
        rows_i = sb("rows_i", [G, 2, GE], i32)
        rows_f = sb("rows_f", [G, 2, GE])
        rows_r = sb("rows_r", [G, 2, K, P], f32r)
        keys = sb("keys", [P, G, 3, K])
        away = sb("away", [P, G, 3, K])
        dummy_i = sb("dummy_i", [P, 3], i32)
        dummy = sb("dummyf", [P, 3])
        gidx = [sb(f"gidx{i}", [P, 2, K], i32) for i in range(3)]
        xg = [sb(f"xg{i}", [P, 2, K, D]) for i in range(2)]
        ef = [sb(f"ef{i}", [P, K, D]) for i in range(2)]
        same = [sb(f"same{i}", [P, 2, K, P]) for i in range(2)]
        target = [sb(f"target{i}", [P, 3, K], i32) for i in range(2)]
        pairs = [sb(f"pairs{i}", [P, K]) for i in range(2)]
        rowto = [sb(f"rowto{i}", [P, 2, K], i32) for i in range(2)]
        outb = [sb(f"outb{i}", [P, 2, K, D]) for i in range(2)]
        sel = sb("sel", [G, P], f32r)
        sd = sb("sd", [P, 2, K, D])
        sdet = sb("sdet", [P, 3, GE])
        pb = sb("pb", [P, HB, GE])
        hpre = sb("hpre", [P, HB, 2, GE])
        h1 = sb("h1", [P, 2, HB, GE])
        h2 = sb("h2", [P, 2, HB, GE])
        es = sb("es", [P, 2, GE])
        match = sb("match", [P, 4, K, P])
        found = sb("found", [P, 4, K])
        shift = sb("shift", [P, 3, K])
        bank = [ctx.enter_context(nc.psum_tensor(f"ebank{i}", [P, 512], fp32)) for i in range(8)]

        s_const = sem("s_const")
        s_wload = sem("s_wload")
        s_iload = sem("s_iload")
        s_zero = sem("s_zero")
        s_ztab = sem("s_ztab")
        s_zadj = sem("s_zadj")
        s_whalf = sem("s_whalf")
        s_wT = sem("s_wT")
        s_wc = sem("s_wc")
        s_rows = sem("s_rows")
        s_dve = sem("s_dve")
        s_keys = sem("s_keys")
        s_gidx = [sem(f"s_gidx{i}") for i in range(3)]
        s_ef = [sem(f"s_ef{i}") for i in range(2)]
        s_x = [sem(f"s_x{i}") for i in range(2)]
        s_sd = sem("s_sd")
        s_sel = sem("s_sel")
        s_sdT = sem("s_sdT")
        s_eT = sem("s_eT")
        s_tev = sem("s_tev")
        s_row = sem("s_row")
        s_cmp = sem("s_cmp")
        s_cs = sem("s_cs")
        s_tgt = sem("s_tgt")
        s_p = sem("s_p")
        s_q = sem("s_q")
        s_pc = sem("s_pc")
        s_hp = sem("s_hp")
        s_h1 = sem("s_h1")
        s_l2 = sem("s_l2")
        s_h2 = sem("s_h2")
        s_l3 = sem("s_l3")
        s_es = sem("s_es")
        s_sum = sem("s_sum")
        s_out = sem("s_out")
        s_rowto = sem("s_rowto")
        s_add = [sem(f"s_add{k}") for k in range(K)]
        s_pace = sem("s_pace")
        s_adj = sem("s_adj")

        block = ctx.enter_context(nc.Block())

        @block.sync
        def _(sp):
            w1v = a["L0_gnn_w1"].rearrange("(f p) c -> p f c", p=P)
            sp.wait_ge(s_zero, 2)
            nf = (G - 1) // 16 * 16
            for s, name in enumerate(("src", "dst")):
                full = a[name][0:(G - 1) * GE].rearrange("(g e) -> g e", e=GE)
                sp.dma_start(rows_i[0:nf, s, :], full[0:nf, :]).then_inc(s_iload, 16)
                sp.dma_start(rows_i[nf:G - 1, s, :], full[nf:G - 1, :]).then_inc(s_iload, 16)
                sp.dma_start(rows_i[G - 1:G, s, 0:LAST],
                             a[name][(G - 1) * GE:E].rearrange("(g e) -> g e", g=1)).then_inc(s_iload, 16)

            def load(g, par):
                for s, name in enumerate(("src", "dst")):
                    sp.dma_start(gidx[par][:, s, :],
                                 a[name][bass.ds(g * GE, GE)].rearrange("(p k) -> p k", k=K)
                                 ).then_inc(s_gidx[par], 16)
                sp.dma_start(ef[par][:, :, :],
                             a["edge_attr_128"][bass.ds(g * GE, GE), :].rearrange("(p k) d -> p k d", k=K)
                             ).then_inc(s_ef[par], 16)

            load(0, 0)
            load(1, 1)
            sp.dma_start(w1n[:, :, :], w1v).then_inc(s_wload, 16)
            sp.dma_start(w2n[:, :, :], a["L0_gnn_w2"].rearrange("(f p) c -> p f c", p=P)).then_inc(s_wload, 16)
            sp.dma_start(w3n[:, :], a["L0_gnn_w3"]).then_inc(s_wload, 16)
            with nc.allow_non_contiguous_dma(reason="256 biases"):
                sp.dma_start(b1c[:, :], a["L0_gnn_b1"].rearrange("(f p) -> p f", p=P)).then_inc(s_wload, 16)
                sp.dma_start(b2c[:, :], a["L0_gnn_b2"].rearrange("(f p) -> p f", p=P)).then_inc(s_wload, 16)
            sp.dma_start(b3r[:, :], a["L0_gnn_b3"].partition_broadcast(P)).then_inc(s_wload, 16)
            sp.wait_ge(s_zero, 3)
            for k in range(K):
                sp.dma_start(tables[k].rearrange("(p r) d -> p (r d)", p=P), zero[:, :]).then_inc(s_ztab, 16)
            adj_z = adj_flat.rearrange("(s p c) o -> s p (c o)", s=AZ, p=P)
            for s in range(AZ):
                sp.dma_start(adj_z[s], zero[:, :]).then_inc(s_zadj, 16)

            def reload(g, par, turn):
                sp.wait_ge(s_x[par], turn * (2 * K * 16))
                sp.wait_ge(s_eT, g - 1)
                load(g, par)

            with sp.Fori(0, (G - 4) // 2) as i:
                for par in range(2):
                    reload(i * 2 + (2 + par), par, i + 1)
            reload(G - 2, 0, (G - 2) // 2)
            par, fp, one = 1, LAST // K, LAST % K
            base = (G - 1) * GE
            sp.wait_ge(s_eT, G - 2)
            for s, name in enumerate(("src", "dst")):
                sp.dma_start(gidx[2][0:fp, s, :],
                             a[name][base:base + fp * K].rearrange("(p k) -> p k", k=K)).then_inc(s_gidx[2], 16)
                sp.dma_start(gidx[2][fp:fp + 1, s, 0:one],
                             a[name][base + fp * K:E].rearrange("(p k) -> p k", p=1)).then_inc(s_gidx[2], 16)
            sp.dma_start(ef[par][0:fp, :, :],
                         a["edge_attr_128"][base:base + fp * K, :].rearrange("(p k) d -> p k d", k=K)
                         ).then_inc(s_ef[par], 16)
            sp.dma_start(ef[par][fp:fp + 1, 0:one, :],
                         a["edge_attr_128"][base + fp * K:E, :].rearrange("(p k) d -> p k d", p=1)
                         ).then_inc(s_ef[par], 16)

        @block.gpsimd
        def _(pool):
            nc.gpsimd.memset(ident[:, :], 0.0).then_inc(s_const, 1)
            nc.gpsimd.memset(lower[:, :], 1.0).then_inc(s_const, 1)
            for j, base in enumerate((DUMMY, DUMMY, ADUMMY)):
                nc.gpsimd.iota(dummy_i[:, j:j + 1], pattern=[[0, 1]], base=base,
                               channel_multiplier=1).then_inc(s_const, 1)
            pool.wait_ge(s_const, 5)
            nc.gpsimd.affine_select(out=ident[:, :], in_=ident[:, :], compare_op=ALU.not_equal, fill=1.0,
                                    base=0, pattern=[[-1, P]], channel_multiplier=1).then_inc(s_const, 1)
            nc.gpsimd.affine_select(out=lower[:, :], in_=lower[:, :], compare_op=ALU.is_gt, fill=0.0,
                                    base=0, pattern=[[-1, P]], channel_multiplier=1).then_inc(s_const, 1)

            def gather(par, k, ids=None):
                ids = gidx[par] if ids is None else ids
                for s in range(2):
                    pool.indirect_dma_start(
                        out=xg[par][:, s, k, :], out_offset=None, in_=a["x"],
                        in_offset=bass.IndirectOffsetOnAxis(ap=ids[:, s, k:k + 1], axis=0)
                    ).then_inc(s_x[par], 16)

            def plain():
                pool.sem_inc(s_pace, 1)

            def pair(g, par, k):
                pool.wait_ge(s_adj, (g * K + k) * 16)
                plain()
                pool.indirect_dma_start(
                    out=adj_flat, out_offset=bass.IndirectOffsetOnAxis(ap=target[par][:, 2, k:k + 1], axis=0),
                    in_=pairs[par][:, k:k + 1], in_offset=None, compute_op=ALU.add).then_inc(s_adj, 16)

            def add(g, par, way, k):
                nth = way if k < K // 2 else 1 - way
                pool.wait_ge(s_add[k], (g * 2 + nth) * 16)
                plain()
                pool.indirect_dma_start(
                    out=tables[k], out_offset=bass.IndirectOffsetOnAxis(ap=rowto[par][:, way, k:k + 1], axis=0),
                    in_=outb[par][:, way, k, :], in_offset=None, compute_op=ALU.add).then_inc(s_add[k], 16)

            def turn(j, par, turns, gathers=True, pairing=True, adding=True):
                if gathers == "last":
                    pool.wait_ge(s_gidx[2], 64)
                elif gathers:
                    pool.wait_ge(s_gidx[par], (turns + 1) * 32 + 32)
                if gathers:
                    pool.wait_ge(s_sd, j + 1)
                if pairing:
                    pool.wait_ge(s_tgt, j + 1)
                if adding:
                    pool.wait_ge(s_out, (j - 1) * 2 + 2)
                    pool.wait_ge(s_rowto, j)
                plain()
                for k in range(K):
                    if gathers:
                        gather(par, k, gidx[2] if gathers == "last" else gidx[par])
                    if adding:
                        add(j - 1, 1 - par, 0, k)
                    if pairing:
                        pair(j, par, k)
                    if adding:
                        add(j - 1, 1 - par, 1, (k + K // 2) % K)

            for par in range(2):
                pool.wait_ge(s_gidx[par], 32)
                for k in range(K):
                    gather(par, k)
            pool.wait_ge(s_zadj, AZ * 16)
            turn(0, 0, 0, adding=False)
            pool.wait_ge(s_ztab, K * 16)
            turn(1, 1, 0)
            with pool.Fori(0, (G - 4) // 2 - 1) as i:
                for par in range(2):
                    turn(i * 2 + (2 + par), par, i + 1)
            turn(G - 4, 0, (G - 4) // 2)
            turn(G - 3, 1, 0, gathers="last")
            turn(G - 2, 0, 0, gathers=False)
            turn(G - 1, 1, 0, gathers=False)
            turn(G, 0, 0, gathers=False, pairing=False)
            pool.wait_ge(s_adj, G * K * 16)
            for k in range(K):
                pool.wait_ge(s_add[k], G * 2 * 16)

        @block.scalar
        def _(act):
            def evac(g, j):
                act.wait_ge((s_sdT, s_sdT, s_eT)[j], (g * 2 + j + 1) if j < 2 else (g + 1))
                nc.scalar.copy(sdet[:, j, :], bank[(0, 1, 0)[j]][:, :]).then_inc(s_tev, 1)

            def first(g):
                for f in range(HB):
                    act.wait_ge(s_p, g * HB + (f + 1))
                    nc.scalar.activation(pb[:, f, :], bank[2 + 2 * f][:, :], ACT.Identity,
                                         bias=b1c[:, f:f + 1]).then_inc(s_pc, 1)
                act.wait_ge(s_l2, g * 4)
                for f in range(HB):
                    act.wait_ge(s_hp, g * HB + (f + 1))
                    for way in range(2):
                        nc.scalar.activation(h1[:, way, f, :], hpre[:, f, way, :], ACT.Relu).then_inc(s_h1, 1)

            def second(g, n):
                way, f = divmod(n, HB)
                act.wait_ge(s_l2, g * 4 + (n + 1))
                act.wait_ge(s_l3, g * 2)
                nc.scalar.activation(h2[:, way, f, :], bank[6 + f][:, :], ACT.Relu,
                                     bias=b2c[:, f:f + 1]).then_inc(s_h2, 1)

            act.wait_ge(s_wload, 6 * 16)
            for j in range(3):
                evac(0, j)
            first(0)

            def turn(g, ahead=True):
                if ahead:
                    evac(g + 1, 0)
                    evac(g + 1, 1)
                second(g, 0)
                if ahead:
                    evac(g + 1, 2)
                for n in range(1, 4):
                    second(g, n)
                if ahead:
                    first(g + 1)

            turn(0)
            with act.Fori(1, G - 1) as g:
                turn(g)
            turn(G - 1, ahead=False)

        @block.vector
        def _(dve):
            steps = [0]

            def step(ins):
                steps[0] += 1
                ins.then_inc(s_dve, 1)
                dve.wait_ge(s_dve, steps[0])

            nc.vector.memset(rows_i[:, :, :], PAD).then_inc(s_zero, 1)
            nc.vector.memset(gidx[2][:, :, :], 0).then_inc(s_zero, 1)
            nc.vector.memset(zero[:, :], 0.0).then_inc(s_zero, 1)
            dve.wait_ge(s_iload, 6 * 16)
            step(nc.vector.tensor_copy(rows_f[:, :, :], rows_i[:, :, :]))
            for s in range(2):
                nc.vector.tensor_copy(rows_r[:, s, :, :],
                                      rows_f[:, s, :].rearrange("g (p k) -> g k p", k=K)).then_inc(s_rows, 1)
            dve.wait_ge(s_wload, 6 * 16)
            for f in range(HB):
                step(nc.vector.tensor_tensor(whalf[:, f, 0, :], w1n[:, f, 0:D], w1n[:, f, D:2 * D], ALU.add))
                step(nc.vector.tensor_tensor(whalf[:, f, 1, :], w1n[:, f, 0:D], w1n[:, f, D:2 * D], ALU.subtract))
            nc.vector.tensor_scalar(whalf[:, :, :, :], whalf[:, :, :, :], 0.5, None, ALU.mult).then_inc(s_whalf, 1)
            dve.wait_ge(s_wT, 2)
            for s in range(2):
                nc.vector.tensor_copy(keys[:, :, 1 - s, :], bank[s][:, 0:K * G].rearrange("p (k g) -> p g k", k=K)
                                      ).then_inc(s_wc, 1)
            dve.wait_ge(s_wc, 2)
            step(nc.vector.tensor_scalar(away[:, :, 2, :], keys[:, :, 1, :], float(AW), None, ALU.mult))
            step(nc.vector.tensor_tensor(keys[:, :, 2, :], away[:, :, 2, :], keys[:, :, 0, :], ALU.add))
            dve.wait_ge(s_const, 7)
            step(nc.vector.tensor_copy(dummy[:, :], dummy_i[:, :]))
            for j in range(3):
                last = nc.vector.tensor_scalar(away[:, :, j, :], keys[:, :, j, :], -1.0, dummy[:, j:j + 1],
                                               ALU.mult, ALU.add)
            step(last)
            dve.wait_ge(s_wT, 5)
            for f in range(HB):
                nc.vector.tensor_copy(wfirst[:, f, :, :], bank[2 + f][:, 0:3 * P]).then_inc(s_wc, 1)
            nc.vector.tensor_copy(w2t[:, :, :, :], bank[4][:, :]).then_inc(s_wc, 1)
            dve.wait_ge(s_wT, 6)
            nc.vector.tensor_copy(w3t[:, :, :], bank[5][:, 0:2 * P]).then_inc(s_wc, 1)

            def sums(g, par, turns):
                dve.wait_ge(s_x[par], (turns + 1) * (2 * K * 16))
                dve.wait_ge(s_sdT, g * 2)
                nc.vector.tensor_tensor(sd[:, 0, :, :], xg[par][:, 0, :, :], xg[par][:, 1, :, :], ALU.add)
                nc.vector.tensor_tensor(sd[:, 1, :, :], xg[par][:, 0, :, :], xg[par][:, 1, :, :],
                                        ALU.subtract).then_inc(s_sd, 1)

            def select(g):
                dve.wait_ge(s_row, g * 2)
                nc.vector.tensor_copy(sel[:, :], ident[0:G, bass.ds(g, 1)].broadcast_to([G, P])).then_inc(s_sel, 1)

            def compare(g, par, early=False):
                if not early:
                    dve.wait_ge(s_sum, (g - 1) * 2)
                    dve.wait_ge(s_adj, (g - 1) * (K * 16))
                for s in (1, 0):
                    dve.wait_ge(s_row, g * 2 + (2 - s))
                    nc.vector.tensor_tensor(
                        same[par][:, s, :, :], bank[s][:, :].rearrange("p (k j) -> p k j", k=K),
                        keys[:, bass.ds(g, 1), s, :].rearrange("p g k -> p (g k)").unsqueeze(2).broadcast_to([P, K, P]),
                        ALU.is_equal).then_inc(s_cmp, 1)
                dve.wait_ge(s_cmp, g * 2 + 2)
                tri = lower[:, :].unsqueeze(1).broadcast_to([P, K, P])
                nc.vector.tensor_tensor(match[:, 3, :, :], same[par][:, 0, :, :], same[par][:, 1, :, :],
                                        ALU.mult).then_inc(s_cs, 1)
                for s in range(2):
                    nc.vector.tensor_tensor(match[:, s, :, :], same[par][:, s, :, :], tri, ALU.mult).then_inc(s_cs, 1)
                dve.wait_ge(s_cs, g * 7 + 3)
                nc.vector.tensor_tensor(match[:, 2, :, :], match[:, 3, :, :], tri, ALU.mult).then_inc(s_cs, 1)
                dve.wait_ge(s_cs, g * 7 + 4)
                nc.vector.tensor_reduce(found[:, :, :].rearrange("p s k -> p (s k)"),
                                        match[:, :, :, :].rearrange("p s k j -> p (s k) j"),
                                        axis=AX.X, op=ALU.add).then_inc(s_cs, 1)
                dve.wait_ge(s_cs, g * 7 + 5)
                nc.vector.scalar_tensor_tensor(
                    out=shift[:, :, :].rearrange("p s k -> p (s k)"),
                    in0=found[:, 0:3, :].rearrange("p s k -> p (s k)"), scalar=1.0,
                    in1=away[:, bass.ds(g, 1), :, :].rearrange("p g s k -> p (g s k)"),
                    op0=ALU.min, op1=ALU.mult).then_inc(s_cs, 1)
                nc.vector.tensor_copy(pairs[par][:, :], found[:, 3, :]).then_inc(s_cs, 1)
                dve.wait_ge(s_cs, g * 7 + 7)
                nc.vector.tensor_tensor(
                    target[par][:, :, :].rearrange("p s k -> p (s k)"),
                    shift[:, :, :].rearrange("p s k -> p (s k)"),
                    keys[:, bass.ds(g, 1), :, :].rearrange("p g s k -> p (g s k)"), ALU.add).then_inc(s_tgt, 1)

            def ways(g):
                for f in range(HB):
                    dve.wait_ge(s_pc, g * HB + (f + 1))
                    dve.wait_ge(s_q, g * HB + (f + 1))
                    dve.wait_ge(s_h1, g * 4)
                    nc.vector.tensor_tensor(hpre[:, f, 0, :], pb[:, f, :], bank[3 + 2 * f][:, :], ALU.add)
                    nc.vector.tensor_tensor(hpre[:, f, 1, :], pb[:, f, :], bank[3 + 2 * f][:, :],
                                            ALU.subtract).then_inc(s_hp, 1)

            def results(g):
                b3 = b3r[:, :].unsqueeze(1).broadcast_to([P, K, D])
                for way in range(2):
                    dve.wait_ge(s_l3, g * 2 + (way + 1))
                    if way == 0:
                        dve.wait_ge(s_sum, g * 2)
                    nc.vector.tensor_tensor(es[:, way, :].rearrange("p (k d) -> p k d", k=K),
                                            bank[6 + way][:, :].rearrange("p (k d) -> p k d", k=K), b3,
                                            ALU.add).then_inc(s_es, 1)

            def deliver(g, par, early=False):
                if not early:
                    for k in range(K):
                        dve.wait_ge(s_add[k], (g - 1) * 32)
                nc.vector.tensor_copy(rowto[par][:, :, :], target[par][:, 0:2, :]).then_inc(s_rowto, 1)
                for way in range(2):
                    dve.wait_ge(s_sum, g * 2 + (way + 1))
                    nc.vector.tensor_copy(outb[par][:, way, :, :].rearrange("p k d -> p (k d)"),
                                          bank[way][:, :]).then_inc(s_out, 1)

            select(0)
            sums(0, 0, 0)
            compare(0, 0, early=True)
            ways(0)
            select(1)
            sums(1, 1, 0)

            def turn(g, par, turns, ahead=2, early=False):
                if ahead:
                    compare(g + 1, 1 - par, early=early == 2)
                    ways(g + 1)
                results(g)
                deliver(g, par, early)
                if ahead == 2:
                    select(g + 2)
                    sums(g + 2, par, turns + 1)

            turn(0, 0, 0, early=2)
            turn(1, 1, 0, early=1)
            with dve.Fori(0, (G - 4) // 2) as i:
                for par in range(2):
                    turn(i * 2 + (2 + par), par, i + 1)
            turn(G - 2, 0, 0, ahead=1)
            turn(G - 1, 1, 0, ahead=0)

        @block.tensor
        def _(pe):
            def transpose(out, in_, n):
                return nc.tensor.transpose(out, in_, ident[0:n, 0:n])

            pe.wait_ge(s_const, 7)
            pe.wait_ge(s_rows, 2)
            for s in range(2):
                for k in range(K):
                    last = transpose(bank[s][:, k * G:(k + 1) * G],
                                     rows_f[:, s, :].rearrange("g (p k) -> g k p", k=K)[:, k, :], G)
                last.then_inc(s_wT, 1)
            pe.wait_ge(s_wload, 6 * 16)
            pe.wait_ge(s_whalf, 1)
            for f in range(HB):
                for j in range(2):
                    transpose(bank[2 + f][:, j * P:(j + 1) * P], whalf[:, f, j, :], P)
                transpose(bank[2 + f][:, 2 * P:3 * P], w1n[:, f, 2 * D:3 * D], P).then_inc(s_wT, 1)
            for f in range(HB):
                for k in range(HB):
                    last = transpose(bank[4][:, (f * HB + k) * P:(f * HB + k + 1) * P],
                                     w2n[:, f, k * P:(k + 1) * P], P)
            last.then_inc(s_wT, 1)
            for k in range(HB):
                last = transpose(bank[5][:, k * P:(k + 1) * P], w3n[:, k * P:(k + 1) * P], P)
            last.then_inc(s_wT, 1)
            pe.wait_ge(s_wc, 6)

            def turn_sd(g, first=False):
                pe.wait_ge(s_sd, g + 1)
                if not first:
                    pe.wait_ge(s_cmp, g * 2)
                    pe.wait_ge(s_out, g * 2 - 2)
                for j in range(2):
                    for k in range(K):
                        last = transpose(bank[j][:, k * P:(k + 1) * P], sd[:, j, k, :], P)
                    last.then_inc(s_sdT, 1)

            def turn_e(g, par, turns, extra=0):
                pe.wait_ge(s_tev, g * 3 + 1)
                pe.wait_ge(s_ef[par], turns * 16 + (16 + extra))
                for k in range(K):
                    last = transpose(bank[0][:, k * P:(k + 1) * P], ef[par][:, k, :], P)
                last.then_inc(s_eT, 1)
                pe.wait_ge(s_tev, g * 3 + 2)
                pe.wait_ge(s_sel, g + 1)
                nc.tensor.matmul(bank[1][:, :], sel[:, :], rows_r[:, 0, :, :].rearrange("g k p -> g (k p)"),
                                 start=True, stop=True).then_inc(s_row, 1)

            def turn_dst(g):
                pe.wait_ge(s_tev, g * 3 + 3)
                nc.tensor.matmul(bank[0][:, :], sel[:, :], rows_r[:, 1, :, :].rearrange("g k p -> g (k p)"),
                                 start=True, stop=True).then_inc(s_row, 1)

            def first(g, start=False):
                pe.wait_ge(s_tev, g * 3 + 3)
                if not start:
                    pe.wait_ge(s_hp, g * HB)
                for f in range(HB):
                    nc.tensor.matmul(bank[2 + 2 * f][:, :], wfirst[:, f, 0, :], sdet[:, 0, :], start=True, stop=False)
                    nc.tensor.matmul(bank[2 + 2 * f][:, :], wfirst[:, f, 2, :], sdet[:, 2, :],
                                     start=False, stop=True).then_inc(s_p, 1)
                    nc.tensor.matmul(bank[3 + 2 * f][:, :], wfirst[:, f, 1, :], sdet[:, 1, :],
                                     start=True, stop=True).then_inc(s_q, 1)

            def second(g, n):
                way, f = divmod(n, HB)
                if n == 0:
                    pe.wait_ge(s_h1, g * 4 + 4)
                    pe.wait_ge(s_es, g * 2)
                if n >= HB:
                    pe.wait_ge(s_h2, g * 4 + (n - 1))
                for k in range(HB):
                    last = nc.tensor.matmul(bank[6 + f][:, :], w2t[:, f, k, :], h1[:, way, k, :],
                                            start=(k == 0), stop=(k == HB - 1))
                last.then_inc(s_l2, 1)

            def third(g):
                pe.wait_ge(s_h2, g * 4 + 4)
                for way in range(2):
                    for t in range(K):
                        for k in range(HB):
                            last = nc.tensor.matmul(bank[6 + way][:, t * P:(t + 1) * P],
                                                    h2[:, way, k, t * P:(t + 1) * P], w3t[:, k, :],
                                                    start=(k == 0), stop=(k == HB - 1))
                    last.then_inc(s_l3, 1)

            def total(g, par, ahead):
                pe.wait_ge(s_cmp, (g + 1) * 2 + (2 if ahead else 0))
                for way in range(2):
                    pe.wait_ge(s_es, g * 2 + (way + 1))
                    for t in range(K):
                        last = nc.tensor.matmul(bank[way][:, t * P:(t + 1) * P], same[par][:, way, t, :],
                                                es[:, way, t * P:(t + 1) * P], start=True, stop=True)
                    last.then_inc(s_sum, 1)

            def turn(g, par, turns, ahead=True, extra=0):
                if ahead:
                    turn_sd(g + 1)
                second(g, 0)
                if ahead:
                    turn_e(g + 1, 1 - par, turns, extra)
                second(g, 1)
                if ahead:
                    turn_dst(g + 1)
                second(g, 2)
                second(g, 3)
                if ahead:
                    first(g + 1)
                third(g)
                total(g, par, ahead)

            turn_sd(0, first=True)
            turn_e(0, 0, 0)
            turn_dst(0)
            first(0, start=True)
            turn(0, 0, 0)
            turn(1, 1, 1)
            with pe.Fori(1, (G - 2) // 2) as i:
                turn(i * 2, 0, i)
                turn(i * 2 + 1, 1, i + 1)
            turn(G - 2, 0, (G - 2) // 2, extra=16)
            turn(G - 1, 1, 0, ahead=False)


def rows_of(x, p0, p1):
    return x[NB * p0:NB * p1, :].rearrange("(p b) d -> p b d", b=NB)


def block_groups():
    return [(b, min(4, NB - b)) for b in range(0, NB, 4)]


def strided(xt, b, nb):
    return xt[:, 0:N].rearrange("d (p b) -> d b p", b=NB)[:, b:b + nb, :]


def layer_norm(nc, dve, act_square, y, out, stat, s_ln, ln0, s_sqrt):
    steps = [ln0]

    def step(ins):
        steps[0] += 1
        ins.then_inc(s_ln, 1)
        dve.wait_ge(s_ln, steps[0])

    mean, var, std, rstd = (stat[0:NP, j, :] for j in range(4))
    wide = lambda v: v.unsqueeze(2).broadcast_to([NP, NB, D])
    step(nc.vector.tensor_reduce(mean, y, axis=AX.X, op=ALU.add))
    step(nc.vector.tensor_scalar(mean, mean, 1.0 / D, None, ALU.mult))
    step(nc.vector.tensor_tensor(y, y, wide(mean), ALU.subtract))
    step(nc.vector.tensor_tensor(act_square, y, y, ALU.mult))
    step(nc.vector.tensor_reduce(var, act_square, axis=AX.X, op=ALU.add))
    step(nc.vector.tensor_scalar(var, var, 1.0 / D, EPS, ALU.mult, ALU.add))
    dve.wait_ge(s_sqrt[0], s_sqrt[1])
    step(nc.vector.reciprocal(rstd, std))
    return nc.vector.tensor_tensor(out, y, wide(rstd), ALU.mult), steps[0]


LN_STEPS = 7


def gru_stage(nc, a, tables, x1):
    ctx = ExitStack()
    with ctx:
        def sb(name, shape, dt=fp32):
            return ctx.enter_context(nc.sbuf_tensor(name, shape, dt))

        def sem(name):
            return ctx.enter_context(nc.semaphore(name))

        ident = sb("gident", [P, P])
        tab = sb("tab", [P, K, NB * D])
        xn = sb("xn", [P, NB, D])
        wn = sb("wn", [P, LAYERS, 2, 3, D])
        wt = sb("wt", [P, LAYERS, 2, 3, P])
        bias = sb("bias", [P, LAYERS, 2, 3])
        both = sb("both", [P, LAYERS, 3])
        xt = sb("xt", [P, AW])
        aggt = sb("aggt", [P, AW])
        s1t = sb("s1t", [P, AW])
        s2t = sb("s2t", [P, AW])
        gates = sb("gates", [P, 2, 2, CH])
        cand = sb("cand", [P, 2, CH])
        diff = sb("diff", [P, 2, CH])
        stat = sb("gstat", [P, 4, NB])
        bank = [ctx.enter_context(nc.psum_tensor(f"gbank{i}", [P, 512], fp32)) for i in range(8)]

        s_const = sem("g_const")
        s_zero = sem("g_zero")
        s_load = sem("g_load")
        s_w = sem("g_w")
        s_agg = sem("g_agg")
        s_both = sem("g_both")
        s_T = sem("g_T")
        s_tc = sem("g_tc")
        s_tc2 = sem("g_tc2")
        s_mm = sem("g_mm")
        s_rz = sem("g_rz")
        s_rh = sem("g_rh")
        s_pre = sem("g_pre")
        s_n = sem("g_n")
        s_d = sem("g_d")
        s_cell = sem("g_cell")
        s_back = sem("g_back")
        s_res = sem("g_res")
        s_ln = sem("g_ln")
        s_sq = sem("g_sq")
        s_done = sem("g_done")
        groups = block_groups()
        NGR = len(groups)
        NC = AW // CH

        block = ctx.enter_context(nc.Block())

        @block.sync
        def _(sp):
            sp.wait_ge(s_zero, 1)
            sp.dma_start(xn[0:112, :, :], rows_of(a["x"], 0, 112)).then_inc(s_load, 16)
            sp.dma_start(xn[112:NP, :, :], rows_of(a["x"], 112, NP)).then_inc(s_load, 16)
            for k in range(K):
                sp.dma_start(tab[:, k, :], tables[k][0:NR, :].rearrange("(p b) d -> p (b d)", b=NB)
                             ).then_inc(s_load, 16)

        @block.gpsimd
        def _(pool):
            nc.gpsimd.memset(ident[:, :], 0.0).then_inc(s_const, 1)
            pool.wait_ge(s_const, 1)
            nc.gpsimd.affine_select(out=ident[:, :], in_=ident[:, :], compare_op=ALU.not_equal, fill=1.0,
                                    base=0, pattern=[[-1, P]], channel_multiplier=1).then_inc(s_const, 1)

        @block.scalar
        def _(act):
            for c in range(LAYERS):
                for m, kind in enumerate(("ih", "hh")):
                    act.dma_start(wn[:, c, m, :, :], a[f"L0_gnn_g{c}_w{kind}"].rearrange("(g p) d -> p g d", p=P)
                                  ).then_inc(s_w, 16)
                    with nc.allow_non_contiguous_dma(reason="384 biases"):
                        act.dma_start(bias[:, c, m, :], a[f"L0_gnn_g{c}_b{kind}"].rearrange("(g p) -> p g", p=P)
                                      ).then_inc(s_w, 16)
            act.wait_ge(s_both, 1)

            def cell(c, n, seq, par):
                if seq >= 2:
                    act.wait_ge(s_cell, seq - 1)
                act.wait_ge(s_mm, seq + 1)
                for j in range(2):
                    nc.scalar.activation(gates[:, par, j, :], bank[4 * par + j][:, 0:CH], ACT.Sigmoid,
                                         bias=both[:, c, j:j + 1]).then_inc(s_rz, 1)
                act.wait_ge(s_pre, seq + 1)
                nc.scalar.activation(cand[:, par, :], cand[:, par, :], ACT.Tanh,
                                     bias=bias[:, c, 0, 2:3]).then_inc(s_n, 1)

            for c in range(LAYERS):
                for n in range(NC):
                    cell(c, n, c * NC + n, (c * NC + n) % 2)
            act.wait_ge(s_ln, LN_STEPS - 1)
            nc.scalar.activation(stat[0:NP, 2, :], stat[0:NP, 1, :], ACT.Sqrt).then_inc(s_sq, 1)

        @block.vector
        def _(dve):
            nc.vector.memset(xn[:, :, :], 0.0).then_inc(s_zero, 1)
            for t in (xt, aggt):
                nc.vector.memset(t[:, N:AW], 0.0)
            dve.wait_ge(s_w, LAYERS * 4 * 16)
            nc.vector.tensor_tensor(both[:, :, :], bias[:, :, 0, :], bias[:, :, 1, :], ALU.add).then_inc(s_both, 1)
            dve.wait_ge(s_load, (2 + K) * 16)
            nc.vector.tensor_tensor(tab[:, 0, :], tab[:, 0, :], tab[:, 1, :], ALU.add)
            nc.vector.tensor_tensor(tab[:, 2, :], tab[:, 2, :], tab[:, 3, :], ALU.add).then_inc(s_agg, 1)
            dve.wait_ge(s_agg, 1)
            nc.vector.tensor_tensor(tab[:, 0, :], tab[:, 0, :], tab[:, 2, :], ALU.add).then_inc(s_agg, 1)
            for j in range(5):
                lo, hi = 4 * j, min(4 * j + 4, 6 * LAYERS)
                dve.wait_ge(s_T, j + 1)
                nc.vector.tensor_copy(wt[:, :, :, :, :].rearrange("p c m g k -> p (c m g k)")[:, lo * P:hi * P],
                                      bank[j][:, 0:(hi - lo) * P]).then_inc(s_tc, 1)
            for q, dest in enumerate((xt, aggt)):
                for j, (b, nb) in enumerate(groups):
                    dve.wait_ge(s_T, 5 + q * NGR + j + 1)
                    nc.vector.tensor_copy(strided(dest, b, nb),
                                          bank[(5 + q * NGR + j) % 8][:, 0:nb * NP].rearrange("d (b p) -> d b p", b=nb)
                                          ).then_inc(s_tc, 1)

            def cell(c, n, seq, par, h, out):
                cols = slice(n * CH, (n + 1) * CH)
                dve.wait_ge(s_rz, seq * 2 + 2)
                nc.vector.scalar_tensor_tensor(out=diff[:, par, :], in0=bank[4 * par + 3][:, 0:CH],
                                               scalar=bias[:, c, 1, 2:3], in1=gates[:, par, 0, :],
                                               op0=ALU.add, op1=ALU.mult).then_inc(s_rh, 1)
                dve.wait_ge(s_rh, seq + 1)
                nc.vector.tensor_tensor(cand[:, par, :], diff[:, par, :], bank[4 * par + 2][:, 0:CH],
                                        ALU.add).then_inc(s_pre, 1)

            def blend(c, n, seq, par, h, out):
                cols = slice(n * CH, (n + 1) * CH)
                dve.wait_ge(s_n, seq + 1)
                nc.vector.tensor_tensor(diff[:, par, :], h[:, cols], cand[:, par, :], ALU.subtract).then_inc(s_d, 1)
                dve.wait_ge(s_d, seq * 2 + 1)
                nc.vector.tensor_tensor(diff[:, par, :], diff[:, par, :], gates[:, par, 1, :], ALU.mult).then_inc(s_d, 1)
                dve.wait_ge(s_d, seq * 2 + 2)
                nc.vector.tensor_tensor(out[:, cols], diff[:, par, :], cand[:, par, :], ALU.add).then_inc(s_cell, 1)

            todo = [(c, n, c * NC + n, (c * NC + n) % 2, (aggt, s1t, s2t)[c], (s1t, s2t, xt)[c])
                    for c in range(LAYERS) for n in range(NC)]
            for q, t in enumerate(todo):
                cell(*t)
                if q:
                    blend(*todo[q - 1])
            blend(*todo[-1])
            for j, (b, nb) in enumerate(groups):
                dve.wait_ge(s_back, j + 1)
                nc.vector.tensor_tensor(xn[0:NP, b:b + nb, :], xn[0:NP, b:b + nb, :],
                                        bank[j][0:NP, 0:nb * D].rearrange("p (b d) -> p b d", b=nb),
                                        ALU.add).then_inc(s_res, 1)
            dve.wait_ge(s_res, NGR)
            nc.vector.memset(x1[:, :, :], 0.0).then_inc(s_done, 1)
            dve.wait_ge(s_done, 1)
            last, _ = layer_norm(nc, dve, tab[0:NP, 1, :].rearrange("p (b d) -> p b d", b=NB),
                                 xn[0:NP, :, :], x1[0:NP, :, :], stat, s_ln, 0, (s_sq, 1))
            last.then_inc(s_done, 1)

        @block.tensor
        def _(pe):
            pe.wait_ge(s_const, 2)
            pe.wait_ge(s_w, LAYERS * 4 * 16)
            flat = wn[:, :, :, :, :].rearrange("p c m g k -> p (c m g k)")
            for j in range(5):
                for q in range(4 * j, min(4 * j + 4, 6 * LAYERS)):
                    last = nc.tensor.transpose(bank[j][:, (q % 4) * P:(q % 4 + 1) * P],
                                               flat[:, q * P:(q + 1) * P], ident[:, :])
                last.then_inc(s_T, 1)
            for q in range(2):
                pe.wait_ge(*((s_load, (2 + K) * 16) if q == 0 else (s_agg, 2)))
                for j, (b, nb) in enumerate(groups):
                    n = 5 + q * NGR + j
                    if n >= 8:
                        pe.wait_ge(s_tc, n - 7)
                    for t in range(nb):
                        src = xn[0:NP, b + t, :] if q == 0 else tab[0:NP, 0, (b + t) * D:(b + t + 1) * D]
                        last = nc.tensor.transpose(bank[n % 8][:, t * NP:(t + 1) * NP], src, ident[0:NP, 0:NP])
                    last.then_inc(s_T, 1)
            pe.wait_ge(s_tc, 5 + 2 * NGR)

            def cell(c, n, seq, par, x, h):
                cols = slice(n * CH, (n + 1) * CH)
                if seq >= 2:
                    pe.wait_ge(s_pre, seq - 1)
                if c:
                    pe.wait_ge(s_cell, (c - 1) * NC + n + 1)
                for j in range(2):
                    nc.tensor.matmul(bank[4 * par + j][:, 0:CH], wt[:, c, 0, j, :], x[:, cols], start=True, stop=False)
                    nc.tensor.matmul(bank[4 * par + j][:, 0:CH], wt[:, c, 1, j, :], h[:, cols], start=False, stop=True)
                nc.tensor.matmul(bank[4 * par + 2][:, 0:CH], wt[:, c, 0, 2, :], x[:, cols], start=True, stop=True)
                nc.tensor.matmul(bank[4 * par + 3][:, 0:CH], wt[:, c, 1, 2, :], h[:, cols],
                                 start=True, stop=True).then_inc(s_mm, 1)

            for c in range(LAYERS):
                for n in range(NC):
                    cell(c, n, c * NC + n, (c * NC + n) % 2, (xt, aggt, s1t)[c], (aggt, s1t, s2t)[c])
            pe.wait_ge(s_cell, LAYERS * NC)
            for j, (b, nb) in enumerate(groups):
                for t in range(nb):
                    last = nc.tensor.transpose(bank[j][0:NP, t * D:(t + 1) * D],
                                               strided(xt, b + t, 1).rearrange("d b p -> d (b p)"), ident[:, :])
                last.then_inc(s_back, 1)


def sum_stage(nc, a, adj_flat, x1, out):
    ctx = ExitStack()
    with ctx:
        def sb(name, shape, dt=fp32):
            return ctx.enter_context(nc.sbuf_tensor(name, shape, dt))

        def sem(name):
            return ctx.enter_context(nc.semaphore(name))

        PB = 5
        ident = sb("sident", [P, P])
        panel = [sb(f"panel{i}", [P, AW]) for i in range(PB)]
        xb = [sb(f"xb{i}", [P, D]) for i in range(PB)]
        xn = sb("xn2", [P, NB, D])
        xt = sb("xt2", [P, AW])
        zt = sb("zt", [P, AW])
        ht = sb("ht", [P, AW])
        w = sb("wl", [P, LAYERS, 2, D])
        bl = sb("bl", [P, LAYERS, 2])
        eps = sb("eps", [P, LAYERS])
        stat = sb("sstat", [P, 4, NB])
        sq = sb("sq", [P, NB, D])
        bank = [ctx.enter_context(nc.psum_tensor(f"sbank{i}", [P, 512], fp32)) for i in range(8)]

        s_const = sem("l_const")
        s_w = sem("l_w")
        s_pan = [sem(f"l_pan{i}") for i in range(PB)]
        s_xb = sem("l_xb")
        s_use = sem("l_use")
        s_T = sem("l_T")
        s_tc = sem("l_tc")
        s_eps = sem("l_eps")
        s_z = sem("l_z")
        s_a = sem("l_a")
        s_h = sem("l_h")
        s_b = sem("l_b")
        s_x = sem("l_x")
        s_back = sem("l_back")
        s_xn = sem("l_xn")
        s_ln = sem("l_ln")
        s_sq = sem("l_sq")
        s_fin = sem("l_fin")
        s_out = sem("l_out")
        groups = block_groups()
        NGR = len(groups)
        NC = AW // CH
        adj = adj_flat[0:NR * AW, :].rearrange("(p b c) o -> b p (c o)", b=NB, c=AW)

        block = ctx.enter_context(nc.Block())

        @block.sync
        def _(sp):
            for i in range(PB):
                sp.dma_start(panel[i][:, :], adj[i]).then_inc(s_pan[i], 16)
            for l in range(LAYERS):
                for t in range(NB // PB):
                    if l or t:
                        for i in range(PB):
                            sp.wait_ge(s_use, (l * NB + t * PB) - PB + i + 1)
                            sp.dma_start(panel[i][:, :], adj[t * PB + i]).then_inc(s_pan[i], 16)
            for p0, p1 in ((0, 112), (112, NP)):
                sp.wait_ge(s_fin, 1)
                sp.dma_start(rows_of(out, p0, p1), xn[p0:p1, :, :]).then_inc(s_out, 16)
            sp.wait_ge(s_out, 32)

        @block.gpsimd
        def _(pool):
            nc.gpsimd.memset(ident[:, :], 0.0).then_inc(s_const, 1)
            pool.wait_ge(s_const, 1)
            nc.gpsimd.affine_select(out=ident[:, :], in_=ident[:, :], compare_op=ALU.not_equal, fill=1.0,
                                    base=0, pattern=[[-1, P]], channel_multiplier=1).then_inc(s_const, 1)

        @block.scalar
        def _(act):
            for m in range(2):
                act.dma_start(w[:, :, m, :], a[f"L1_gnn_W{m + 1}"].rearrange("l k n -> k l n")).then_inc(s_w, 16)
                with nc.allow_non_contiguous_dma(reason="384 biases"):
                    act.dma_start(bl[:, :, m], a[f"L1_gnn_b{m + 1}"].rearrange("l p -> p l")).then_inc(s_w, 16)
            act.dma_start(eps[:, :], a["L1_gnn_eps"].partition_broadcast(P)).then_inc(s_w, 16)
            act.wait_ge(s_w, 5 * 16)
            for l in range(LAYERS):
                src = x1 if l == 0 else xn
                if l:
                    act.wait_ge(s_xn, l * NGR + 1)
                for b in range(NB):
                    i = b % PB
                    if l * NB + b >= PB:
                        act.wait_ge(s_use, l * NB + b - PB + 1)
                    nc.scalar.copy(xb[i][:, :], src[:, b, :]).then_inc(s_xb, 1)
                for n in range(NC):
                    act.wait_ge(s_a, l * NC + n + 1)
                    nc.scalar.activation(ht[:, n * CH:(n + 1) * CH], bank[n][:, 0:CH], ACT.Relu,
                                         bias=bl[:, l, 0:1]).then_inc(s_h, 1)
                for n in range(NC):
                    act.wait_ge(s_b, l * NC + n + 1)
                    nc.scalar.activation(xt[:, n * CH:(n + 1) * CH], bank[n][:, 0:CH], ACT.Identity,
                                         bias=bl[:, l, 1:2]).then_inc(s_x, 1)
            act.wait_ge(s_ln, LN_STEPS - 1)
            nc.scalar.activation(stat[0:NP, 2, :], stat[0:NP, 1, :], ACT.Sqrt).then_inc(s_sq, 1)

        @block.vector
        def _(dve):
            dve.wait_ge(s_w, 5 * 16)
            nc.vector.tensor_scalar(eps[:, :], eps[:, :], 1.0, None, ALU.add).then_inc(s_eps, 1)
            nc.vector.memset(xt[:, N:AW], 0.0)
            nc.vector.memset(xn[:, :, :], 0.0).then_inc(s_xn, 1)
            for j, (b, nb) in enumerate(groups):
                dve.wait_ge(s_T, j + 1)
                nc.vector.tensor_copy(strided(xt, b, nb), bank[j][:, 0:nb * NP].rearrange("d (b p) -> d b p", b=nb)
                                      ).then_inc(s_tc, 1)
            dve.wait_ge(s_eps, 1)
            dve.wait_ge(s_tc, NGR)
            dve.wait_ge(s_xn, 1)
            for l in range(LAYERS):
                dve.wait_ge(s_use, (l + 1) * NB)
                if l:
                    dve.wait_ge(s_x, l * NC)
                for n in range(NC):
                    cols = slice(n * CH, (n + 1) * CH)
                    nc.vector.scalar_tensor_tensor(out=zt[:, cols], in0=xt[:, cols], scalar=eps[:, l:l + 1],
                                                   in1=bank[n][:, 0:CH], op0=ALU.mult, op1=ALU.add).then_inc(s_z, 1)
                for j, (b, nb) in enumerate(groups):
                    dve.wait_ge(s_back, l * NGR + j + 1)
                    got = bank[j][0:NP, 0:nb * D].rearrange("p (b d) -> p b d", b=nb)
                    if l < LAYERS - 1:
                        nc.vector.tensor_copy(xn[0:NP, b:b + nb, :], got).then_inc(s_xn, 1)
                    else:
                        nc.vector.tensor_tensor(xn[0:NP, b:b + nb, :], x1[0:NP, b:b + nb, :], got,
                                                ALU.add).then_inc(s_xn, 1)
            dve.wait_ge(s_xn, 1 + LAYERS * NGR)
            last, _ = layer_norm(nc, dve, sq[0:NP, :, :],
                                 xn[0:NP, :, :], xn[0:NP, :, :], stat, s_ln, 0, (s_sq, 1))
            last.then_inc(s_fin, 1)

        @block.tensor
        def _(pe):
            pe.wait_ge(s_const, 2)
            for j, (b, nb) in enumerate(groups):
                for t in range(nb):
                    last = nc.tensor.transpose(bank[j][:, t * NP:(t + 1) * NP], x1[0:NP, b + t, :], ident[0:NP, 0:NP])
                last.then_inc(s_T, 1)
            pe.wait_ge(s_tc, NGR)
            pe.wait_ge(s_w, 5 * 16)
            for l in range(LAYERS):
                for b in range(NB):
                    i, seq = b % PB, l * NB + b
                    pe.wait_ge(s_pan[i], (seq // PB + 1) * 16)
                    pe.wait_ge(s_xb, seq + 1)
                    for n in range(NC):
                        if b == 0 and l:
                            pe.wait_ge(s_xn, 1 + l * NGR)
                        last = nc.tensor.matmul(bank[n][:, 0:CH], xb[i][:, :], panel[i][:, n * CH:(n + 1) * CH],
                                                start=(b == 0), stop=(b == NB - 1))
                    last.then_inc(s_use, 1)
                for n in range(NC):
                    pe.wait_ge(s_z, l * NC + n + 1)
                    nc.tensor.matmul(bank[n][:, 0:CH], w[:, l, 0, :], zt[:, n * CH:(n + 1) * CH],
                                     start=True, stop=True).then_inc(s_a, 1)
                for n in range(NC):
                    pe.wait_ge(s_h, l * NC + n + 1)
                    nc.tensor.matmul(bank[n][:, 0:CH], w[:, l, 1, :], ht[:, n * CH:(n + 1) * CH],
                                     start=True, stop=True).then_inc(s_b, 1)
                pe.wait_ge(s_x, (l + 1) * NC)
                for j, (b, nb) in enumerate(groups):
                    for t in range(nb):
                        last = nc.tensor.transpose(bank[j][0:NP, t * D:(t + 1) * D],
                                                   strided(xt, b + t, 1).rearrange("d b p -> d (b p)"), ident[:, :])
                    last.then_inc(s_back, 1)


def gnn_kernel(nc, a, out):
    adj_flat = nc.dram_tensor("adj", (ASIZE, 1), fp32, kind="Internal").ap()
    tables = [nc.dram_tensor(f"sums{k}", (AROWS, D), fp32, kind="Internal").ap() for k in range(K)]
    with nc.sbuf_tensor("x1", [P, NB, D], fp32) as x1:
        edge_stage(nc, a, adj_flat, tables)
        gru_stage(nc, a, tables, x1)
        sum_stage(nc, a, adj_flat, x1, out)


_INS = (["x", "src", "dst", "edge_attr_128"] + [f"L0_gnn_{k}{i}" for i in (1, 2, 3) for k in "wb"]
        + [f"L0_gnn_g{i}_{k}" for i in range(3) for k in ("wih", "whh", "bih", "bhh")]
        + ["L1_gnn_eps", "L1_gnn_W1", "L1_gnn_b1", "L1_gnn_W2", "L1_gnn_b2"])


def kernel(**inputs):
    import numpy as _np
    import concourse.bacc as _bacc
    from concourse import mybir as _mybir
    from concourse.bass_utils import run_bass_kernel_spmd as _run

    nc = _bacc.Bacc("TRN2", target_bir_lowering=False, num_devices=1)
    arrays, aps = {}, {}
    for name in _INS:
        v = _np.ascontiguousarray(inputs[name])
        arrays[f"in_{name}"] = v
        aps[name] = nc.dram_tensor(f"in_{name}", v.shape, _mybir.dt.from_np(v.dtype), kind="ExternalInput").ap()
    out = nc.dram_tensor("out_0", (N, D), fp32, kind="ExternalOutput").ap()
    gnn_kernel(nc, aps, out)
    r = _run(nc, [arrays], core_ids=[0])
    return r.results[0]["out_0"]
```

```python
import numpy as np
import concourse.bass as bass
from concourse import mybir
from contextlib import ExitStack

fp32 = mybir.dt.float32
f32r = mybir.dt.float32r
i32 = mybir.dt.int32
ALU = mybir.AluOpType
ACT = mybir.ActivationFunctionType
AX = mybir.AxisListType

P = 128
D = 128
H = 256
HB = H // P
N = 3125
E = 53125
EARLY = 6
ZG = 6
K = 4
GE = K * P
G = (E + GE - 1) // GE
LAST = E - (G - 1) * GE
PAD = N
AW = 3136
DUMMY = PAD + 1
AROWS = 3328
NR = 3200
PADS = [P - (LAST - k + K - 1) // K for k in range(K)]
PAD_SURPLUS = sum(n * (n - 1) for n in PADS)
ADUMMY = NR * AW
ZW = AROWS * D // P
AZ = -(-(ADUMMY + P) // (P * ZW))
ASIZE = AZ * P * ZW
NP = 125
NB = N // NP
CH = 448
CHUNKS = [(c, min(CH, N - c)) for c in range(0, N, CH)]
LAYERS = 3
EPS = 1e-5


def add_pairs(pool, adj_flat, places, counts, s_adj):
    pool.indirect_dma_start(out=adj_flat, out_offset=bass.IndirectOffsetOnAxis(ap=places, axis=0),
                            in_=counts, in_offset=None, compute_op=ALU.add).then_inc(s_adj, 16)


def edge_stage(nc, a, adj_flat, tables, early_to, early_n, npairs, s_adj):
    ctx = ExitStack()
    with ctx:
        def sb(name, shape, dt=fp32):
            return ctx.enter_context(nc.sbuf_tensor(name, shape, dt))

        def sem(name):
            return ctx.enter_context(nc.semaphore(name))

        ident = sb("ident", [P, P])
        lower = sb("lower", [P, P])
        column = sb("column", [P, P])
        place = sb("place", [P, 1])
        count_i = sb("count_i", [P, P + 4], i32)
        ones = sb("ones", [P, P])
        ones_r = sb("ones_r", [P, P], f32r)
        w1n = sb("w1n", [P, HB, 3 * D])
        w2n = sb("w2n", [P, HB, H])
        w3n = sb("w3n", [P, H])
        whalf = sb("whalf", [P, HB, 2, D])
        wfirst = sb("wfirst", [P, HB, 3, P])
        w2h = sb("w2h", [P, HB, HB, P], f32r)
        w2l = sb("w2l", [P, HB, HB, P], f32r)
        w3t = sb("w3t", [P, HB, P])
        b1c = sb("b1c", [P, HB])
        b2c = sb("b2c", [P, HB])
        b3r = sb("b3r", [P, D])
        b3p = sb("b3p", [P, 3, D])
        b3hl = sb("b3hl", [P, K, D], f32r)
        zero = sb("zero", [P, ZW])
        rows_i = sb("rows_i", [G, 2, GE], i32)
        rows_f = sb("rows_f", [G, 2, GE])
        rows_r = sb("rows_r", [G, 2, K, P], f32r)
        keys = sb("keys", [P, G, 3, K])
        away = sb("away", [P, G, 3, K])
        dummy = sb("dummyf", [P, 3])
        lows = sb("lows", [G, 4])
        diag = sb("diag", [G, G + 1])
        base_f = sb("base_f", [P, G])
        base_i = sb("base_i", [1, G], i32)
        wnode = sb("wnode", [P, G])
        inwin = sb("inwin", [P, G, K])
        fits = sb("fits", [1, 1], i32)
        gidx = [sb(f"gidx{i}", [P, 2, K], i32) for i in range(3)]
        xg = [sb(f"xg{i}", [P, 2, K, D]) for i in range(2)]
        xw = [sb(f"xw{i}", [P, D]) for i in range(2)]
        ef = [sb(f"ef{i}", [P, K, D]) for i in range(2)]
        same = [sb(f"same{i}", [P, 2, K, P]) for i in range(2)]
        target = [sb(f"target{i}", [P, 3, K], i32) for i in range(2)]
        pairs = [sb(f"pairs{i}", [P, K]) for i in range(2)]
        rowto = [sb(f"rowto{i}", [P, 2, K], i32) for i in range(2)]
        outb = [sb(f"outb{i}", [P, 2, K, D]) for i in range(2)]
        sel = [sb(f"sel{i}", [G, P], f32r) for i in range(2)]
        sd = sb("sd", [P, 2, K, D])
        xwh = sb("xwh", [P, D], f32r)
        xwl = sb("xwl", [P, D], f32r)
        hot = sb("hot", [P, GE], f32r)
        samed = sb("samed", [P, K, P])
        sdet = sb("sdet", [P, 3, GE])
        pb = sb("pb", [P, HB, GE])
        hpre = sb("hpre", [P, HB, 2, GE])
        h1h = sb("h1h", [P, 2, HB, GE], f32r)
        h1l = sb("h1l", [P, 2, HB, GE], f32r)
        h2 = sb("h2", [P, 2, HB, GE])
        es = sb("es", [P, 2, GE])
        match = sb("match", [P, 4, K, P])
        found = sb("found", [P, 4, K])
        shift = sb("shift", [P, 3, K])
        bank = [ctx.enter_context(nc.psum_tensor(f"ebank{i}", [P, 512], fp32)) for i in range(8)]

        s_const = sem("s_const")
        s_wload = sem("s_wload")
        s_iload = sem("s_iload")
        s_zero = sem("s_zero")
        s_ztab = sem("s_ztab")
        s_zadj = sem("s_zadj")
        s_whalf = sem("s_whalf")
        s_wT = sem("s_wT")
        s_wc = sem("s_wc")
        s_rows = sem("s_rows")
        s_diag = sem("s_diag")
        s_bases = sem("s_bases")
        s_fits = sem("s_fits")
        s_dve = sem("s_dve")
        s_gidx = [sem(f"s_gidx{i}") for i in range(3)]
        s_ef = [sem(f"s_ef{i}") for i in range(2)]
        s_xw = [sem(f"s_xw{i}") for i in range(2)]
        s_x = [sem(f"s_x{i}") for i in range(2)]
        s_xh = sem("s_xh")
        s_xl = sem("s_xl")
        s_sd = sem("s_sd")
        s_sel = sem("s_sel")
        s_sdT = sem("s_sdT")
        s_eT = sem("s_eT")
        s_tev = sem("s_tev")
        s_row = sem("s_row")
        s_roww = sem("s_roww")
        s_hot = sem("s_hot")
        s_cmp = sem("s_cmp")
        s_cs = sem("s_cs")
        s_tgt = sem("s_tgt")
        s_p = sem("s_p")
        s_q = sem("s_q")
        s_pc = sem("s_pc")
        s_hp = sem("s_hp")
        s_h1 = sem("s_h1")
        s_h1l = sem("s_h1l")
        s_l2 = sem("s_l2")
        s_h2 = sem("s_h2")
        s_l3 = sem("s_l3")
        s_es = sem("s_es")
        s_sum = sem("s_sum")
        s_out = sem("s_out")
        s_rowto = sem("s_rowto")
        s_add = [sem(f"s_add{k}") for k in range(K + 1)]
        s_pace = sem("s_pace")

        block = ctx.enter_context(nc.Block())

        def wait_added(eng, g, win):
            for k in range(K + 1 if win else K):
                eng.wait_ge(s_add[k], (g - 1) * (16 if win else 32))

        @block.sync
        def _(sp):
            w1v = a["L0_gnn_w1"].rearrange("(f p) c -> p f c", p=P)
            sp.wait_ge(s_zero, 2)
            nf = (G - 1) // 16 * 16
            for s, name in enumerate(("src", "dst")):
                full = a[name][0:(G - 1) * GE].rearrange("(g e) -> g e", e=GE)
                sp.dma_start(rows_i[0:nf, s, :], full[0:nf, :]).then_inc(s_iload, 16)
                sp.dma_start(rows_i[nf:G - 1, s, :], full[nf:G - 1, :]).then_inc(s_iload, 16)
                sp.dma_start(rows_i[G - 1:G, s, 0:LAST],
                             a[name][(G - 1) * GE:E].rearrange("(g e) -> g e", g=1)).then_inc(s_iload, 16)

            def indices(g, par, s):
                sp.dma_start(gidx[par][:, s, :],
                             a[("src", "dst")[s]][bass.ds(g * GE, GE)].rearrange("(p k) -> p k", k=K)
                             ).then_inc(s_gidx[par], 16)

            def features(g, par):
                sp.dma_start(ef[par][:, :, :],
                             a["edge_attr_128"][bass.ds(g * GE, GE), :].rearrange("(p k) d -> p k d", k=K)
                             ).then_inc(s_ef[par], 16)

            for g in range(2):
                for s in range(2):
                    indices(g, g, s)
                features(g, g)
            sp.dma_start(w1n[:, :, :], w1v).then_inc(s_wload, 16)
            sp.dma_start(w2n[:, :, :], a["L0_gnn_w2"].rearrange("(f p) c -> p f c", p=P)).then_inc(s_wload, 16)
            sp.dma_start(w3n[:, :], a["L0_gnn_w3"]).then_inc(s_wload, 16)
            with nc.allow_non_contiguous_dma(reason="256 biases"):
                sp.dma_start(b1c[:, :], a["L0_gnn_b1"].rearrange("(f p) -> p f", p=P)).then_inc(s_wload, 16)
                sp.dma_start(b2c[:, :], a["L0_gnn_b2"].rearrange("(f p) -> p f", p=P)).then_inc(s_wload, 16)
            sp.dma_start(b3r[:, :], a["L0_gnn_b3"].partition_broadcast(P)).then_inc(s_wload, 16)
            fp, one, base = LAST // K, LAST % K, (G - 1) * GE
            for s, name in enumerate(("src", "dst")):
                sp.dma_start(gidx[2][0:fp, s, :],
                             a[name][base:base + fp * K].rearrange("(p k) -> p k", k=K)).then_inc(s_gidx[2], 16)
                sp.dma_start(gidx[2][fp:fp + 1, s, 0:one],
                             a[name][base + fp * K:E].rearrange("(p k) -> p k", p=1)).then_inc(s_gidx[2], 16)

            def program(win):
                def window(g, par):
                    base = sp.value_load(base_i[0:1, bass.ds(g, 1)], min_val=0, max_val=N - P)
                    sp.dma_start(xw[par][:, :], a["x"][bass.ds(base, P), :]).then_inc(s_xw[par], 16)

                def reload(g, par, turn):
                    sp.wait_ge(s_x[par], turn * ((1 if win else 2) * K * 16))
                    indices(g, par, 0)
                    if not win:
                        indices(g, par, 1)
                    sp.wait_ge(s_eT, g - 1)
                    features(g, par)
                    if win:
                        sp.wait_ge(s_xl, g - 1)
                        window(g, par)

                if win:
                    window(0, 0)
                    window(1, 1)
                sp.wait_ge(s_zero, 3)
                for k in range(K + 1):
                    sp.dma_start(tables[k].rearrange("(p r) d -> p (r d)", p=P), zero[:, :]).then_inc(s_ztab, 16)
                adj_z = adj_flat.rearrange("(s p c) o -> s p (c o)", s=AZ, p=P)
                for g in range(2, 2 + ZG):
                    for s in range((g - 2) * AZ // ZG, (g - 1) * AZ // ZG):
                        sp.dma_start(adj_z[s], zero[:, :]).then_inc(s_zadj, 16)
                    reload(g, g % 2, g // 2)
                with sp.Fori((2 + ZG) // 2, (G - 2) // 2) as i:
                    for par in range(2):
                        reload(i * 2 + par, par, i)
                reload(G - 2, 0, (G - 2) // 2)
                sp.wait_ge(s_eT, G - 2)
                sp.dma_start(ef[1][0:fp, :, :],
                             a["edge_attr_128"][base:base + fp * K, :].rearrange("(p k) d -> p k d", k=K)
                             ).then_inc(s_ef[1], 16)
                sp.dma_start(ef[1][fp:fp + 1, 0:one, :],
                             a["edge_attr_128"][base + fp * K:E, :].rearrange("(p k) d -> p k d", p=1)
                             ).then_inc(s_ef[1], 16)
                if win:
                    sp.wait_ge(s_xl, G - 2)
                    window(G - 1, 1)

            sp.wait_ge(s_fits, 1)
            flag = sp.value_load(fits[0:1, 0:1], min_val=0, max_val=1)
            with sp.If(flag > 0):
                program(True)
            with sp.Else():
                program(False)

        @block.gpsimd
        def _(pool):
            nc.gpsimd.memset(ident[:, :], 0.0).then_inc(s_const, 1)
            nc.gpsimd.memset(lower[:, :], 1.0).then_inc(s_const, 1)
            nc.gpsimd.iota(count_i[:, 0:P], pattern=[[1, P]], base=0, channel_multiplier=0).then_inc(s_const, 1)
            for j, base in enumerate((DUMMY, DUMMY, ADUMMY, 0)):
                nc.gpsimd.iota(count_i[:, P + j:P + j + 1], pattern=[[0, 1]], base=base,
                               channel_multiplier=1).then_inc(s_const, 1)
            pool.wait_ge(s_const, 7)
            nc.gpsimd.affine_select(out=ident[:, :], in_=ident[:, :], compare_op=ALU.not_equal, fill=1.0,
                                    base=0, pattern=[[-1, P]], channel_multiplier=1).then_inc(s_const, 1)
            nc.gpsimd.affine_select(out=lower[:, :], in_=lower[:, :], compare_op=ALU.is_gt, fill=0.0,
                                    base=0, pattern=[[-1, P]], channel_multiplier=1).then_inc(s_const, 1)

            def program(win):
                def gather(par, k, ids):
                    for s in range(1 if win else 2):
                        pool.indirect_dma_start(
                            out=xg[par][:, s, k, :], out_offset=None, in_=a["x"],
                            in_offset=bass.IndirectOffsetOnAxis(ap=ids[:, s, k:k + 1], axis=0)
                        ).then_inc(s_x[par], 16)

                def plain():
                    pool.sem_inc(s_pace, 1)

                def pair(g, par, k):
                    pool.wait_ge(s_adj, ((g - EARLY) * K + k) * 16)
                    plain()
                    add_pairs(pool, adj_flat, target[par][:, 2, k:k + 1], pairs[par][:, k:k + 1], s_adj)

                def add(g, par, way, k):
                    if win and way == 0:
                        table, before = K, g
                    elif win:
                        table, before = k, g
                    else:
                        table, before = k, g * 2 + (way if k < K // 2 else 1 - way)
                    pool.wait_ge(s_add[table], before * 16)
                    plain()
                    pool.indirect_dma_start(
                        out=tables[table],
                        out_offset=bass.IndirectOffsetOnAxis(ap=rowto[par][:, way, k:k + 1], axis=0),
                        in_=outb[par][:, way, k, :], in_offset=None, compute_op=ALU.add).then_inc(s_add[table], 16)

                def turn(j, par, turns, gathers=True, pairing=True, adding=True):
                    if gathers == "last":
                        pool.wait_ge(s_gidx[2], 64)
                    elif gathers and win:
                        pool.wait_ge(s_gidx[par], turns * 16 + 48)
                    elif gathers:
                        pool.wait_ge(s_gidx[par], turns * 32 + 64)
                    if gathers:
                        pool.wait_ge(s_sdT if win else s_sd, j * 2 + 1 if win else j + 1)
                    if pairing:
                        pool.wait_ge(s_tgt, j + 1)
                    if adding:
                        pool.wait_ge(s_out, (j - 1) * 2 + 2)
                        pool.wait_ge(s_rowto, j)
                    plain()
                    for k in range(K):
                        if gathers:
                            gather(par, k, gidx[2] if gathers == "last" else gidx[par])
                        if adding and (k == 0 or not win):
                            add(j - 1, 1 - par, 0, k)
                        if pairing:
                            pair(j, par, k)
                        if adding:
                            add(j - 1, 1 - par, 1, (k + K // 2) % K)

                for par in range(2):
                    pool.wait_ge(s_gidx[par], 32)
                    for k in range(K):
                        gather(par, k, gidx[par])
                turn(0, 0, 0, pairing=False, adding=False)
                pool.wait_ge(s_ztab, (K + 1) * 16)
                for j in range(1, EARLY):
                    turn(j, j % 2, j // 2, pairing=False)
                pool.wait_ge(s_zadj, AZ * 16)
                turn(EARLY, 0, EARLY // 2)
                turn(EARLY + 1, 1, EARLY // 2)
                with pool.Fori(EARLY // 2 + 1, (G - 4) // 2) as i:
                    for par in range(2):
                        turn(i * 2 + par, par, i)
                turn(G - 4, 0, (G - 4) // 2)
                turn(G - 3, 1, 0, gathers="last")
                turn(G - 2, 0, 0, gathers=False)
                turn(G - 1, 1, 0, gathers=False)
                turn(G, 0, 0, gathers=False, pairing=False)
                for k in range(K + 1 if win else K):
                    pool.wait_ge(s_add[k], G * (16 if win else 32))

            pool.wait_ge(s_fits, 1)
            flag = pool.value_load(fits[0:1, 0:1], min_val=0, max_val=1)
            with pool.If(flag > 0):
                program(True)
            with pool.Else():
                program(False)
            pool.wait_ge(s_adj, (G - EARLY) * K * 16)

        @block.scalar
        def _(act):
            def program(win):
                def evac(g, j):
                    act.wait_ge((s_sdT, s_sdT, s_eT)[j], (g * 2 + (j + 1)) if j < 2 else (g + 1))
                    if win and j == 0:
                        nc.scalar.copy(sd[:, 0, :, :].rearrange("p k d -> p (k d)"), bank[0][:, :]).then_inc(s_tev, 1)
                    else:
                        nc.scalar.copy(sdet[:, j, :], bank[(0, 1, 0)[j]][:, :]).then_inc(s_tev, 1)

                def upper(g, par, turns):
                    act.wait_ge(s_xw[par], turns * 16 + 16)
                    if not (isinstance(g, int) and g == 0):
                        act.wait_ge(s_sdT, g * 2)
                    nc.scalar.copy(xwh[:, :], xw[par][:, :]).then_inc(s_xh, 1)

                def first(g):
                    for f in range(HB):
                        act.wait_ge(s_p, g * HB + (f + 1))
                        nc.scalar.activation(pb[:, f, :], bank[2 + 2 * f][:, :], ACT.Identity,
                                             bias=b1c[:, f:f + 1]).then_inc(s_pc, 1)
                    act.wait_ge(s_l2, g * 4)
                    for f in range(HB):
                        act.wait_ge(s_hp, g * HB + (f + 1))
                        for way in range(2):
                            nc.scalar.activation(h1h[:, way, f, :], hpre[:, f, way, :], ACT.Relu).then_inc(s_h1, 1)

                def second(g, n):
                    way, f = divmod(n, HB)
                    act.wait_ge(s_l2, g * 4 + (n + 1))
                    act.wait_ge(s_l3, g * 2)
                    nc.scalar.activation(h2[:, way, f, :], bank[6 + f][:, :], ACT.Relu,
                                         bias=b2c[:, f:f + 1]).then_inc(s_h2, 1)

                def results(g):
                    for way in range(2):
                        act.wait_ge(s_l3, g * 2 + (way + 1))
                        if way == 0:
                            act.wait_ge(s_sum, g * 2)
                        nc.scalar.copy(es[:, way, :], bank[6 + way][:, :]).then_inc(s_es, 1)

                def sums(g, par, early=False):
                    if not early:
                        wait_added(act, g, win)
                    for way in range(2):
                        act.wait_ge(s_sum, g * 2 + (way + 1))
                        used = D if win and way == 0 else K * D
                        nc.scalar.copy(outb[par][:, way, :, :].rearrange("p k d -> p (k d)")[:, 0:used],
                                       bank[way][:, 0:used]).then_inc(s_out, 1)

                def turn(g, par, turns, ahead=2, early=False):
                    if ahead:
                        evac(g + 1, 0)
                        if not win:
                            evac(g + 1, 1)
                    second(g, 0)
                    if ahead:
                        evac(g + 1, 2)
                    for n in range(1, 4):
                        second(g, n)
                    if ahead:
                        first(g + 1)
                    results(g)
                    sums(g, par, early)
                    if win and ahead == 2:
                        upper(g + 2, par, turns + 1)

                if win:
                    upper(0, 0, 0)
                evac(0, 0)
                if not win:
                    evac(0, 1)
                evac(0, 2)
                first(0)
                if win:
                    upper(1, 1, 0)
                turn(0, 0, 0, early=True)
                turn(1, 1, 0, early=True)
                with act.Fori(1, (G - 2) // 2) as i:
                    for par in range(2):
                        turn(i * 2 + par, par, i)
                turn(G - 2, 0, 0, ahead=1)
                turn(G - 1, 1, 0, ahead=0)

            act.wait_ge(s_wload, 6 * 16)
            act.wait_ge(s_fits, 1)
            flag = act.value_load(fits[0:1, 0:1], min_val=0, max_val=1)
            with act.If(flag > 0):
                program(True)
            with act.Else():
                program(False)

        @block.vector
        def _(dve):
            steps = [0]

            def step(ins):
                steps[0] += 1
                ins.then_inc(s_dve, 1)
                dve.wait_ge(s_dve, steps[0])

            nc.vector.memset(rows_i[:, :, :], PAD).then_inc(s_zero, 1)
            nc.vector.memset(gidx[2][:, :, :], 0).then_inc(s_zero, 1)
            nc.vector.memset(zero[:, :], 0.0).then_inc(s_zero, 1)
            nc.vector.memset(ones[:, :], 1.0)
            nc.vector.memset(npairs[:, :], 0.0)
            step(nc.vector.memset(sd[:, :, :, :], 1.0))
            nc.vector.tensor_copy(ones_r[:, :], sd[:, 0, 0, :])
            dve.wait_ge(s_const, 9)
            nc.vector.tensor_copy(column[:, :], count_i[:, 0:P])
            nc.vector.tensor_copy(dummy[:, :], count_i[:, P:P + 3])
            step(nc.vector.tensor_copy(place[:, :], count_i[:, P + 3:P + 4]))
            dve.wait_ge(s_iload, 6 * 16)
            step(nc.vector.tensor_copy(rows_f[:, :, :], rows_i[:, :, :]))
            for s in range(2):
                nc.vector.tensor_copy(rows_r[:, s, :, :],
                                      rows_f[:, s, :].rearrange("g (p k) -> g k p", k=K)).then_inc(s_rows, 1)
            nc.vector.tensor_reduce(lows[:, 0:1], rows_f[:, 1, :], axis=AX.X, op=ALU.min)
            step(nc.vector.scalar_tensor_tensor(out=hpre[0:G, 0, 0, :], in0=rows_f[:, 1, :], scalar=float(N),
                                                in1=rows_f[:, 1, :], op0=ALU.is_lt, op1=ALU.mult))
            nc.vector.tensor_reduce(lows[:, 1:2], hpre[0:G, 0, 0, :], axis=AX.X, op=ALU.max)
            step(nc.vector.tensor_scalar(lows[:, 2:3], lows[:, 0:1], float(N - P), None, ALU.min))
            step(nc.vector.tensor_tensor(lows[:, 3:4], lows[:, 1:2], lows[:, 2:3], ALU.subtract))
            nc.vector.tensor_scalar(diag[:, G:G + 1], lows[:, 3:4], float(P - 1), None, ALU.is_le)
            nc.vector.tensor_scalar(diag[:, 0:G], ident[0:G, 0:G], lows[:, 2:3], None, ALU.mult).then_inc(s_diag, 1)
            dve.wait_ge(s_bases, 1)
            nc.vector.tensor_copy(base_f[:, :], bank[7][:, 0:G])
            nc.vector.tensor_copy(base_i[:, :], bank[7][0:1, 0:G])
            step(nc.vector.tensor_scalar(fits[:, :], bank[7][0:1, G:G + 1], float(G), None, ALU.is_ge))
            nc.vector.tensor_scalar(wnode[:, :], base_f[:, :], place[:, :], None, ALU.add).then_inc(s_fits, 1)
            dve.wait_ge(s_wT, 2)
            for s in range(2):
                nc.vector.tensor_copy(keys[:, :, 1 - s, :], bank[s][:, 0:K * G].rearrange("p (k g) -> p g k", k=K)
                                      ).then_inc(s_wc, 1)
            dve.wait_ge(s_wc, 2)
            step(nc.vector.tensor_tensor(inwin[:, :, :], keys[:, :, 0, :],
                                         base_f[:, :].unsqueeze(2).broadcast_to([P, G, K]), ALU.subtract))
            step(nc.vector.tensor_scalar(away[:, :, 2, :], keys[:, :, 1, :], float(AW), None, ALU.mult))
            step(nc.vector.tensor_tensor(keys[:, :, 2, :], away[:, :, 2, :], keys[:, :, 0, :], ALU.add))
            for j in range(3):
                last = nc.vector.tensor_scalar(away[:, :, j, :], keys[:, :, j, :], -1.0, dummy[:, j:j + 1],
                                               ALU.mult, ALU.add)
            step(last)
            dve.wait_ge(s_wload, 6 * 16)
            for f in range(HB):
                step(nc.vector.tensor_tensor(whalf[:, f, 0, :], w1n[:, f, 0:D], w1n[:, f, D:2 * D], ALU.add))
                step(nc.vector.tensor_tensor(whalf[:, f, 1, :], w1n[:, f, 0:D], w1n[:, f, D:2 * D], ALU.subtract))
            nc.vector.tensor_scalar(whalf[:, :, :, :], whalf[:, :, :, :], 0.5, None, ALU.mult).then_inc(s_whalf, 1)
            step(nc.vector.tensor_scalar(b3p[:, 0, :], b3r[:, :], 1.0 / 64, None, ALU.mult))
            wide = lambda v, n: v.unsqueeze(1).broadcast_to([n, K, D])
            step(nc.vector.tensor_copy(b3hl[:, :, :], wide(b3p[:, 0, :], P)))
            step(nc.vector.tensor_tensor(b3p[:, 1, :], b3p[:, 0, :], b3hl[:, 0, :].bitcast(fp32), ALU.subtract))
            nc.vector.tensor_copy(b3hl[64:P, :, :], wide(b3p[64:P, 1, :], 64))
            dve.wait_ge(s_wT, 5)
            for f in range(HB):
                nc.vector.tensor_copy(wfirst[:, f, :, :], bank[2 + f][:, 0:3 * P]).then_inc(s_wc, 1)
            w2hf, w2lf = (w[:, :, :, :].rearrange("p a b m -> p (a b m)") for w in (w2h, w2l))
            step(nc.vector.tensor_copy(w2hf, bank[4][:, :]))
            nc.vector.tensor_tensor(w2lf, bank[4][:, :], w2hf.bitcast(fp32), ALU.subtract).then_inc(s_wc, 1)
            dve.wait_ge(s_wT, 6)
            nc.vector.tensor_copy(w3t[:, :, :], bank[5][:, 0:2 * P]).then_inc(s_wc, 1)

            def program(win):
                CS = 8 if not win else 7

                def sums(g, par, turns):
                    if win:
                        dve.wait_ge(s_tev, g * 2 + 1)
                        dve.wait_ge(s_sdT, g * 2 + 2)
                        xs = sd[:, 0, :, :].rearrange("p k d -> p (k d)")
                        nc.vector.tensor_tensor(sdet[:, 0, :], xs, bank[1][:, :], ALU.add)
                        nc.vector.tensor_tensor(sdet[:, 1, :], xs, bank[1][:, :], ALU.subtract).then_inc(s_sd, 1)
                    else:
                        dve.wait_ge(s_x[par], (turns + 1) * (2 * K * 16))
                        if not (isinstance(g, int) and g == 0):
                            dve.wait_ge(s_sdT, g * 2)
                        nc.vector.tensor_tensor(sd[:, 0, :, :], xg[par][:, 0, :, :], xg[par][:, 1, :, :], ALU.add)
                        nc.vector.tensor_tensor(sd[:, 1, :, :], xg[par][:, 0, :, :], xg[par][:, 1, :, :],
                                                ALU.subtract).then_inc(s_sd, 1)

                def window(g, par):
                    dve.wait_ge(s_xh, g + 1)
                    nc.vector.tensor_tensor(xwl[:, :], xw[par][:, :], xwh[:, :].bitcast(fp32),
                                            ALU.subtract).then_inc(s_xl, 1)

                def select(g, par):
                    if not (isinstance(g, int) and g < 2):
                        dve.wait_ge(s_row, (g - 1) * 2)
                    nc.vector.tensor_copy(sel[par][:, :], ident[0:G, bass.ds(g, 1)].broadcast_to([G, P])
                                          ).then_inc(s_sel, 1)

                def onehot(g):
                    dve.wait_ge(s_roww, g + 1)
                    nc.vector.tensor_tensor(hot[:, :], bank[1][:, :],
                                            wnode[:, bass.ds(g, 1)].broadcast_to([P, GE]),
                                            ALU.is_equal).then_inc(s_hot, 1)

                def compare(g, par, early=False):
                    kept = isinstance(g, int) and g < EARLY
                    if not early:
                        dve.wait_ge(s_sum, (g - 1) * 2)
                    if not kept and not (isinstance(g, int) and g < EARLY + 2):
                        dve.wait_ge(s_adj, (g - (EARLY + 1)) * (K * 16))
                    wide_key = lambda s: keys[:, bass.ds(g, 1), s, :].rearrange(
                        "p g k -> p (g k)").unsqueeze(2).broadcast_to([P, K, P])
                    samedst = samed[:, :, :] if win else same[par][:, 0, :, :]
                    for s, out in ((1, same[par][:, 1, :, :]), (0, samedst)):
                        dve.wait_ge(s_row, g * 2 + (2 - s))
                        nc.vector.tensor_tensor(out, bank[s][:, :].rearrange("p (k j) -> p k j", k=K),
                                                wide_key(s), ALU.is_equal).then_inc(s_cmp, 1)
                        if win and s == 1:
                            nc.vector.tensor_tensor(
                                same[par][:, 0, :, :], column[:, :].unsqueeze(1).broadcast_to([P, K, P]),
                                inwin[:, bass.ds(g, 1), :].rearrange("p g k -> p (g k)").unsqueeze(2)
                                .broadcast_to([P, K, P]), ALU.is_equal)
                    if win:
                        onehot_next(g)
                    dve.wait_ge(s_cmp, g * 2 + 2)
                    tri = lower[:, :].unsqueeze(1).broadcast_to([P, K, P])
                    nc.vector.tensor_tensor(match[:, 3, :, :], samedst, same[par][:, 1, :, :], ALU.mult).then_inc(s_cs, 1)
                    for s in range(1 if win else 0, 2):
                        nc.vector.tensor_tensor(match[:, s, :, :], same[par][:, s, :, :], tri, ALU.mult).then_inc(s_cs, 1)
                    n = CS - 5
                    dve.wait_ge(s_cs, g * CS + n)
                    nc.vector.tensor_tensor(match[:, 2, :, :], match[:, 3, :, :], tri, ALU.mult).then_inc(s_cs, 1)
                    dve.wait_ge(s_cs, g * CS + (n + 1))
                    lo = 1 if win else 0
                    nc.vector.tensor_reduce(found[:, lo:4, :].rearrange("p s k -> p (s k)"),
                                            match[:, lo:4, :, :].rearrange("p s k j -> p (s k) j"),
                                            axis=AX.X, op=ALU.add).then_inc(s_cs, 1)
                    dve.wait_ge(s_cs, g * CS + (n + 2))
                    nc.vector.scalar_tensor_tensor(
                        out=shift[:, lo:3, :].rearrange("p s k -> p (s k)"),
                        in0=found[:, lo:3, :].rearrange("p s k -> p (s k)"), scalar=1.0,
                        in1=away[:, bass.ds(g, 1), lo:3, :].rearrange("p g s k -> p (g s k)"),
                        op0=ALU.min, op1=ALU.mult).then_inc(s_cs, 1)
                    nc.vector.tensor_copy(early_n[:, g, :] if kept else pairs[par][:, :], found[:, 3, :]).then_inc(s_cs, 1)
                    nc.vector.tensor_tensor(npairs[:, :], npairs[:, :], found[:, 3, :], ALU.add).then_inc(s_cs, 1)
                    dve.wait_ge(s_cs, g * CS + (n + 5))
                    if kept:
                        nc.vector.tensor_tensor(early_to[:, g, :], shift[:, 2, :], keys[:, g, 2, :], ALU.add)
                    nc.vector.tensor_tensor(
                        target[par][:, lo:3, :].rearrange("p s k -> p (s k)"),
                        shift[:, lo:3, :].rearrange("p s k -> p (s k)"),
                        keys[:, bass.ds(g, 1), lo:3, :].rearrange("p g s k -> p (g s k)"), ALU.add).then_inc(s_tgt, 1)

                def onehot_next(g):
                    if not (isinstance(g, int) and g == G - 1):
                        onehot(g + 1)

                def ways(g):
                    for f in range(HB):
                        dve.wait_ge(s_pc, g * HB + (f + 1))
                        dve.wait_ge(s_q, g * HB + (f + 1))
                        nc.vector.tensor_tensor(hpre[:, f, 0, :], pb[:, f, :], bank[3 + 2 * f][:, :], ALU.add)
                        nc.vector.tensor_tensor(hpre[:, f, 1, :], pb[:, f, :], bank[3 + 2 * f][:, :],
                                                ALU.subtract).then_inc(s_hp, 1)
                    for f in range(HB):
                        for way in range(2):
                            dve.wait_ge(s_h1, g * 4 + (f * 2 + way + 1))
                            nc.vector.scalar_tensor_tensor(
                                out=h1l[:, way, f, :], in0=hpre[:, f, way, :], scalar=0.0,
                                in1=h1h[:, way, f, :].bitcast(fp32), op0=ALU.max, op1=ALU.subtract).then_inc(s_h1l, 1)

                def deliver(g, par, early=False):
                    if not early:
                        wait_added(dve, g, win)
                    if win:
                        nc.vector.tensor_copy(rowto[par][:, 0, 0:1], wnode[:, bass.ds(g, 1)])
                    else:
                        nc.vector.tensor_copy(rowto[par][:, 0, :], target[par][:, 0, :])
                    nc.vector.tensor_copy(rowto[par][:, 1, :], target[par][:, 1, :]).then_inc(s_rowto, 1)

                def turn(g, par, turns, ahead=2, early=0):
                    if ahead == 2:
                        select(g + 2, par)
                    if ahead:
                        if win:
                            sums(g + 1, 1 - par, 0)
                        compare(g + 1, 1 - par, early=early == 2)
                        ways(g + 1)
                    deliver(g, par, early)
                    if ahead == 2:
                        if win:
                            window(g + 2, par)
                        else:
                            sums(g + 2, par, turns + 1)

                select(0, 0)
                select(1, 1)
                if win:
                    onehot(0)
                    window(0, 0)
                sums(0, 0, 0)
                compare(0, 0, early=True)
                ways(0)
                if win:
                    window(1, 1)
                else:
                    sums(1, 1, 0)
                for g in range(EARLY + 2):
                    turn(g, g % 2, g // 2, early=max(0, 2 - g))
                with dve.Fori(EARLY // 2 + 1, (G - 2) // 2) as i:
                    for par in range(2):
                        turn(i * 2 + par, par, i)
                turn(G - 2, 0, 0, ahead=1)
                turn(G - 1, 1, 0, ahead=0)

            flag = dve.value_load(fits[0:1, 0:1], min_val=0, max_val=1)
            with dve.If(flag > 0):
                program(True)
            with dve.Else():
                program(False)

        @block.tensor
        def _(pe):
            def transpose(out, in_, n):
                return nc.tensor.transpose(out, in_, ident[0:n, 0:n])

            pe.wait_ge(s_const, 9)
            pe.wait_ge(s_rows, 2)
            for s in range(2):
                for k in range(K):
                    last = transpose(bank[s][:, k * G:(k + 1) * G],
                                     rows_f[:, s, :].rearrange("g (p k) -> g k p", k=K)[:, k, :], G)
                last.then_inc(s_wT, 1)
            pe.wait_ge(s_diag, 1)
            nc.tensor.matmul(bank[7][:, 0:G + 1], ones[0:G, :], diag[:, :], start=True, stop=True).then_inc(s_bases, 1)
            pe.wait_ge(s_wload, 6 * 16)
            pe.wait_ge(s_whalf, 1)
            for f in range(HB):
                for j in range(2):
                    transpose(bank[2 + f][:, j * P:(j + 1) * P], whalf[:, f, j, :], P)
                transpose(bank[2 + f][:, 2 * P:3 * P], w1n[:, f, 2 * D:3 * D], P).then_inc(s_wT, 1)
            for f in range(HB):
                for k in range(HB):
                    last = transpose(bank[4][:, (f * HB + k) * P:(f * HB + k + 1) * P],
                                     w2n[:, f, k * P:(k + 1) * P], P)
            last.then_inc(s_wT, 1)
            for k in range(HB):
                last = transpose(bank[5][:, k * P:(k + 1) * P], w3n[:, k * P:(k + 1) * P], P)
            last.then_inc(s_wT, 1)
            pe.wait_ge(s_wc, 6)
            pe.wait_ge(s_fits, 1)

            def program(win):
                EV = 2 if win else 3

                def along(bk, s, par):
                    return nc.tensor.matmul(bank[bk][:, :], sel[par][:, :],
                                            rows_r[:, s, :, :].rearrange("g k p -> g (k p)"), start=True, stop=True)

                def turn_sd(g, par, turns, start=False):
                    if not start:
                        pe.wait_ge(s_cmp, g * 2)
                        pe.wait_ge(s_out, g * 2 - 2)
                    if win:
                        pe.wait_ge(s_x[par], turns * (K * 16) + K * 16)
                        for k in range(K):
                            last = transpose(bank[0][:, k * P:(k + 1) * P], xg[par][:, 0, k, :], P)
                        last.then_inc(s_sdT, 1)
                        pe.wait_ge(s_hot, g + 1)
                        pe.wait_ge(s_xl, g + 1)
                        nc.tensor.matmul(bank[1][:, :], xwh[:, :], hot[:, :], start=True, stop=False)
                        nc.tensor.matmul(bank[1][:, :], xwl[:, :], hot[:, :], start=False, stop=True
                                         ).then_inc(s_sdT, 1)
                        return
                    pe.wait_ge(s_sd, g + 1)
                    for j in range(2):
                        for k in range(K):
                            last = transpose(bank[j][:, k * P:(k + 1) * P], sd[:, j, k, :], P)
                        last.then_inc(s_sdT, 1)

                def turn_e(g, par, turns, extra=0):
                    pe.wait_ge(s_tev, g * EV + 1)
                    pe.wait_ge(s_ef[par], turns * 16 + (16 + extra))
                    for k in range(K):
                        last = transpose(bank[0][:, k * P:(k + 1) * P], ef[par][:, k, :], P)
                    last.then_inc(s_eT, 1)
                    if win:
                        pe.wait_ge(s_sd, g + 1)
                    else:
                        pe.wait_ge(s_tev, g * EV + 2)
                    pe.wait_ge(s_sel, g + 1)
                    along(1, 0, par).then_inc(s_row, 1)

                def turn_dst(g, par, ahead=True):
                    pe.wait_ge(s_tev, g * EV + EV)
                    along(0, 1, par).then_inc(s_row, 1)
                    if win and ahead:
                        pe.wait_ge(s_cmp, g * 2 + 1)
                        pe.wait_ge(s_sel, g + 2)
                        along(1, 1, 1 - par).then_inc(s_roww, 1)

                def first(g, start=False):
                    pe.wait_ge(s_tev, g * EV + EV)
                    if win:
                        pe.wait_ge(s_sd, g + 1)
                    if not start:
                        pe.wait_ge(s_hp, g * HB)
                    for f in range(HB):
                        nc.tensor.matmul(bank[2 + 2 * f][:, :], wfirst[:, f, 0, :], sdet[:, 0, :],
                                         start=True, stop=False)
                        nc.tensor.matmul(bank[2 + 2 * f][:, :], wfirst[:, f, 2, :], sdet[:, 2, :],
                                         start=False, stop=True).then_inc(s_p, 1)
                        nc.tensor.matmul(bank[3 + 2 * f][:, :], wfirst[:, f, 1, :], sdet[:, 1, :],
                                         start=True, stop=True).then_inc(s_q, 1)

                def second(g, n):
                    way, f = divmod(n, HB)
                    if n == 0:
                        pe.wait_ge(s_h1l, g * 4 + 4)
                        if not (isinstance(g, int) and g == 0):
                            pe.wait_ge(s_es, g * 2)
                    if n >= HB:
                        pe.wait_ge(s_h2, g * 4 + (n - 1))
                    parts = [(w, k, h) for k in range(HB) for w, h in ((w2h, h1h), (w2h, h1l), (w2l, h1h))]
                    for q, (w, k, h) in enumerate(parts):
                        last = nc.tensor.matmul(bank[6 + f][:, :], w[:, f, k, :], h[:, way, k, :],
                                                start=(q == 0), stop=(q == len(parts) - 1))
                    last.then_inc(s_l2, 1)

                def third(g):
                    pe.wait_ge(s_h2, g * 4 + 4)
                    for way in range(2):
                        nc.tensor.matmul(bank[6 + way][:, :], ones_r[:, :], b3hl[:, :, :].rearrange("p k d -> p (k d)"),
                                         start=True, stop=False)
                        for t in range(K):
                            for k in range(HB):
                                last = nc.tensor.matmul(bank[6 + way][:, t * P:(t + 1) * P],
                                                        h2[:, way, k, t * P:(t + 1) * P], w3t[:, k, :],
                                                        start=False, stop=(t == K - 1 and k == HB - 1))
                        last.then_inc(s_l3, 1)

                def total(g, par, ahead):
                    pe.wait_ge(s_cmp, (g + 1) * 2 + (2 if ahead else 0))
                    if win and ahead == 2:
                        pe.wait_ge(s_hot, g + 3)
                    for way in range(2):
                        pe.wait_ge(s_es, g * 2 + (way + 1))
                        for t in range(K):
                            whole = win and way == 0
                            last = nc.tensor.matmul(bank[way][:, 0:P] if whole else bank[way][:, t * P:(t + 1) * P],
                                                    same[par][:, way, t, :], es[:, way, t * P:(t + 1) * P],
                                                    start=(t == 0) if whole else True,
                                                    stop=(t == K - 1) if whole else True)
                        last.then_inc(s_sum, 1)

                def turn(g, par, turns, ahead=2, extra=0):
                    if ahead:
                        turn_sd(g + 1, 1 - par, turns)
                    second(g, 0)
                    if ahead:
                        turn_e(g + 1, 1 - par, turns, extra)
                    second(g, 1)
                    if ahead:
                        turn_dst(g + 1, 1 - par, ahead == 2)
                    second(g, 2)
                    second(g, 3)
                    if ahead:
                        first(g + 1)
                    third(g)
                    total(g, par, ahead)

                if win:
                    pe.wait_ge(s_sel, 1)
                    along(1, 1, 0).then_inc(s_roww, 1)
                turn_sd(0, 0, 0, start=True)
                turn_e(0, 0, 0)
                turn_dst(0, 0)
                first(0, start=True)
                turn(0, 0, 0)
                turn(1, 1, 1)
                with pe.Fori(1, (G - 2) // 2) as i:
                    turn(i * 2, 0, i)
                    turn(i * 2 + 1, 1, i + 1)
                turn(G - 2, 0, (G - 2) // 2, ahead=1, extra=16)
                turn(G - 1, 1, 0, ahead=0)

            flag = pe.value_load(fits[0:1, 0:1], min_val=0, max_val=1)
            with pe.If(flag > 0):
                program(True)
            with pe.Else():
                program(False)


def rows_of(x, p0, p1):
    return x[NB * p0:NB * p1, :].rearrange("(p b) d -> p b d", b=NB)


def block_groups():
    return [(b, min(4, NB - b)) for b in range(0, NB, 4)]


def strided(xt, b, nb):
    return xt[:, 0:N].rearrange("d (p b) -> d b p", b=NB)[:, b:b + nb, :]


def layer_norm(nc, dve, act_square, y, out, stat, s_ln, ln0, s_sqrt):
    steps = [ln0]

    def step(ins):
        steps[0] += 1
        ins.then_inc(s_ln, 1)
        dve.wait_ge(s_ln, steps[0])

    mean, var, std, rstd = (stat[0:NP, j, :] for j in range(4))
    wide = lambda v: v.unsqueeze(2).broadcast_to([NP, NB, D])
    step(nc.vector.tensor_reduce(mean, y, axis=AX.X, op=ALU.add))
    step(nc.vector.tensor_scalar(mean, mean, 1.0 / D, None, ALU.mult))
    step(nc.vector.tensor_tensor(y, y, wide(mean), ALU.subtract))
    step(nc.vector.tensor_tensor(act_square, y, y, ALU.mult))
    step(nc.vector.tensor_reduce(var, act_square, axis=AX.X, op=ALU.add))
    step(nc.vector.tensor_scalar(var, var, 1.0 / D, EPS, ALU.mult, ALU.add))
    dve.wait_ge(s_sqrt[0], s_sqrt[1])
    step(nc.vector.reciprocal(rstd, std))
    return nc.vector.tensor_tensor(out, y, wide(rstd), ALU.mult), steps[0]


LN_STEPS = 7


def gru_stage(nc, a, tables, x1, adj_flat, early_to, early_n, npairs, few, s_adj):
    ctx = ExitStack()
    with ctx:
        def sb(name, shape, dt=fp32):
            return ctx.enter_context(nc.sbuf_tensor(name, shape, dt))

        def sem(name):
            return ctx.enter_context(nc.semaphore(name))

        ident = sb("gident", [P, P])
        tab = sb("tab", [P, K + 1, NB * D])
        xn = sb("xn", [P, NB, D])
        wn = sb("wn", [P, LAYERS, 2, 3, D])
        wt = sb("wt", [P, LAYERS, 2, 3, P])
        bias = sb("bias", [P, LAYERS, 2, 3])
        both = sb("both", [P, LAYERS, 3])
        xt = sb("xt", [P, AW])
        aggt = sb("aggt", [P, AW])
        s1t = sb("s1t", [P, AW])
        s2t = sb("s2t", [P, AW])
        gates = sb("gates", [P, 2, 2, CH])
        cand = sb("cand", [P, 2, CH])
        diff = sb("diff", [P, 2, CH])
        stat = sb("gstat", [P, 4, NB])
        ones = sb("gones", [P, P])
        total = sb("gtotal", [1, 1])
        bank = [ctx.enter_context(nc.psum_tensor(f"gbank{i}", [P, 512], fp32)) for i in range(8)]

        s_const = sem("g_const")
        s_zero = sem("g_zero")
        s_load = sem("g_load")
        s_w = sem("g_w")
        s_agg = sem("g_agg")
        s_both = sem("g_both")
        s_T = sem("g_T")
        s_tc = sem("g_tc")
        s_tc2 = sem("g_tc2")
        s_mm = sem("g_mm")
        s_rz = sem("g_rz")
        s_rh = sem("g_rh")
        s_pre = sem("g_pre")
        s_n = sem("g_n")
        s_d = sem("g_d")
        s_cell = sem("g_cell")
        s_np = sem("g_np")
        s_few = sem("g_few")
        s_back = sem("g_back")
        s_res = sem("g_res")
        s_ln = sem("g_ln")
        s_sq = sem("g_sq")
        s_done = sem("g_done")
        groups = block_groups()
        NGR = len(groups)
        NC = AW // CH

        block = ctx.enter_context(nc.Block())

        @block.sync
        def _(sp):
            sp.wait_ge(s_zero, 1)
            sp.dma_start(xn[0:112, :, :], rows_of(a["x"], 0, 112)).then_inc(s_load, 16)
            sp.dma_start(xn[112:NP, :, :], rows_of(a["x"], 112, NP)).then_inc(s_load, 16)
            for k in range(K + 1):
                sp.dma_start(tab[:, k, :], tables[k][0:NR, :].rearrange("(p b) d -> p (b d)", b=NB)
                             ).then_inc(s_load, 16)

        @block.gpsimd
        def _(pool):
            nc.gpsimd.memset(ident[:, :], 0.0).then_inc(s_const, 1)
            pool.wait_ge(s_const, 1)
            nc.gpsimd.affine_select(out=ident[:, :], in_=ident[:, :], compare_op=ALU.not_equal, fill=1.0,
                                    base=0, pattern=[[-1, P]], channel_multiplier=1).then_inc(s_const, 1)
            for t in range(EARLY * K):
                g, k = divmod(t, K)
                pool.wait_ge(s_adj, ((G - EARLY) * K + t) * 16)
                add_pairs(pool, adj_flat, early_to[:, g, k:k + 1], early_n[:, g, k:k + 1], s_adj)
            pool.wait_ge(s_adj, G * K * 16)

        @block.scalar
        def _(act):
            for c in range(LAYERS):
                for m, kind in enumerate(("ih", "hh")):
                    act.dma_start(wn[:, c, m, :, :], a[f"L0_gnn_g{c}_w{kind}"].rearrange("(g p) d -> p g d", p=P)
                                  ).then_inc(s_w, 16)
                    with nc.allow_non_contiguous_dma(reason="384 biases"):
                        act.dma_start(bias[:, c, m, :], a[f"L0_gnn_g{c}_b{kind}"].rearrange("(g p) -> p g", p=P)
                                      ).then_inc(s_w, 16)
            act.wait_ge(s_both, 1)

            def cell(c, n, seq, par):
                if seq >= 2:
                    act.wait_ge(s_cell, seq - 1)
                act.wait_ge(s_mm, seq + 1)
                for j in range(2):
                    nc.scalar.activation(gates[:, par, j, :], bank[4 * par + j][:, 0:CH], ACT.Sigmoid,
                                         bias=both[:, c, j:j + 1]).then_inc(s_rz, 1)
                act.wait_ge(s_pre, seq + 1)
                nc.scalar.activation(cand[:, par, :], cand[:, par, :], ACT.Tanh,
                                     bias=bias[:, c, 0, 2:3]).then_inc(s_n, 1)

            for c in range(LAYERS):
                for n in range(NC):
                    cell(c, n, c * NC + n, (c * NC + n) % 2)
            act.wait_ge(s_ln, LN_STEPS - 1)
            nc.scalar.activation(stat[0:NP, 2, :], stat[0:NP, 1, :], ACT.Sqrt).then_inc(s_sq, 1)

        @block.vector
        def _(dve):
            nc.vector.memset(xn[:, :, :], 0.0).then_inc(s_zero, 1)
            nc.vector.memset(ones[:, :], 1.0).then_inc(s_zero, 1)
            for t in (xt, aggt):
                nc.vector.memset(t[:, N:AW], 0.0)
            dve.wait_ge(s_w, LAYERS * 4 * 16)
            nc.vector.tensor_tensor(both[:, :, :], bias[:, :, 0, :], bias[:, :, 1, :], ALU.add).then_inc(s_both, 1)
            dve.wait_ge(s_np, 1)
            nc.vector.tensor_reduce(total[:, :], bank[7][0:1, 0:K], axis=AX.X, op=ALU.add).then_inc(s_few, 1)
            dve.wait_ge(s_few, 1)
            nc.vector.tensor_scalar(few[:, :], total[:, :], float(G * GE + PAD_SURPLUS + 4095 - G * K), None,
                                    ALU.is_le).then_inc(s_few, 1)
            dve.wait_ge(s_load, (3 + K) * 16)
            nc.vector.tensor_tensor(tab[:, 0, :], tab[:, 0, :], tab[:, 1, :], ALU.add)
            nc.vector.tensor_tensor(tab[:, 2, :], tab[:, 2, :], tab[:, 3, :], ALU.add).then_inc(s_agg, 1)
            dve.wait_ge(s_agg, 1)
            nc.vector.tensor_tensor(tab[:, 0, :], tab[:, 0, :], tab[:, 2, :], ALU.add).then_inc(s_agg, 1)
            dve.wait_ge(s_agg, 2)
            nc.vector.tensor_tensor(tab[:, 0, :], tab[:, 0, :], tab[:, 4, :], ALU.add).then_inc(s_agg, 1)
            for j in range(5):
                lo, hi = 4 * j, min(4 * j + 4, 6 * LAYERS)
                dve.wait_ge(s_T, j + 1)
                nc.vector.tensor_copy(wt[:, :, :, :, :].rearrange("p c m g k -> p (c m g k)")[:, lo * P:hi * P],
                                      bank[j][:, 0:(hi - lo) * P]).then_inc(s_tc, 1)
            for q, dest in enumerate((xt, aggt)):
                for j, (b, nb) in enumerate(groups):
                    dve.wait_ge(s_T, 5 + q * NGR + j + 1)
                    nc.vector.tensor_copy(strided(dest, b, nb),
                                          bank[(5 + q * NGR + j) % 8][:, 0:nb * NP].rearrange("d (b p) -> d b p", b=nb)
                                          ).then_inc(s_tc, 1)

            def cell(c, n, seq, par, h, out):
                cols = slice(n * CH, (n + 1) * CH)
                dve.wait_ge(s_rz, seq * 2 + 2)
                nc.vector.scalar_tensor_tensor(out=diff[:, par, :], in0=bank[4 * par + 3][:, 0:CH],
                                               scalar=bias[:, c, 1, 2:3], in1=gates[:, par, 0, :],
                                               op0=ALU.add, op1=ALU.mult).then_inc(s_rh, 1)
                dve.wait_ge(s_rh, seq + 1)
                nc.vector.tensor_tensor(cand[:, par, :], diff[:, par, :], bank[4 * par + 2][:, 0:CH],
                                        ALU.add).then_inc(s_pre, 1)

            def blend(c, n, seq, par, h, out):
                cols = slice(n * CH, (n + 1) * CH)
                dve.wait_ge(s_n, seq + 1)
                nc.vector.tensor_tensor(diff[:, par, :], h[:, cols], cand[:, par, :], ALU.subtract).then_inc(s_d, 1)
                dve.wait_ge(s_d, seq * 2 + 1)
                nc.vector.tensor_tensor(diff[:, par, :], diff[:, par, :], gates[:, par, 1, :], ALU.mult).then_inc(s_d, 1)
                dve.wait_ge(s_d, seq * 2 + 2)
                nc.vector.tensor_tensor(out[:, cols], diff[:, par, :], cand[:, par, :], ALU.add).then_inc(s_cell, 1)

            todo = [(c, n, c * NC + n, (c * NC + n) % 2, (aggt, s1t, s2t)[c], (s1t, s2t, xt)[c])
                    for c in range(LAYERS) for n in range(NC)]
            for q, t in enumerate(todo):
                cell(*t)
                if q:
                    blend(*todo[q - 1])
            blend(*todo[-1])
            for j, (b, nb) in enumerate(groups):
                dve.wait_ge(s_back, j + 1)
                nc.vector.tensor_tensor(xn[0:NP, b:b + nb, :], xn[0:NP, b:b + nb, :],
                                        bank[j][0:NP, 0:nb * D].rearrange("p (b d) -> p b d", b=nb),
                                        ALU.add).then_inc(s_res, 1)
            dve.wait_ge(s_res, NGR)
            nc.vector.memset(x1[:, :, :], 0.0).then_inc(s_done, 1)
            dve.wait_ge(s_done, 1)
            last, _ = layer_norm(nc, dve, tab[0:NP, 1, :].rearrange("p (b d) -> p b d", b=NB),
                                 xn[0:NP, :, :], x1[0:NP, :, :], stat, s_ln, 0, (s_sq, 1))
            last.then_inc(s_done, 1)

        @block.tensor
        def _(pe):
            pe.wait_ge(s_const, 2)
            pe.wait_ge(s_zero, 2)
            nc.tensor.matmul(bank[7][:, 0:K], ones[:, :], npairs[:, :], start=True, stop=True).then_inc(s_np, 1)
            pe.wait_ge(s_w, LAYERS * 4 * 16)
            flat = wn[:, :, :, :, :].rearrange("p c m g k -> p (c m g k)")
            for j in range(5):
                for q in range(4 * j, min(4 * j + 4, 6 * LAYERS)):
                    last = nc.tensor.transpose(bank[j][:, (q % 4) * P:(q % 4 + 1) * P],
                                               flat[:, q * P:(q + 1) * P], ident[:, :])
                last.then_inc(s_T, 1)
            pe.wait_ge(s_few, 1)
            for q in range(2):
                pe.wait_ge(*((s_load, (3 + K) * 16) if q == 0 else (s_agg, 3)))
                for j, (b, nb) in enumerate(groups):
                    n = 5 + q * NGR + j
                    if n >= 8:
                        pe.wait_ge(s_tc, n - 7)
                    for t in range(nb):
                        src = xn[0:NP, b + t, :] if q == 0 else tab[0:NP, 0, (b + t) * D:(b + t + 1) * D]
                        last = nc.tensor.transpose(bank[n % 8][:, t * NP:(t + 1) * NP], src, ident[0:NP, 0:NP])
                    last.then_inc(s_T, 1)
            pe.wait_ge(s_tc, 5 + 2 * NGR)

            def cell(c, n, seq, par, x, h):
                cols = slice(n * CH, (n + 1) * CH)
                if seq >= 2:
                    pe.wait_ge(s_pre, seq - 1)
                if c:
                    pe.wait_ge(s_cell, (c - 1) * NC + n + 1)
                for j in range(2):
                    nc.tensor.matmul(bank[4 * par + j][:, 0:CH], wt[:, c, 0, j, :], x[:, cols], start=True, stop=False)
                    nc.tensor.matmul(bank[4 * par + j][:, 0:CH], wt[:, c, 1, j, :], h[:, cols], start=False, stop=True)
                nc.tensor.matmul(bank[4 * par + 2][:, 0:CH], wt[:, c, 0, 2, :], x[:, cols], start=True, stop=True)
                nc.tensor.matmul(bank[4 * par + 3][:, 0:CH], wt[:, c, 1, 2, :], h[:, cols],
                                 start=True, stop=True).then_inc(s_mm, 1)

            for c in range(LAYERS):
                for n in range(NC):
                    cell(c, n, c * NC + n, (c * NC + n) % 2, (xt, aggt, s1t)[c], (aggt, s1t, s2t)[c])
            pe.wait_ge(s_cell, LAYERS * NC)
            for j, (b, nb) in enumerate(groups):
                for t in range(nb):
                    last = nc.tensor.transpose(bank[j][0:NP, t * D:(t + 1) * D],
                                               strided(xt, b + t, 1).rearrange("d b p -> d (b p)"), ident[:, :])
                last.then_inc(s_back, 1)


def sum_stage(nc, a, adj_flat, x1, few, out):
    ctx = ExitStack()
    with ctx:
        def sb(name, shape, dt=fp32):
            return ctx.enter_context(nc.sbuf_tensor(name, shape, dt))

        def sem(name):
            return ctx.enter_context(nc.semaphore(name))

        STAY, RING, HEAD = 5, 5, 3
        TURNS = (NB - STAY) // RING
        ident = sb("sident", [P, P])
        sq = sb("sq", [P, NB, D])
        stay = [sb(f"stay{i}", [P, AW], f32r) for i in range(STAY)]
        ring = [sb(f"ring{i}", [P, AW], f32r) for i in range(RING)]
        xb = [sb(f"xb{i}", [P, D]) for i in range(RING)]
        xh = [sb(f"xh{i}", [P, D], f32r) for i in range(RING)]
        xl = [sb(f"xl{i}", [P, D], f32r) for i in range(RING)]
        xn = sb("xn2", [P, NB, D])
        xt = sb("xt2", [P, AW])
        zt = sb("zt", [P, AW])
        w = sb("wl", [P, LAYERS, 2, D])
        bl = sb("bl", [P, LAYERS, 2])
        eps = sb("eps", [P, LAYERS])
        stat = sb("sstat", [P, 4, NB])
        bank = [ctx.enter_context(nc.psum_tensor(f"sbank{i}", [P, 512], fp32)) for i in range(8)]

        s_const = sem("l_const")
        s_w = sem("l_w")
        s_stay = sem("l_stay"), sem("l_stay2")
        s_ring = [sem(f"l_ring{i}") for i in range(RING)]
        s_xb = sem("l_xb")
        s_xl = sem("l_xl")
        s_use = sem("l_use")
        s_T = sem("l_T")
        s_tc = sem("l_tc")
        s_eps = sem("l_eps")
        s_z = sem("l_z")
        s_a = sem("l_a")
        s_h = sem("l_h")
        s_b = sem("l_b")
        s_x = sem("l_x")
        s_back = sem("l_back")
        s_xn = sem("l_xn")
        s_ln = sem("l_ln")
        s_sq = sem("l_sq")
        s_fin = sem("l_fin")
        s_out = sem("l_out")
        groups = block_groups()
        NGR = len(groups)
        NC = AW // CH
        adj = adj_flat[0:NR * AW, :].rearrange("(p b c) o -> p b (c o)", b=NB, c=AW)

        def panels(eng, each):
            for i in range(HEAD):
                each(i, i, i, i, None)
            with eng.Fori(0, TURNS) as t:
                for i in range(RING):
                    each(t * RING + (HEAD + i), t * RING + (STAY + i), i, i, t)
            for i in range(HEAD, STAY):
                each(NB - STAY + i, i, i, i, None)

        block = ctx.enter_context(nc.Block())

        @block.sync
        def _(sp):
            def load(t, i):
                sp.dma_start(ring[i][:, :].bitcast(fp32).unsqueeze(1), adj[:, bass.ds(t * RING + (STAY + i), 1), :]
                             ).then_inc(s_ring[i], 16)

            for i in range(STAY):
                if i == HEAD:
                    for j in range(RING):
                        load(0, j)
                sp.dma_start(stay[i][:, :].bitcast(fp32), adj[:, i, :]).then_inc(s_stay[i >= HEAD], 16)
            for l in range(LAYERS):
                if l:
                    for i in range(RING):
                        sp.wait_ge(s_use, (l - 1) * NB + HEAD + (TURNS - 1) * RING + i + 1)
                        load(0, i)
                with sp.Fori(1, TURNS) as t:
                    for i in range(RING):
                        sp.wait_ge(s_use, t * RING + (l * NB + HEAD - RING + i + 1))
                        load(t, i)
            sp.wait_ge(s_fin, 1)
            for p0, p1 in ((0, 112), (112, NP)):
                sp.dma_start(rows_of(out, p0, p1), xn[p0:p1, :, :]).then_inc(s_out, 16)
            sp.wait_ge(s_out, 32)

        @block.gpsimd
        def _(pool):
            nc.gpsimd.memset(ident[:, :], 0.0).then_inc(s_const, 1)
            pool.wait_ge(s_const, 1)
            nc.gpsimd.affine_select(out=ident[:, :], in_=ident[:, :], compare_op=ALU.not_equal, fill=1.0,
                                    base=0, pattern=[[-1, P]], channel_multiplier=1).then_inc(s_const, 1)

        @block.scalar
        def _(act):
            for m in range(2):
                act.dma_start(w[:, :, m, :], a[f"L1_gnn_W{m + 1}"].rearrange("l k n -> k l n")).then_inc(s_w, 16)
                with nc.allow_non_contiguous_dma(reason="384 biases"):
                    act.dma_start(bl[:, :, m], a[f"L1_gnn_b{m + 1}"].rearrange("l p -> p l")).then_inc(s_w, 16)
            act.dma_start(eps[:, :], a["L1_gnn_eps"].partition_broadcast(P)).then_inc(s_w, 16)
            act.wait_ge(s_w, 5 * 16)
            for l in range(LAYERS):
                src = x1 if l == 0 else xn
                if l:
                    act.wait_ge(s_xn, 1 + l * NGR)

                def block_of_x(nth, b, _, i, t):
                    if l or t is not None or nth >= 2:
                        act.wait_ge(s_use, nth + (l * NB - 1))
                    nc.scalar.copy(xb[i][:, :].unsqueeze(1), src[:, bass.ds(b, 1), :]).then_inc(s_xb, 1)
                    nc.scalar.copy(xh[i][:, :].unsqueeze(1), src[:, bass.ds(b, 1), :]).then_inc(s_xb, 1)

                panels(act, block_of_x)
                for n in range(NC):
                    act.wait_ge(s_a, l * NC + n + 1)
                    nc.scalar.activation(zt[:, n * CH:(n + 1) * CH], bank[n][:, 0:CH], ACT.Relu,
                                         bias=bl[:, l, 0:1]).then_inc(s_h, 1)
                for n in range(NC):
                    act.wait_ge(s_b, l * NC + n + 1)
                    nc.scalar.activation(xt[:, n * CH:(n + 1) * CH], bank[n][:, 0:CH], ACT.Identity,
                                         bias=bl[:, l, 1:2]).then_inc(s_x, 1)
            act.wait_ge(s_ln, LN_STEPS - 1)
            nc.scalar.activation(stat[0:NP, 2, :], stat[0:NP, 1, :], ACT.Sqrt).then_inc(s_sq, 1)

        @block.vector
        def _(dve):
            dve.wait_ge(s_w, 5 * 16)
            nc.vector.tensor_scalar(eps[:, :], eps[:, :], 1.0, None, ALU.add).then_inc(s_eps, 1)
            nc.vector.memset(xt[:, N:AW], 0.0)
            nc.vector.memset(xn[:, :, :], 0.0).then_inc(s_xn, 1)
            for j, (b, nb) in enumerate(groups):
                dve.wait_ge(s_T, j + 1)
                nc.vector.tensor_copy(strided(xt, b, nb), bank[j][:, 0:nb * NP].rearrange("d (b p) -> d b p", b=nb)
                                      ).then_inc(s_tc, 1)
            dve.wait_ge(s_eps, 1)
            dve.wait_ge(s_tc, NGR)
            dve.wait_ge(s_xn, 1)
            for l in range(LAYERS):
                def lower_part(nth, b, _, i, t):
                    dve.wait_ge(s_xb, nth * 2 + (l * NB * 2 + 2))
                    nc.vector.tensor_tensor(xl[i][:, :], xb[i][:, :], xh[i][:, :].bitcast(fp32),
                                            ALU.subtract).then_inc(s_xl, 1)

                panels(dve, lower_part)
                dve.wait_ge(s_use, (l + 1) * NB)
                if l:
                    dve.wait_ge(s_x, l * NC)
                for n in range(NC):
                    cols = slice(n * CH, (n + 1) * CH)
                    nc.vector.scalar_tensor_tensor(out=zt[:, cols], in0=xt[:, cols], scalar=eps[:, l:l + 1],
                                                   in1=bank[n][:, 0:CH], op0=ALU.mult, op1=ALU.add).then_inc(s_z, 1)
                for j, (b, nb) in enumerate(groups):
                    dve.wait_ge(s_back, l * NGR + j + 1)
                    got = bank[j][0:NP, 0:nb * D].rearrange("p (b d) -> p b d", b=nb)
                    if l < LAYERS - 1:
                        nc.vector.tensor_copy(xn[0:NP, b:b + nb, :], got).then_inc(s_xn, 1)
                    else:
                        nc.vector.tensor_tensor(xn[0:NP, b:b + nb, :], x1[0:NP, b:b + nb, :], got,
                                                ALU.add).then_inc(s_xn, 1)
            dve.wait_ge(s_xn, 1 + LAYERS * NGR)
            last, _ = layer_norm(nc, dve, sq[0:NP, :, :],
                                 xn[0:NP, :, :], xn[0:NP, :, :], stat, s_ln, 0, (s_sq, 1))
            last.then_inc(s_fin, 1)

        @block.tensor
        def _(pe):
            pe.wait_ge(s_const, 2)
            for j, (b, nb) in enumerate(groups):
                for t in range(nb):
                    last = nc.tensor.transpose(bank[j][:, t * NP:(t + 1) * NP], x1[0:NP, b + t, :], ident[0:NP, 0:NP])
                last.then_inc(s_T, 1)
            pe.wait_ge(s_tc, NGR)
            pe.wait_ge(s_w, 5 * 16)

            def program(exact):
                for l in range(LAYERS):
                    def product(nth, b, buf, i, t):
                        if t is None:
                            panel = stay[buf]
                            if l == 0:
                                pe.wait_ge(s_stay[buf >= HEAD], (HEAD if buf < HEAD else STAY - HEAD) * 16)
                        else:
                            panel = ring[buf]
                            pe.wait_ge(s_ring[i], t * 16 + (l * TURNS * 16 + 16))
                        pe.wait_ge(s_xl, nth + (l * NB + 1))
                        start = isinstance(nth, int) and nth == 0
                        stop = isinstance(nth, int) and nth == NB - 1
                        parts = (xh[i], xl[i]) if exact else (xb[i],)
                        for q, part in enumerate(parts):
                            for n in range(NC):
                                cols = panel[:, n * CH:(n + 1) * CH]
                                last = nc.tensor.matmul(bank[n][:, 0:CH], part[:, :], cols if exact else cols.bitcast(fp32),
                                                        start=start and q == 0, stop=stop and q == len(parts) - 1)
                        last.then_inc(s_use, 1)

                    if l:
                        pe.wait_ge(s_xn, 1 + l * NGR)
                    panels(pe, product)
                    for n in range(NC):
                        pe.wait_ge(s_z, l * NC + n + 1)
                        nc.tensor.matmul(bank[n][:, 0:CH], w[:, l, 0, :], zt[:, n * CH:(n + 1) * CH],
                                         start=True, stop=True).then_inc(s_a, 1)
                    for n in range(NC):
                        pe.wait_ge(s_h, l * NC + n + 1)
                        nc.tensor.matmul(bank[n][:, 0:CH], w[:, l, 1, :], zt[:, n * CH:(n + 1) * CH],
                                         start=True, stop=True).then_inc(s_b, 1)
                    pe.wait_ge(s_x, (l + 1) * NC)
                    for j, (b, nb) in enumerate(groups):
                        for t in range(nb):
                            last = nc.tensor.transpose(bank[j][0:NP, t * D:(t + 1) * D],
                                                       strided(xt, b + t, 1).rearrange("d b p -> d (b p)"), ident[:, :])
                        last.then_inc(s_back, 1)

            flag = pe.value_load(few[0:1, 0:1], min_val=0, max_val=1)
            with pe.If(flag > 0):
                program(True)
            with pe.Else():
                program(False)


def gnn_kernel(nc, a, out):
    adj_flat = nc.dram_tensor("adj", (ASIZE, 1), fp32, kind="Internal").ap()
    tables = [nc.dram_tensor(f"sums{k}", (AROWS, D), fp32, kind="Internal").ap() for k in range(K + 1)]
    with (
        nc.sbuf_tensor("x1", [P, NB, D], fp32) as x1,
        nc.sbuf_tensor("early_to", [P, EARLY, K], i32) as early_to,
        nc.sbuf_tensor("early_n", [P, EARLY, K], fp32) as early_n,
        nc.sbuf_tensor("npairs", [P, K], fp32) as npairs,
        nc.sbuf_tensor("few", [1, 1], i32) as few,
        nc.semaphore("s_adj") as s_adj,
    ):
        edge_stage(nc, a, adj_flat, tables, early_to, early_n, npairs, s_adj)
        gru_stage(nc, a, tables, x1, adj_flat, early_to, early_n, npairs, few, s_adj)
        sum_stage(nc, a, adj_flat, x1, few, out)


_INS = (["x", "src", "dst", "edge_attr_128"] + [f"L0_gnn_{k}{i}" for i in (1, 2, 3) for k in "wb"]
        + [f"L0_gnn_g{i}_{k}" for i in range(3) for k in ("wih", "whh", "bih", "bhh")]
        + ["L1_gnn_eps", "L1_gnn_W1", "L1_gnn_b1", "L1_gnn_W2", "L1_gnn_b2"])


def kernel(**inputs):
    import numpy as _np
    import concourse.bacc as _bacc
    from concourse import mybir as _mybir
    from concourse.bass_utils import run_bass_kernel_spmd as _run

    nc = _bacc.Bacc("TRN2", target_bir_lowering=False, num_devices=1)
    arrays, aps = {}, {}
    for name in _INS:
        v = _np.ascontiguousarray(inputs[name])
        arrays[f"in_{name}"] = v
        aps[name] = nc.dram_tensor(f"in_{name}", v.shape, _mybir.dt.from_np(v.dtype), kind="ExternalInput").ap()
    out = nc.dram_tensor("out_0", (N, D), fp32, kind="ExternalOutput").ap()
    gnn_kernel(nc, aps, out)
    r = _run(nc, [arrays], core_ids=[0])
    return r.results[0]["out_0"]
```

```python
import numpy as np
import concourse.bass as bass
from concourse import mybir
from contextlib import ExitStack

fp32 = mybir.dt.float32
f32r = mybir.dt.float32r
i32 = mybir.dt.int32
ALU = mybir.AluOpType
ACT = mybir.ActivationFunctionType
AX = mybir.AxisListType

P = 128
D = 128
H = 256
HB = H // P
N = 3125
E = 53125
EARLY = 12
ZG = 12
K = 4
GE = K * P
G = (E + GE - 1) // GE
LAST = E - (G - 1) * GE
PAD = N
AW = 3136
DUMMY = PAD + 1
AROWS = 3328
NR = 3200
PADS = [P - (LAST - k + K - 1) // K for k in range(K)]
PAD_SURPLUS = sum(n * (n - 1) for n in PADS)
ADUMMY = NR * AW
ZW = AROWS * D // P
AZ = -(-(ADUMMY + P) // (P * ZW))
ASIZE = AZ * P * ZW
NP = 125
NB = N // NP
CH = 448
CHUNKS = [(c, min(CH, N - c)) for c in range(0, N, CH)]
LAYERS = 3
RING = 3
TURNS = 6
assert 1 + TURNS * (RING + 1) == NB
EPS = 1e-5


def add_pairs(pool, adj_flat, places, counts, s_adj):
    pool.indirect_dma_start(out=adj_flat, out_offset=bass.IndirectOffsetOnAxis(ap=places, axis=0),
                            in_=counts, in_offset=None, compute_op=ALU.add).then_inc(s_adj, 16)


def edge_stage(nc, a, adj_flat, tables, along, early_to, early_n, npairs, s_adj, later):
    ctx = ExitStack()
    with ctx:
        def sb(name, shape, dt=fp32):
            return ctx.enter_context(nc.sbuf_tensor(name, shape, dt))

        def sem(name):
            return ctx.enter_context(nc.semaphore(name))

        ident = later.ident
        lower = sb("lower", [P, P])
        column = sb("column", [P, P])
        place = sb("place", [P, 1])
        count_i = sb("count_i", [P, P + 4], i32)
        ones = sb("ones", [P, P])
        ones_r = sb("ones_r", [P, P], f32r)
        w1n = sb("w1n", [P, HB, 3 * D])
        w2n = sb("w2n", [P, HB, H])
        w3n = sb("w3n", [P, H])
        whalf = sb("whalf", [P, HB, 2, D])
        w1h = sb("w1h", [P, HB, 3, P], f32r)
        w1l = sb("w1l", [P, HB, 3, P], f32r)
        w2h = sb("w2h", [P, HB, HB, P], f32r)
        w2l = sb("w2l", [P, HB, HB, P], f32r)
        w3t = sb("w3t", [P, HB, P])
        b1c = sb("b1c", [P, HB])
        b2c = sb("b2c", [P, HB])
        b3r = sb("b3r", [P, D])
        b3p = sb("b3p", [P, 3, D])
        b3hl = sb("b3hl", [P, K, D], f32r)
        zero = sb("zero", [P, ZW])
        rows_i = sb("rows_i", [G, 2, GE], i32)
        rows_f = sb("rows_f", [G, 2, GE])
        keys = sb("keys", [P, G, 3, K])
        away = sb("away", [P, G, 3, K])
        dummy = sb("dummyf", [P, 3])
        lows = sb("lows", [G, 4])
        diag = sb("diag", [G, G + 1])
        base_f = sb("base_f", [P, G])
        base_i = sb("base_i", [1, G], i32)
        wnode = sb("wnode", [P, G])
        inwin = sb("inwin", [P, G, K])
        fits = sb("fits", [1, 1], i32)
        gidx = [sb(f"gidx{i}", [P, 2, K], i32) for i in range(3)]
        xg = [sb(f"xg{i}", [P, 2, K, D]) for i in range(2)]
        xw = [sb(f"xw{i}", [P, D]) for i in range(2)]
        ef = [sb(f"ef{i}", [P, K, D]) for i in range(2)]
        rowb = [sb(f"rowb{i}", [P, 3, GE]) for i in range(2)]
        same = [sb(f"same{i}", [P, 3, K, P]) for i in range(2)]
        target = [sb(f"target{i}", [P, 3, K], i32) for i in range(2)]
        pairs = [sb(f"pairs{i}", [P, K]) for i in range(2)]
        rowto = [sb(f"rowto{i}", [P, 2, K], i32) for i in range(2)]
        outb = [sb(f"outb{i}", [P, 2, K, D]) for i in range(2)]
        sd = sb("sd", [P, 2, K, D])
        xwh = sb("xwh", [P, D], f32r)
        xwl = sb("xwl", [P, D], f32r)
        hot = sb("hot", [P, GE], f32r)
        sdh = sb("sdh", [P, 3, GE], f32r)
        sdl = sb("sdl", [P, 3, GE], f32r)
        pb = sb("pb", [P, HB, GE])
        hpre = sb("hpre", [P, HB, 2, GE])
        h1h = sb("h1h", [P, 2, HB, GE], f32r)
        h1l = sb("h1l", [P, 2, HB, GE], f32r)
        h2 = sb("h2", [P, 2, HB, GE])
        es = sb("es", [P, 2, GE])
        match = sb("match", [P, 3, K, P])
        found = sb("found", [P, 4, K])
        shift = sb("shift", [P, 3, K])
        bank = [ctx.enter_context(nc.psum_tensor(f"ebank{i}", [P, 512], fp32)) for i in range(8)]

        s_const = sem("s_const")
        s_wload = sem("s_wload")
        s_iload = sem("s_iload")
        s_zero = sem("s_zero")
        s_ztab = sem("s_ztab")
        s_zadj = sem("s_zadj")
        s_whalf = sem("s_whalf")
        s_wT = sem("s_wT")
        s_wc = sem("s_wc")
        s_rows = sem("s_rows")
        s_along = sem("s_along")
        s_rowb = [sem(f"s_rowb{i}") for i in range(2)]
        s_diag = sem("s_diag")
        s_bases = sem("s_bases")
        s_fits = sem("s_fits")
        s_dve = sem("s_dve")
        s_gidx = [sem(f"s_gidx{i}") for i in range(3)]
        s_ef = [sem(f"s_ef{i}") for i in range(2)]
        s_xw = [sem(f"s_xw{i}") for i in range(2)]
        s_x = [sem(f"s_x{i}") for i in range(2)]
        s_xh = sem("s_xh")
        s_xl = sem("s_xl")
        s_sd = sem("s_sd")
        s_sdT = sem("s_sdT")
        s_eT = sem("s_eT")
        s_xs = sem("s_xs")
        s_hi = sem("s_hi")
        s_lo = sem("s_lo")
        s_hot = sem("s_hot")
        s_cmp = sem("s_cmp")
        s_cs = sem("s_cs")
        s_tgt = sem("s_tgt")
        s_p = sem("s_p")
        s_q = sem("s_q")
        s_pc = sem("s_pc")
        s_hp = sem("s_hp")
        s_h1 = sem("s_h1")
        s_h1l = sem("s_h1l")
        s_l2 = sem("s_l2")
        s_h2 = sem("s_h2")
        s_l3 = sem("s_l3")
        s_es = sem("s_es")
        s_sum = sem("s_sum")
        s_out = sem("s_out")
        s_rowto = sem("s_rowto")
        s_add = [sem(f"s_add{k}") for k in range(K)]
        s_pace = sem("s_pace")

        block = ctx.enter_context(nc.Block())

        def wait_added(eng, g, win):
            for k in range(K):
                eng.wait_ge(s_add[k], (g - 1) * (16 if win and k else 32))

        @block.sync
        def _(sp):
            w1v = a["L0_gnn_w1"].rearrange("(f p) c -> p f c", p=P)
            sp.wait_ge(s_zero, 2)
            nf = (G - 1) // 16 * 16
            for s, name in enumerate(("src", "dst")):
                full = a[name][0:(G - 1) * GE].rearrange("(g e) -> g e", e=GE)
                sp.dma_start(rows_i[0:nf, s, :], full[0:nf, :]).then_inc(s_iload, 16)
                sp.dma_start(rows_i[nf:G - 1, s, :], full[nf:G - 1, :]).then_inc(s_iload, 16)
                sp.dma_start(rows_i[G - 1:G, s, 0:LAST],
                             a[name][(G - 1) * GE:E].rearrange("(g e) -> g e", g=1)).then_inc(s_iload, 16)

            def indices(g, par, s):
                sp.dma_start(gidx[par][:, s, :],
                             a[("src", "dst")[s]][bass.ds(g * GE, GE)].rearrange("(p k) -> p k", k=K)
                             ).then_inc(s_gidx[par], 16)

            def features(g, par):
                sp.dma_start(ef[par][:, :, :],
                             a["edge_attr_128"][bass.ds(g * GE, GE), :].rearrange("(p k) d -> p k d", k=K)
                             ).then_inc(s_ef[par], 16)

            for g in range(2):
                for s in range(2):
                    indices(g, g, s)
                features(g, g)
            sp.dma_start(w1n[:, :, :], w1v).then_inc(s_wload, 16)
            sp.dma_start(w2n[:, :, :], a["L0_gnn_w2"].rearrange("(f p) c -> p f c", p=P)).then_inc(s_wload, 16)
            sp.dma_start(w3n[:, :], a["L0_gnn_w3"]).then_inc(s_wload, 16)
            with nc.allow_non_contiguous_dma(reason="256 biases"):
                sp.dma_start(b1c[:, :], a["L0_gnn_b1"].rearrange("(f p) -> p f", p=P)).then_inc(s_wload, 16)
                sp.dma_start(b2c[:, :], a["L0_gnn_b2"].rearrange("(f p) -> p f", p=P)).then_inc(s_wload, 16)
            sp.dma_start(b3r[:, :], a["L0_gnn_b3"].partition_broadcast(P)).then_inc(s_wload, 16)
            fp, one, base = LAST // K, LAST % K, (G - 1) * GE
            for s, name in enumerate(("src", "dst")):
                sp.dma_start(gidx[2][0:fp, s, :],
                             a[name][base:base + fp * K].rearrange("(p k) -> p k", k=K)).then_inc(s_gidx[2], 16)
                sp.dma_start(gidx[2][fp:fp + 1, s, 0:one],
                             a[name][base + fp * K:E].rearrange("(p k) -> p k", p=1)).then_inc(s_gidx[2], 16)

            sp.wait_ge(s_rows, 3)
            sp.dma_start(along.rearrange("(g e) -> g e", g=G),
                         h2[0:G, :, :, :].rearrange("g w f e -> g (w f e)")[:, 0:3 * GE]).then_inc(s_along, 16)
            sp.wait_ge(s_along, 16)

            def everywhere(g, par):
                sp.dma_start(rowb[par][:, :, :].rearrange("p s e -> p (s e)"),
                             along[bass.ds(g * (3 * GE), 3 * GE)].partition_broadcast(P)).then_inc(s_rowb[par], 16)

            for g in range(2):
                everywhere(g, g)

            def program(win):
                def window(g, par):
                    base = sp.value_load(base_i[0:1, bass.ds(g, 1)], min_val=0, max_val=N - P)
                    sp.dma_start(xw[par][:, :], a["x"][bass.ds(base, P), :]).then_inc(s_xw[par], 16)

                def reload(g, par, turn):
                    sp.wait_ge(s_x[par], turn * ((1 if win else 2) * K * 16))
                    indices(g, par, 0)
                    if not win:
                        indices(g, par, 1)
                    sp.wait_ge(s_eT, g - 1)
                    features(g, par)
                    sp.wait_ge(s_cmp, g - 1)
                    everywhere(g, par)
                    if win:
                        sp.wait_ge(s_xl, g - 1)
                        window(g, par)

                if win:
                    window(0, 0)
                    window(1, 1)
                sp.wait_ge(s_zero, 3)
                for g in range(2):
                    for k in range(g * K // 2, (g + 1) * K // 2):
                        sp.dma_start(tables[k].rearrange("(p r) d -> p (r d)", p=P), zero[:, :]).then_inc(s_ztab, 16)
                    reload(g + 2, g, 1)
                adj_z = adj_flat.rearrange("(s p c) o -> s p (c o)", s=AZ, p=P)
                for g in range(4, 4 + ZG):
                    for s in range((g - 4) * AZ // ZG, (g - 3) * AZ // ZG):
                        sp.dma_start(adj_z[s], zero[:, :]).then_inc(s_zadj, 16)
                    reload(g, g % 2, g // 2)
                later.load(sp, a)
                with sp.Fori((4 + ZG) // 2, (G - 2) // 2) as i:
                    for par in range(2):
                        reload(i * 2 + par, par, i)
                reload(G - 2, 0, (G - 2) // 2)
                sp.wait_ge(s_eT, G - 2)
                sp.dma_start(ef[1][0:fp, :, :],
                             a["edge_attr_128"][base:base + fp * K, :].rearrange("(p k) d -> p k d", k=K)
                             ).then_inc(s_ef[1], 16)
                sp.dma_start(ef[1][fp:fp + 1, 0:one, :],
                             a["edge_attr_128"][base + fp * K:E, :].rearrange("(p k) d -> p k d", p=1)
                             ).then_inc(s_ef[1], 16)
                sp.wait_ge(s_cmp, G - 2)
                everywhere(G - 1, 1)
                if win:
                    sp.wait_ge(s_xl, G - 2)
                    window(G - 1, 1)

            sp.wait_ge(s_fits, 1)
            flag = sp.value_load(fits[0:1, 0:1], min_val=0, max_val=1)
            with sp.If(flag > 0):
                program(True)
            with sp.Else():
                program(False)

        @block.gpsimd
        def _(pool):
            nc.gpsimd.memset(ident[:, :], 0.0).then_inc(s_const, 1)
            nc.gpsimd.memset(lower[:, :], 1.0).then_inc(s_const, 1)
            nc.gpsimd.iota(count_i[:, 0:P], pattern=[[1, P]], base=0, channel_multiplier=0).then_inc(s_const, 1)
            for j, base in enumerate((DUMMY, DUMMY, ADUMMY, 0)):
                nc.gpsimd.iota(count_i[:, P + j:P + j + 1], pattern=[[0, 1]], base=base,
                               channel_multiplier=1).then_inc(s_const, 1)
            nc.gpsimd.memset(later.x1[:, :, :], 0.0).then_inc(later.s_zero, 1)
            pool.wait_ge(s_const, 7)
            nc.gpsimd.affine_select(out=ident[:, :], in_=ident[:, :], compare_op=ALU.not_equal, fill=1.0,
                                    base=0, pattern=[[-1, P]], channel_multiplier=1).then_inc(s_const, 1)
            nc.gpsimd.affine_select(out=lower[:, :], in_=lower[:, :], compare_op=ALU.is_gt, fill=0.0,
                                    base=0, pattern=[[-1, P]], channel_multiplier=1).then_inc(s_const, 1)

            def program(win):
                def gather(par, k, ids):
                    for s in range(1 if win else 2):
                        pool.indirect_dma_start(
                            out=xg[par][:, s, k, :], out_offset=None, in_=a["x"],
                            in_offset=bass.IndirectOffsetOnAxis(ap=ids[:, s, k:k + 1], axis=0)
                        ).then_inc(s_x[par], 16)

                def plain():
                    pool.sem_inc(s_pace, 1)

                def pair(g, par, k):
                    pool.wait_ge(s_adj, ((g - EARLY) * K + k) * 16)
                    plain()
                    add_pairs(pool, adj_flat, target[par][:, 2, k:k + 1], pairs[par][:, k:k + 1], s_adj)

                def add(g, par, way, k):
                    if win:
                        table, before = k, g if k else g * 2 + way
                    else:
                        table, before = k, g * 2 + (way if k < K // 2 else 1 - way)
                    pool.wait_ge(s_add[table], before * 16)
                    plain()
                    pool.indirect_dma_start(
                        out=tables[table],
                        out_offset=bass.IndirectOffsetOnAxis(ap=rowto[par][:, way, k:k + 1], axis=0),
                        in_=outb[par][:, way, k, :], in_offset=None, compute_op=ALU.add).then_inc(s_add[table], 16)

                def turn(j, par, turns, gathers=True, pairing=True, adding=True):
                    if gathers == "last":
                        pool.wait_ge(s_gidx[2], 64)
                    elif gathers and win:
                        pool.wait_ge(s_gidx[par], turns * 16 + 48)
                    elif gathers:
                        pool.wait_ge(s_gidx[par], turns * 32 + 64)
                    if gathers:
                        pool.wait_ge(s_sdT if win else s_sd, j * 2 + 1 if win else j + 1)
                    if adding:
                        pool.wait_ge(s_out, (j - 1) * 2 + 2)
                        pool.wait_ge(s_rowto, j)
                    plain()
                    for k in range(K):
                        if gathers:
                            gather(par, k, gidx[2] if gathers == "last" else gidx[par])
                        if adding and (k == 0 or not win):
                            add(j - 1, 1 - par, 0, k)
                        if adding:
                            add(j - 1, 1 - par, 1, (k + K // 2) % K)
                        if pairing:
                            if k == 0:
                                pool.wait_ge(s_tgt, j + 1)
                            pair(j, par, k)

                for par in range(2):
                    pool.wait_ge(s_gidx[par], 32)
                    for k in range(K):
                        gather(par, k, gidx[par])
                turn(0, 0, 0, pairing=False, adding=False)
                pool.wait_ge(s_ztab, K * 16)
                for j in range(1, EARLY):
                    turn(j, j % 2, j // 2, pairing=False)
                pool.wait_ge(s_zadj, AZ * 16)
                turn(EARLY, 0, EARLY // 2)
                turn(EARLY + 1, 1, EARLY // 2)
                with pool.Fori(EARLY // 2 + 1, (G - 4) // 2) as i:
                    for par in range(2):
                        turn(i * 2 + par, par, i)
                turn(G - 4, 0, (G - 4) // 2)
                turn(G - 3, 1, 0, gathers="last")
                turn(G - 2, 0, 0, gathers=False)
                turn(G - 1, 1, 0, gathers=False)
                turn(G, 0, 0, gathers=False, pairing=False)
                for k in range(K):
                    pool.wait_ge(s_add[k], G * (16 if win and k else 32))

            pool.wait_ge(s_fits, 1)
            flag = pool.value_load(fits[0:1, 0:1], min_val=0, max_val=1)
            with pool.If(flag > 0):
                program(True)
            with pool.Else():
                program(False)
            pool.wait_ge(s_adj, (G - EARLY) * K * 16)

        @block.scalar
        def _(act):
            def program(win):
                def xs_out(g):
                    act.wait_ge(s_sdT, g * 2 + 1)
                    nc.scalar.copy(sd[:, 0, :, :].rearrange("p k d -> p (k d)"), bank[0][:, :]).then_inc(s_xs, 1)

                def upper_sd(g):
                    if win:
                        act.wait_ge(s_sd, g + 1)
                        nc.scalar.copy(sdh[:, 0:2, :], sd[:, :, :, :].rearrange("p s k d -> p s (k d)")).then_inc(s_hi, 1)
                    else:
                        act.wait_ge(s_sdT, g * 2 + 2)
                        nc.scalar.copy(sdh[:, 0, :], bank[0][:, :])
                        nc.scalar.copy(sdh[:, 1, :], bank[1][:, :]).then_inc(s_hi, 1)

                def upper_e(g):
                    act.wait_ge(s_eT, g + 1)
                    nc.scalar.copy(sdh[:, 2, :], bank[0][:, :]).then_inc(s_hi, 1)

                def upper(g, par, turns):
                    act.wait_ge(s_xw[par], turns * 16 + 16)
                    if not (isinstance(g, int) and g == 0):
                        act.wait_ge(s_sdT, g * 2)
                    nc.scalar.copy(xwh[:, :], xw[par][:, :]).then_inc(s_xh, 1)

                def first(g):
                    for f in range(HB):
                        act.wait_ge(s_p, g * HB + (f + 1))
                        nc.scalar.activation(pb[:, f, :], bank[2 + 2 * f][:, :], ACT.Identity,
                                             bias=b1c[:, f:f + 1]).then_inc(s_pc, 1)
                    act.wait_ge(s_l2, g * 4)
                    for f in range(HB):
                        act.wait_ge(s_hp, g * HB + (f + 1))
                        for way in range(2):
                            nc.scalar.activation(h1h[:, way, f, :], hpre[:, f, way, :], ACT.Relu).then_inc(s_h1, 1)

                def second(g, n):
                    way, f = divmod(n, HB)
                    act.wait_ge(s_l2, g * 4 + (n + 1))
                    act.wait_ge(s_l3, g * 2)
                    nc.scalar.activation(h2[:, way, f, :], bank[6 + f][:, :], ACT.Relu,
                                         bias=b2c[:, f:f + 1]).then_inc(s_h2, 1)

                def results(g):
                    for way in range(2):
                        act.wait_ge(s_l3, g * 2 + (way + 1))
                        if way == 0:
                            act.wait_ge(s_sum, g * 2)
                        nc.scalar.copy(es[:, way, :], bank[6 + way][:, :]).then_inc(s_es, 1)

                def sums(g, par, early=False):
                    if not early:
                        wait_added(act, g, win)
                    for way in range(2):
                        act.wait_ge(s_sum, g * 2 + (way + 1))
                        used = D if win and way == 0 else K * D
                        nc.scalar.copy(outb[par][:, way, :, :].rearrange("p k d -> p (k d)")[:, 0:used],
                                       bank[way][:, 0:used]).then_inc(s_out, 1)

                def turn(g, par, turns, ahead=2, early=False):
                    second(g, 0)
                    if ahead:
                        if win:
                            xs_out(g + 1)
                        else:
                            upper_sd(g + 1)
                    second(g, 1)
                    if ahead:
                        upper_e(g + 1)
                        if win:
                            upper_sd(g + 1)
                    for n in range(2, 4):
                        second(g, n)
                    if win and ahead == 2:
                        upper(g + 2, par, turns + 1)
                    if ahead:
                        first(g + 1)
                    results(g)
                    sums(g, par, early)

                if win:
                    upper(0, 0, 0)
                    xs_out(0)
                    upper_e(0)
                    upper_sd(0)
                    upper(1, 1, 0)
                else:
                    upper_sd(0)
                    upper_e(0)
                first(0)
                turn(0, 0, 0, early=True)
                turn(1, 1, 0, early=True)
                with act.Fori(1, (G - 2) // 2) as i:
                    for par in range(2):
                        turn(i * 2 + par, par, i)
                turn(G - 2, 0, 0, ahead=1)
                turn(G - 1, 1, 0, ahead=0)

            act.wait_ge(s_wload, 6 * 16)
            act.wait_ge(s_fits, 1)
            flag = act.value_load(fits[0:1, 0:1], min_val=0, max_val=1)
            with act.If(flag > 0):
                program(True)
            with act.Else():
                program(False)

        @block.vector
        def _(dve):
            steps = [0]

            def step(ins):
                steps[0] += 1
                ins.then_inc(s_dve, 1)
                dve.wait_ge(s_dve, steps[0])

            nc.vector.memset(rows_i[:, :, :], PAD).then_inc(s_zero, 1)
            nc.vector.memset(gidx[2][:, :, :], 0).then_inc(s_zero, 1)
            nc.vector.memset(zero[:, :], 0.0).then_inc(s_zero, 1)
            nc.vector.memset(ones[:, :], 1.0)
            nc.vector.memset(npairs[:, :], 0.0)
            step(nc.vector.memset(sd[:, :, :, :], 1.0))
            nc.vector.tensor_copy(ones_r[:, :], sd[:, 0, 0, :])
            dve.wait_ge(s_const, 9)
            nc.vector.tensor_copy(column[:, :], count_i[:, 0:P])
            nc.vector.tensor_copy(dummy[:, :], count_i[:, P:P + 3])
            step(nc.vector.tensor_copy(place[:, :], count_i[:, P + 3:P + 4]))
            dve.wait_ge(s_iload, 6 * 16)
            step(nc.vector.tensor_copy(rows_f[:, :, :], rows_i[:, :, :]))
            by_tile = lambda s: rows_f[:, s, :].rearrange("g (p k) -> g k p", k=K)
            rows = h2[0:G, :, :, :].rearrange("g w f e -> g (w f) e")
            row = lambda j: rows[:, j, :].rearrange("g (k p) -> g k p", k=K)
            nc.vector.tensor_copy(row(0), by_tile(1)).then_inc(s_rows, 1)
            nc.vector.tensor_copy(row(1), by_tile(0)).then_inc(s_rows, 1)
            nc.vector.scalar_tensor_tensor(out=row(2), in0=by_tile(0), scalar=float(AW), in1=by_tile(1),
                                           op0=ALU.mult, op1=ALU.add).then_inc(s_rows, 1)
            nc.vector.tensor_reduce(lows[:, 0:1], rows_f[:, 1, :], axis=AX.X, op=ALU.min)
            step(nc.vector.scalar_tensor_tensor(out=hpre[0:G, 0, 0, :], in0=rows_f[:, 1, :], scalar=float(N),
                                                in1=rows_f[:, 1, :], op0=ALU.is_lt, op1=ALU.mult))
            nc.vector.tensor_reduce(lows[:, 1:2], hpre[0:G, 0, 0, :], axis=AX.X, op=ALU.max)
            step(nc.vector.tensor_scalar(lows[:, 2:3], lows[:, 0:1], float(N - P), None, ALU.min))
            step(nc.vector.tensor_tensor(lows[:, 3:4], lows[:, 1:2], lows[:, 2:3], ALU.subtract))
            nc.vector.tensor_scalar(diag[:, G:G + 1], lows[:, 3:4], float(P - 1), None, ALU.is_le)
            nc.vector.tensor_scalar(diag[:, 0:G], ident[0:G, 0:G], lows[:, 2:3], None, ALU.mult).then_inc(s_diag, 1)
            dve.wait_ge(s_bases, 1)
            nc.vector.tensor_copy(base_f[:, :], bank[7][:, 0:G])
            nc.vector.tensor_copy(base_i[:, :], bank[7][0:1, 0:G])
            step(nc.vector.tensor_scalar(fits[:, :], bank[7][0:1, G:G + 1], float(G), None, ALU.is_ge))
            nc.vector.tensor_scalar(wnode[:, :], base_f[:, :], place[:, :], None, ALU.add).then_inc(s_fits, 1)
            dve.wait_ge(s_wT, 2)
            for s in range(2):
                nc.vector.tensor_copy(keys[:, :, 1 - s, :], bank[s][:, 0:K * G].rearrange("p (k g) -> p g k", k=K)
                                      ).then_inc(s_wc, 1)
            dve.wait_ge(s_wc, 2)
            step(nc.vector.tensor_tensor(inwin[:, :, :], keys[:, :, 0, :],
                                         base_f[:, :].unsqueeze(2).broadcast_to([P, G, K]), ALU.subtract))
            step(nc.vector.tensor_scalar(away[:, :, 2, :], keys[:, :, 1, :], float(AW), None, ALU.mult))
            step(nc.vector.tensor_tensor(keys[:, :, 2, :], away[:, :, 2, :], keys[:, :, 0, :], ALU.add))
            for j in range(3):
                last = nc.vector.tensor_scalar(away[:, :, j, :], keys[:, :, j, :], -1.0, dummy[:, j:j + 1],
                                               ALU.mult, ALU.add)
            step(last)
            dve.wait_ge(s_wload, 6 * 16)
            for f in range(HB):
                step(nc.vector.tensor_tensor(whalf[:, f, 0, :], w1n[:, f, 0:D], w1n[:, f, D:2 * D], ALU.add))
                step(nc.vector.tensor_tensor(whalf[:, f, 1, :], w1n[:, f, 0:D], w1n[:, f, D:2 * D], ALU.subtract))
            nc.vector.tensor_scalar(whalf[:, :, :, :], whalf[:, :, :, :], 0.5, None, ALU.mult).then_inc(s_whalf, 1)
            step(nc.vector.tensor_scalar(b3p[:, 0, :], b3r[:, :], 1.0 / 64, None, ALU.mult))
            wide = lambda v, n: v.unsqueeze(1).broadcast_to([n, K, D])
            step(nc.vector.tensor_copy(b3hl[:, :, :], wide(b3p[:, 0, :], P)))
            step(nc.vector.tensor_tensor(b3p[:, 1, :], b3p[:, 0, :], b3hl[:, 0, :].bitcast(fp32), ALU.subtract))
            nc.vector.tensor_copy(b3hl[64:P, :, :], wide(b3p[64:P, 1, :], 64))
            dve.wait_ge(s_wT, 5)
            for f in range(HB):
                w1hf, w1lf = (w[:, f, :, :].rearrange("p j m -> p (j m)") for w in (w1h, w1l))
                step(nc.vector.tensor_copy(w1hf, bank[2 + f][:, 0:3 * P]))
                nc.vector.tensor_tensor(w1lf, bank[2 + f][:, 0:3 * P], w1hf.bitcast(fp32), ALU.subtract).then_inc(s_wc, 1)
            w2hf, w2lf = (w[:, :, :, :].rearrange("p a b m -> p (a b m)") for w in (w2h, w2l))
            step(nc.vector.tensor_copy(w2hf, bank[4][:, :]))
            nc.vector.tensor_tensor(w2lf, bank[4][:, :], w2hf.bitcast(fp32), ALU.subtract).then_inc(s_wc, 1)
            dve.wait_ge(s_wT, 6)
            nc.vector.tensor_copy(w3t[:, :, :], bank[5][:, 0:2 * P]).then_inc(s_wc, 1)

            def program(win):
                CS = 6

                def sums(g, par, turns):
                    if win:
                        dve.wait_ge(s_xs, g + 1)
                        dve.wait_ge(s_sdT, g * 2 + 2)
                        xs, d = (sd[:, j, :, :].rearrange("p k d -> p (k d)") for j in range(2))
                        nc.vector.tensor_tensor(d, xs, bank[1][:, :], ALU.subtract)
                        nc.vector.tensor_tensor(xs, xs, bank[1][:, :], ALU.add).then_inc(s_sd, 1)
                    else:
                        dve.wait_ge(s_x[par], (turns + 1) * (2 * K * 16))
                        if not (isinstance(g, int) and g == 0):
                            dve.wait_ge(s_sdT, g * 2)
                        nc.vector.tensor_tensor(sd[:, 0, :, :], xg[par][:, 0, :, :], xg[par][:, 1, :, :], ALU.add)
                        nc.vector.tensor_tensor(sd[:, 1, :, :], xg[par][:, 0, :, :], xg[par][:, 1, :, :],
                                                ALU.subtract).then_inc(s_sd, 1)

                def window(g, par):
                    dve.wait_ge(s_xh, g + 1)
                    nc.vector.tensor_tensor(xwl[:, :], xw[par][:, :], xwh[:, :].bitcast(fp32),
                                            ALU.subtract).then_inc(s_xl, 1)

                def lower_parts(g):
                    dve.wait_ge(s_hi, g * 2 + 1)
                    if win:
                        nc.vector.tensor_tensor(sdl[:, 2, :], bank[0][:, :], sdh[:, 2, :].bitcast(fp32),
                                                ALU.subtract).then_inc(s_lo, 1)
                        dve.wait_ge(s_hi, g * 2 + 2)
                        nc.vector.tensor_tensor(sdl[:, 0:2, :], sd[:, :, :, :].rearrange("p s k d -> p s (k d)"),
                                                sdh[:, 0:2, :].bitcast(fp32), ALU.subtract).then_inc(s_lo, 1)
                    else:
                        nc.vector.tensor_tensor(sdl[:, 0, :], bank[0][:, :], sdh[:, 0, :].bitcast(fp32), ALU.subtract)
                        nc.vector.tensor_tensor(sdl[:, 1, :], bank[1][:, :], sdh[:, 1, :].bitcast(fp32),
                                                ALU.subtract).then_inc(s_lo, 1)
                        dve.wait_ge(s_hi, g * 2 + 2)
                        nc.vector.tensor_tensor(sdl[:, 2, :], bank[0][:, :], sdh[:, 2, :].bitcast(fp32),
                                                ALU.subtract).then_inc(s_lo, 1)

                def onehot(g, par, turns):
                    dve.wait_ge(s_rowb[par], turns * 16 + 16)
                    if not (isinstance(g, int) and g == 0):
                        dve.wait_ge(s_sdT, g * 2)
                    nc.vector.tensor_tensor(hot[:, :], rowb[par][:, 0, :],
                                            wnode[:, bass.ds(g, 1)].broadcast_to([P, GE]),
                                            ALU.is_equal).then_inc(s_hot, 1)

                def windowed(g, par, early=False):
                    if not early:
                        dve.wait_ge(s_sum, (g - 1) * 2)
                    nc.vector.tensor_tensor(
                        same[par][:, 0, :, :], column[:, :].unsqueeze(1).broadcast_to([P, K, P]),
                        inwin[:, bass.ds(g, 1), :].rearrange("p g k -> p (g k)").unsqueeze(2)
                        .broadcast_to([P, K, P]), ALU.is_equal)

                def compare(g, par, turns, early=False):
                    if not early:
                        dve.wait_ge(s_sum, (g - 1) * 2)
                    dve.wait_ge(s_rowb[par], turns * 16 + 16)
                    lo = 1 if win else 0
                    nc.vector.tensor_tensor(
                        same[par][:, lo:3, :, :], rowb[par][:, lo:3, :].rearrange("p s (k j) -> p s k j", k=K),
                        keys[:, bass.ds(g, 1), lo:3, :].rearrange("p g s k -> p (g s) k").unsqueeze(3)
                        .broadcast_to([P, 3 - lo, K, P]), ALU.is_equal).then_inc(s_cmp, 1)

                def places(g, par):
                    kept = isinstance(g, int) and g < EARLY
                    if not kept and not (isinstance(g, int) and g < EARLY + 2):
                        dve.wait_ge(s_adj, (g - (EARLY + 1)) * (K * 16))
                    lo = 1 if win else 0
                    dve.wait_ge(s_cmp, g + 1)
                    nc.vector.tensor_tensor(match[:, lo:3, :, :], same[par][:, lo:3, :, :],
                                            lower[:, :].unsqueeze(1).unsqueeze(1).broadcast_to([P, 3 - lo, K, P]),
                                            ALU.mult).then_inc(s_cs, 1)
                    nc.vector.tensor_reduce(found[:, 3, :], same[par][:, 2, :, :], axis=AX.X, op=ALU.add).then_inc(s_cs, 1)
                    dve.wait_ge(s_cs, g * CS + 1)
                    nc.vector.tensor_reduce(found[:, lo:3, :].rearrange("p s k -> p (s k)"),
                                            match[:, lo:3, :, :].rearrange("p s k j -> p (s k) j"),
                                            axis=AX.X, op=ALU.add).then_inc(s_cs, 1)
                    dve.wait_ge(s_cs, g * CS + 3)
                    nc.vector.scalar_tensor_tensor(
                        out=shift[:, lo:3, :].rearrange("p s k -> p (s k)"),
                        in0=found[:, lo:3, :].rearrange("p s k -> p (s k)"), scalar=1.0,
                        in1=away[:, bass.ds(g, 1), lo:3, :].rearrange("p g s k -> p (g s k)"),
                        op0=ALU.min, op1=ALU.mult).then_inc(s_cs, 1)
                    nc.vector.tensor_copy(early_n[:, g, :] if kept else pairs[par][:, :], found[:, 3, :]).then_inc(s_cs, 1)
                    nc.vector.tensor_tensor(npairs[:, :], npairs[:, :], found[:, 3, :], ALU.add).then_inc(s_cs, 1)
                    dve.wait_ge(s_cs, g * CS + 6)
                    if kept:
                        nc.vector.tensor_tensor(early_to[:, g, :], shift[:, 2, :], keys[:, g, 2, :], ALU.add)
                    nc.vector.tensor_tensor(
                        target[par][:, lo:3, :].rearrange("p s k -> p (s k)"),
                        shift[:, lo:3, :].rearrange("p s k -> p (s k)"),
                        keys[:, bass.ds(g, 1), lo:3, :].rearrange("p g s k -> p (g s k)"), ALU.add).then_inc(s_tgt, 1)

                def ways(g):
                    for f in range(HB):
                        dve.wait_ge(s_pc, g * HB + (f + 1))
                        dve.wait_ge(s_q, g * HB + (f + 1))
                        nc.vector.tensor_tensor(hpre[:, f, 0, :], pb[:, f, :], bank[3 + 2 * f][:, :], ALU.add)
                        nc.vector.tensor_tensor(hpre[:, f, 1, :], pb[:, f, :], bank[3 + 2 * f][:, :],
                                                ALU.subtract).then_inc(s_hp, 1)
                    for f in range(HB):
                        for way in range(2):
                            dve.wait_ge(s_h1, g * 4 + (f * 2 + way + 1))
                            nc.vector.scalar_tensor_tensor(
                                out=h1l[:, way, f, :], in0=hpre[:, f, way, :], scalar=0.0,
                                in1=h1h[:, way, f, :].bitcast(fp32), op0=ALU.max, op1=ALU.subtract).then_inc(s_h1l, 1)

                def deliver(g, par, early=False):
                    if not early:
                        wait_added(dve, g, win)
                    dve.wait_ge(s_tgt, g + 1)
                    if win:
                        nc.vector.tensor_copy(rowto[par][:, 0, 0:1], wnode[:, bass.ds(g, 1)])
                    else:
                        nc.vector.tensor_copy(rowto[par][:, 0, :], target[par][:, 0, :])
                    nc.vector.tensor_copy(rowto[par][:, 1, :], target[par][:, 1, :]).then_inc(s_rowto, 1)

                def turn(g, par, turns, ahead=2, early=0):
                    if ahead:
                        if win:
                            sums(g + 1, 1 - par, 0)
                            windowed(g + 1, 1 - par, early=early == 2)
                        lower_parts(g + 1)
                        compare(g + 1, 1 - par, turns + par, early=early == 2)
                        if win and ahead == 2:
                            onehot(g + 2, par, turns + 1)
                            window(g + 2, par)
                        ways(g + 1)
                    deliver(g, par, early)
                    if ahead:
                        places(g + 1, 1 - par)
                    if ahead == 2 and not win:
                        sums(g + 2, par, turns + 1)

                if win:
                    onehot(0, 0, 0)
                    window(0, 0)
                sums(0, 0, 0)
                if win:
                    windowed(0, 0, early=True)
                lower_parts(0)
                compare(0, 0, 0, early=True)
                if win:
                    onehot(1, 1, 0)
                    window(1, 1)
                ways(0)
                places(0, 0)
                if not win:
                    sums(1, 1, 0)
                for g in range(EARLY + 2):
                    turn(g, g % 2, g // 2, early=max(0, 2 - g))
                with dve.Fori(EARLY // 2 + 1, (G - 2) // 2) as i:
                    for par in range(2):
                        turn(i * 2 + par, par, i)
                turn(G - 2, 0, (G - 2) // 2, ahead=1)
                turn(G - 1, 1, 0, ahead=0)

            flag = dve.value_load(fits[0:1, 0:1], min_val=0, max_val=1)
            with dve.If(flag > 0):
                program(True)
            with dve.Else():
                program(False)

        @block.tensor
        def _(pe):
            def transpose(out, in_, n):
                return nc.tensor.transpose(out, in_, ident[0:n, 0:n])

            pe.wait_ge(s_const, 9)
            pe.wait_ge(s_rows, 1)
            for s in range(2):
                for k in range(K):
                    last = transpose(bank[s][:, k * G:(k + 1) * G],
                                     rows_f[:, s, :].rearrange("g (p k) -> g k p", k=K)[:, k, :], G)
                last.then_inc(s_wT, 1)
            pe.wait_ge(s_diag, 1)
            nc.tensor.matmul(bank[7][:, 0:G + 1], ones[0:G, :], diag[:, :], start=True, stop=True).then_inc(s_bases, 1)
            pe.wait_ge(s_wload, 6 * 16)
            pe.wait_ge(s_whalf, 1)
            for f in range(HB):
                for j in range(2):
                    transpose(bank[2 + f][:, j * P:(j + 1) * P], whalf[:, f, j, :], P)
                transpose(bank[2 + f][:, 2 * P:3 * P], w1n[:, f, 2 * D:3 * D], P).then_inc(s_wT, 1)
            for f in range(HB):
                for k in range(HB):
                    last = transpose(bank[4][:, (f * HB + k) * P:(f * HB + k + 1) * P],
                                     w2n[:, f, k * P:(k + 1) * P], P)
            last.then_inc(s_wT, 1)
            for k in range(HB):
                last = transpose(bank[5][:, k * P:(k + 1) * P], w3n[:, k * P:(k + 1) * P], P)
            last.then_inc(s_wT, 1)
            pe.wait_ge(s_wc, 6)
            pe.wait_ge(s_fits, 1)

            def program(win):
                def turn_sd(g, par, turns, start=False):
                    if not start:
                        pe.wait_ge(s_out, g * 2 - 2)
                    if win:
                        pe.wait_ge(s_x[par], turns * (K * 16) + K * 16)
                        for k in range(K):
                            last = transpose(bank[0][:, k * P:(k + 1) * P], xg[par][:, 0, k, :], P)
                        last.then_inc(s_sdT, 1)
                        pe.wait_ge(s_hot, g + 1)
                        pe.wait_ge(s_xl, g + 1)
                        nc.tensor.matmul(bank[1][:, :], xwh[:, :], hot[:, :], start=True, stop=False)
                        nc.tensor.matmul(bank[1][:, :], xwl[:, :], hot[:, :], start=False, stop=True
                                         ).then_inc(s_sdT, 1)
                        return
                    pe.wait_ge(s_sd, g + 1)
                    for j in range(2):
                        for k in range(K):
                            last = transpose(bank[j][:, k * P:(k + 1) * P], sd[:, j, k, :], P)
                        last.then_inc(s_sdT, 1)

                def turn_e(g, par, turns, extra=0):
                    if win:
                        pe.wait_ge(s_xs, g + 1)
                    else:
                        pe.wait_ge(s_lo, g * 2 + 1)
                    pe.wait_ge(s_ef[par], turns * 16 + (16 + extra))
                    for k in range(K):
                        last = transpose(bank[0][:, k * P:(k + 1) * P], ef[par][:, k, :], P)
                    last.then_inc(s_eT, 1)

                def first(g, start=False):
                    pe.wait_ge(s_lo, g * 2 + (1 if win else 2))
                    if not start:
                        pe.wait_ge(s_hp, g * HB)
                    for f in range(HB):
                        for bk, signal, js in ((2, s_p, (2, 0)), (3, s_q, (1,))):
                            parts = [(w, j, x) for j in js for w, x in ((w1h, sdh), (w1h, sdl), (w1l, sdh))]
                            for q, (w, j, x) in enumerate(parts):
                                if win and f == 0 and j == 0 and q == 3:
                                    pe.wait_ge(s_lo, g * 2 + 2)
                                last = nc.tensor.matmul(bank[bk + 2 * f][:, :], w[:, f, j, :], x[:, j, :],
                                                        start=(q == 0), stop=(q == len(parts) - 1))
                            last.then_inc(signal, 1)

                def second(g, n):
                    way, f = divmod(n, HB)
                    if n == 0:
                        pe.wait_ge(s_h1l, g * 4 + 4)
                        if not (isinstance(g, int) and g == 0):
                            pe.wait_ge(s_es, g * 2)
                    if n >= HB:
                        pe.wait_ge(s_h2, g * 4 + (n - 1))
                    parts = [(w, k, h) for k in range(HB) for w, h in ((w2h, h1h), (w2h, h1l), (w2l, h1h))]
                    for q, (w, k, h) in enumerate(parts):
                        last = nc.tensor.matmul(bank[6 + f][:, :], w[:, f, k, :], h[:, way, k, :],
                                                start=(q == 0), stop=(q == len(parts) - 1))
                    last.then_inc(s_l2, 1)

                def third(g):
                    pe.wait_ge(s_h2, g * 4 + 4)
                    for way in range(2):
                        nc.tensor.matmul(bank[6 + way][:, :], ones_r[:, :], b3hl[:, :, :].rearrange("p k d -> p (k d)"),
                                         start=True, stop=False)
                        for t in range(K):
                            for k in range(HB):
                                last = nc.tensor.matmul(bank[6 + way][:, t * P:(t + 1) * P],
                                                        h2[:, way, k, t * P:(t + 1) * P], w3t[:, k, :],
                                                        start=False, stop=(t == K - 1 and k == HB - 1))
                        last.then_inc(s_l3, 1)

                def total(g, par):
                    pe.wait_ge(s_cmp, g + 1)
                    for way in range(2):
                        pe.wait_ge(s_es, g * 2 + (way + 1))
                        for t in range(K):
                            whole = win and way == 0
                            last = nc.tensor.matmul(bank[way][:, 0:P] if whole else bank[way][:, t * P:(t + 1) * P],
                                                    same[par][:, way, t, :], es[:, way, t * P:(t + 1) * P],
                                                    start=(t == 0) if whole else True,
                                                    stop=(t == K - 1) if whole else True)
                        last.then_inc(s_sum, 1)

                def turn(g, par, turns, ahead=2, extra=0):
                    second(g, 0)
                    if ahead:
                        turn_sd(g + 1, 1 - par, turns)
                    second(g, 1)
                    if ahead:
                        turn_e(g + 1, 1 - par, turns, extra)
                    second(g, 2)
                    second(g, 3)
                    if ahead:
                        first(g + 1)
                    third(g)
                    total(g, par)

                turn_sd(0, 0, 0, start=True)
                turn_e(0, 0, 0)
                first(0, start=True)
                turn(0, 0, 0)
                turn(1, 1, 1)
                with pe.Fori(1, (G - 2) // 2) as i:
                    turn(i * 2, 0, i)
                    turn(i * 2 + 1, 1, i + 1)
                turn(G - 2, 0, (G - 2) // 2, ahead=1, extra=16)
                turn(G - 1, 1, 0, ahead=0)

            flag = pe.value_load(fits[0:1, 0:1], min_val=0, max_val=1)
            with pe.If(flag > 0):
                program(True)
            with pe.Else():
                program(False)


def rows_of(x, p0, p1):
    return x[NB * p0:NB * p1, :].rearrange("(p b) d -> p b d", b=NB)


def block_groups():
    return [(b, min(4, NB - b)) for b in range(0, NB, 4)]


def strided(xt, b, nb):
    return xt[:, 0:N].rearrange("d (p b) -> d b p", b=NB)[:, b:b + nb, :]


LN_HERE = 5


def norm_vector(nc, dve, centred, squares, stat, out, s_sqd, s_ln, s_std, s_norm):
    groups = block_groups()
    total, var, std, rstd = (stat[0:NP, j, :] for j in range(4))
    for j, (b, nb) in enumerate(groups):
        dve.wait_ge(s_sqd, j + 1)
        nc.vector.tensor_reduce(total[:, b:b + nb], squares(j)[0:NP, 0:nb * D].rearrange("p (b d) -> p b d", b=nb),
                                axis=AX.X, op=ALU.add).then_inc(s_ln, 1)
    dve.wait_ge(s_ln, len(groups))
    nc.vector.tensor_scalar(var, total, 1.0 / D, EPS, ALU.mult, ALU.add).then_inc(s_ln, 1)
    dve.wait_ge(s_std, 1)
    nc.vector.reciprocal(rstd, std).then_inc(s_ln, 1)
    dve.wait_ge(s_ln, len(groups) + 2)
    for j, (b, nb) in enumerate(groups[:LN_HERE]):
        nc.vector.tensor_tensor(out[0:NP, b:b + nb, :], centred(j), rstd[:, b:b + nb].unsqueeze(2)
                                .broadcast_to([NP, nb, D]), ALU.mult).then_inc(s_norm, 1)


def norm_scalar(nc, act, centred, squares, stat, out, s_ready, ready0, s_sqd, s_ln, s_std, s_norm):
    groups = block_groups()
    for j, (b, nb) in enumerate(groups):
        act.wait_ge(s_ready, ready0 + j + 1)
        if j >= 2:
            act.wait_ge(s_ln, j - 1)
        nc.scalar.activation(squares(j)[0:NP, 0:nb * D].rearrange("p (b d) -> p b d", b=nb), centred(j),
                             ACT.Square).then_inc(s_sqd, 1)
    act.wait_ge(s_ln, len(groups) + 1)
    nc.scalar.activation(stat[0:NP, 2, :], stat[0:NP, 1, :], ACT.Sqrt).then_inc(s_std, 1)
    act.wait_ge(s_ln, len(groups) + 2)
    for j, (b, nb) in enumerate(groups):
        if j >= LN_HERE:
            for t in range(nb):
                last = nc.scalar.activation(out[0:NP, b + t, :], centred(j)[:, t, :], ACT.Identity,
                                            scale=stat[0:NP, 3, b + t:b + t + 1])
            last.then_inc(s_norm, 1)


class Later:

    def __init__(self, nc, ctx):
        def sb(name, shape):
            return ctx.enter_context(nc.sbuf_tensor(name, shape, fp32))

        self.nc = nc
        self.ident = sb("ident", [P, P])
        self.x1 = sb("x1", [P, NB, D])
        self.wn = sb("wn", [P, LAYERS, 2, 3, D])
        self.bias = sb("bias", [P, LAYERS, 2, 3])
        self.w = sb("wl", [P, LAYERS, 2, D])
        self.bl = sb("bl", [P, LAYERS, 2])
        self.b2r = sb("b2r", [P, LAYERS, D])
        self.eps = sb("eps", [P, LAYERS])
        self.s_zero = ctx.enter_context(nc.semaphore("s_x1zero"))
        self.s_in = ctx.enter_context(nc.semaphore("s_later"))
        self.loads = 0

    def load(self, eng, a):
        self.loads = 0

        def dma(out, in_):
            eng.dma_start(out, in_).then_inc(self.s_in, 16)
            self.loads += 1

        eng.wait_ge(self.s_zero, 1)
        dma(self.x1[0:112, :, :], rows_of(a["x"], 0, 112))
        dma(self.x1[112:NP, :, :], rows_of(a["x"], 112, NP))
        with self.nc.allow_non_contiguous_dma(reason="1500 biases"):
            for c in range(LAYERS):
                for m, kind in enumerate(("ih", "hh")):
                    dma(self.wn[:, c, m, :, :], a[f"L0_gnn_g{c}_w{kind}"].rearrange("(g p) d -> p g d", p=P))
                    dma(self.bias[:, c, m, :], a[f"L0_gnn_g{c}_b{kind}"].rearrange("(g p) -> p g", p=P))
            for m in range(2):
                dma(self.w[:, :, m, :], a[f"L1_gnn_W{m + 1}"].rearrange("l k n -> k l n"))
                dma(self.bl[:, :, m], a[f"L1_gnn_b{m + 1}"].rearrange("l p -> p l"))
        dma(self.b2r[:, :, :].rearrange("p l d -> p (l d)"),
            a["L1_gnn_b2"].rearrange("l d -> (l d)").partition_broadcast(P))
        dma(self.eps[:, :], a["L1_gnn_eps"].partition_broadcast(P))


def panels_of(adj_flat):
    return adj_flat[0:NR * AW, :].rearrange("(p b c) o -> p b (c o)", b=NB, c=AW)


def gru_stage(nc, a, tables, adj_flat, early_to, early_n, npairs, few, s_adj, later, stay, s_stay):
    ctx = ExitStack()
    with ctx:
        def sb(name, shape, dt=fp32):
            return ctx.enter_context(nc.sbuf_tensor(name, shape, dt))

        def sem(name):
            return ctx.enter_context(nc.semaphore(name))

        ident, x1, bias, wn = later.ident, later.x1, later.bias, later.wn
        cen = sb("cen", [P, P])
        tab0 = sb("tab0", [P, NB * D])
        wt = sb("wt", [P, LAYERS, 2, 3, P])
        both = sb("both", [P, LAYERS, 3])
        xt = sb("xt", [P, AW])
        aggt = sb("aggt", [P, AW])
        s1t = sb("s1t", [P, AW])
        s2t = sb("s2t", [P, AW])
        gates = sb("gates", [P, 2, 2, CH])
        cand = sb("cand", [P, 2, CH])
        diff = sb("diff", [P, 2, CH])
        stat = sb("gstat", [P, 4, NB])
        sqr = sb("gsqr", [P, 2, 4 * D])
        ones = sb("gones", [P, P])
        total = sb("gtotal", [1, 1])
        bank = [ctx.enter_context(nc.psum_tensor(f"gbank{i}", [P, 512], fp32)) for i in range(8)]

        s_zero = sem("g_zero")
        s_load = [sem(f"g_load{k}") for k in range(K)]
        s_agg = sem("g_agg")
        s_both = sem("g_both")
        s_T = sem("g_T")
        s_tc = sem("g_tc")
        s_mm = sem("g_mm")
        s_rz = sem("g_rz")
        s_rh = sem("g_rh")
        s_pre = sem("g_pre")
        s_n = sem("g_n")
        s_d = sem("g_d")
        s_last = sem("g_last")
        s_cell = sem("g_cell")
        s_np = sem("g_np")
        s_few = sem("g_few")
        s_back = sem("g_back")
        s_sqd = sem("g_sqd")
        s_ln = sem("g_ln")
        s_std = sem("g_std")
        s_norm = sem("g_norm")
        s_norm2 = sem("g_norm2")
        groups = block_groups()

        def tab(k):
            return tab0[:, :] if k == 0 else stay[:, k - 1, :].bitcast(fp32)

        def centred(j):
            nb = groups[j][1]
            return bank[j][0:NP, 0:nb * D].rearrange("p (b d) -> p b d", b=nb)

        def squares(j):
            return sqr[:, j % 2, 0:groups[j][1] * D]

        NGR = len(groups)
        NC = AW // CH

        block = ctx.enter_context(nc.Block())

        @block.sync
        def _(sp):
            for k in range(K):
                sp.dma_start(tab(k), tables[k][0:NR, :].rearrange("(p b) d -> p (b d)", b=NB)
                             ).then_inc(s_load[k], 16)
            sp.wait_ge(s_adj, G * K * 16)
            sp.wait_ge(s_agg, K - 2 + len(groups))
            for t in range(TURNS):
                sp.dma_start(stay[:, t, 0:AW].bitcast(fp32), panels_of(adj_flat)[:, t * (RING + 1) + 1, :]
                             ).then_inc(s_stay, 16)

        @block.gpsimd
        def _(pool):
            for t in range(EARLY * K):
                g, k = divmod(t, K)
                pool.wait_ge(s_adj, ((G - EARLY) * K + t) * 16)
                add_pairs(pool, adj_flat, early_to[:, g, k:k + 1], early_n[:, g, k:k + 1], s_adj)
            pool.wait_ge(s_adj, G * K * 16)

        @block.scalar
        def _(act):
            act.wait_ge(s_both, 1)

            def cell(c, n, seq, par):
                if seq >= 2:
                    act.wait_ge(s_cell, seq - 1)
                act.wait_ge(s_mm, seq + 1)
                for j in range(2):
                    nc.scalar.activation(gates[:, par, j, :], bank[4 * par + j][:, 0:CH], ACT.Sigmoid,
                                         bias=both[:, c, j:j + 1]).then_inc(s_rz, 1)
                act.wait_ge(s_pre, seq + 1)
                nc.scalar.activation(cand[:, par, :], cand[:, par, :], ACT.Tanh,
                                     bias=bias[:, c, 0, 2:3]).then_inc(s_n, 1)

            for c in range(LAYERS):
                for n in range(NC):
                    cell(c, n, c * NC + n, (c * NC + n) % 2)
            norm_scalar(nc, act, centred, squares, stat, x1, s_back, 0, s_sqd, s_ln, s_std, s_norm2)

        @block.vector
        def _(dve):
            nc.vector.memset(ones[:, :], 1.0).then_inc(s_zero, 1)
            nc.vector.tensor_scalar(cen[:, :], ident[:, :], -1.0 / D, None, ALU.add).then_inc(s_zero, 1)
            for t in (xt, aggt):
                nc.vector.memset(t[:, N:AW], 0.0)
            dve.wait_ge(later.s_in, later.loads * 16)
            nc.vector.tensor_tensor(both[:, :, :], bias[:, :, 0, :], bias[:, :, 1, :], ALU.add).then_inc(s_both, 1)
            dve.wait_ge(s_np, 1)
            nc.vector.tensor_reduce(total[:, :], bank[7][0:1, 0:K], axis=AX.X, op=ALU.add).then_inc(s_few, 1)
            dve.wait_ge(s_few, 1)
            nc.vector.tensor_scalar(few[:, :], total[:, :], float(G * GE + PAD_SURPLUS + 4095 - G * K), None,
                                    ALU.is_le).then_inc(s_few, 1)
            for j in range(5):
                lo, hi = 4 * j, min(4 * j + 4, 6 * LAYERS)
                dve.wait_ge(s_T, j + 1)
                nc.vector.tensor_copy(wt[:, :, :, :, :].rearrange("p c m g k -> p (c m g k)")[:, lo * P:hi * P],
                                      bank[j][:, 0:(hi - lo) * P]).then_inc(s_tc, 1)

            def blocks_out(dest, q):
                for j, (b, nb) in enumerate(groups):
                    dve.wait_ge(s_T, 5 + q * NGR + j + 1)
                    nc.vector.tensor_copy(strided(dest, b, nb),
                                          bank[(5 + q * NGR + j) % 8][:, 0:nb * NP].rearrange("d (b p) -> d b p", b=nb)
                                          ).then_inc(s_tc, 1)

            blocks_out(xt, 0)
            dve.wait_ge(s_load[0], 16)
            for k in range(1, K - 1):
                dve.wait_ge(s_load[k], 16)
                if k > 1:
                    dve.wait_ge(s_agg, k - 1)
                nc.vector.tensor_tensor(tab(0), tab(0), tab(k), ALU.add).then_inc(s_agg, 1)
            dve.wait_ge(s_load[K - 1], 16)
            dve.wait_ge(s_agg, K - 2)
            for b, nb in groups:
                cols = slice(b * D, (b + nb) * D)
                nc.vector.tensor_tensor(tab(0)[:, cols], tab(0)[:, cols], tab(K - 1)[:, cols], ALU.add).then_inc(s_agg, 1)
            blocks_out(aggt, 1)

            def cell(c, n, seq, par, h, out):
                cols = slice(n * CH, (n + 1) * CH)
                dve.wait_ge(s_rz, seq * 2 + 2)
                nc.vector.scalar_tensor_tensor(out=diff[:, par, :], in0=bank[4 * par + 3][:, 0:CH],
                                               scalar=bias[:, c, 1, 2:3], in1=gates[:, par, 0, :],
                                               op0=ALU.add, op1=ALU.mult).then_inc(s_rh, 1)
                dve.wait_ge(s_rh, seq + 1)
                nc.vector.tensor_tensor(cand[:, par, :], diff[:, par, :], bank[4 * par + 2][:, 0:CH],
                                        ALU.add).then_inc(s_pre, 1)

            def blend(c, n, seq, par, h, out):
                cols = slice(n * CH, (n + 1) * CH)
                dve.wait_ge(s_n, seq + 1)
                nc.vector.tensor_tensor(diff[:, par, :], h[:, cols], cand[:, par, :], ALU.subtract).then_inc(s_d, 1)
                dve.wait_ge(s_d, seq * 2 + 1)
                nc.vector.tensor_tensor(diff[:, par, :], diff[:, par, :], gates[:, par, 1, :], ALU.mult).then_inc(s_d, 1)
                dve.wait_ge(s_d, seq * 2 + 2)
                if c < LAYERS - 1:
                    nc.vector.tensor_tensor(out[:, cols], diff[:, par, :], cand[:, par, :], ALU.add).then_inc(s_cell, 1)
                else:
                    nc.vector.tensor_tensor(diff[:, par, :], diff[:, par, :], cand[:, par, :], ALU.add).then_inc(s_last, 1)
                    dve.wait_ge(s_last, n + 1)
                    nc.vector.tensor_tensor(out[:, cols], diff[:, par, :], xt[:, cols], ALU.add).then_inc(s_cell, 1)

            todo = [(c, n, c * NC + n, (c * NC + n) % 2, (aggt, s1t, s2t)[c], (s1t, s2t, aggt)[c])
                    for c in range(LAYERS) for n in range(NC)]
            for q, t in enumerate(todo):
                cell(*t)
                if q:
                    blend(*todo[q - 1])
            blend(*todo[-1])
            norm_vector(nc, dve, centred, squares, stat, x1, s_sqd, s_ln, s_std, s_norm)
            dve.wait_ge(s_norm, LN_HERE)

        @block.tensor
        def _(pe):
            pe.wait_ge(s_zero, 1)
            nc.tensor.matmul(bank[7][:, 0:K], ones[:, :], npairs[:, :], start=True, stop=True).then_inc(s_np, 1)
            pe.wait_ge(later.s_in, later.loads * 16)
            flat = wn[:, :, :, :, :].rearrange("p c m g k -> p (c m g k)")
            for j in range(5):
                for q in range(4 * j, min(4 * j + 4, 6 * LAYERS)):
                    last = nc.tensor.transpose(bank[j][:, (q % 4) * P:(q % 4 + 1) * P],
                                               flat[:, q * P:(q + 1) * P], ident[:, :])
                last.then_inc(s_T, 1)
            pe.wait_ge(s_few, 1)
            for q in range(2):
                for j, (b, nb) in enumerate(groups):
                    if q:
                        pe.wait_ge(s_agg, K - 1 + j)
                    n = 5 + q * NGR + j
                    if n >= 8:
                        pe.wait_ge(s_tc, n - 7)
                    for t in range(nb):
                        src = x1[0:NP, b + t, :] if q == 0 else tab0[0:NP, (b + t) * D:(b + t + 1) * D]
                        last = nc.tensor.transpose(bank[n % 8][:, t * NP:(t + 1) * NP], src, ident[0:NP, 0:NP])
                    last.then_inc(s_T, 1)
            pe.wait_ge(s_tc, 5 + 2 * NGR)

            def cell(c, n, seq, par, x, h):
                cols = slice(n * CH, (n + 1) * CH)
                if seq >= 2:
                    pe.wait_ge(s_pre, seq - 1)
                if c:
                    pe.wait_ge(s_cell, (c - 1) * NC + n + 1)
                for j in range(2):
                    nc.tensor.matmul(bank[4 * par + j][:, 0:CH], wt[:, c, 0, j, :], x[:, cols], start=True, stop=False)
                    nc.tensor.matmul(bank[4 * par + j][:, 0:CH], wt[:, c, 1, j, :], h[:, cols], start=False, stop=True)
                nc.tensor.matmul(bank[4 * par + 2][:, 0:CH], wt[:, c, 0, 2, :], x[:, cols], start=True, stop=True)
                nc.tensor.matmul(bank[4 * par + 3][:, 0:CH], wt[:, c, 1, 2, :], h[:, cols],
                                 start=True, stop=True).then_inc(s_mm, 1)

            for c in range(LAYERS):
                for n in range(NC):
                    cell(c, n, c * NC + n, (c * NC + n) % 2, (xt, aggt, s1t)[c], (aggt, s1t, s2t)[c])
            pe.wait_ge(s_cell, LAYERS * NC)
            pe.wait_ge(s_zero, 2)
            for j, (b, nb) in enumerate(groups):
                for t in range(nb):
                    last = nc.tensor.matmul(bank[j][0:NP, t * D:(t + 1) * D],
                                            strided(aggt, b + t, 1).rearrange("d b p -> d (b p)"), cen[:, :],
                                            start=True, stop=True)
                last.then_inc(s_back, 1)


def sum_stage(nc, a, adj_flat, few, out, later, stay, s_stay):
    ctx = ExitStack()
    with ctx:
        def sb(name, shape, dt=fp32):
            return ctx.enter_context(nc.sbuf_tensor(name, shape, dt))

        def sem(name):
            return ctx.enter_context(nc.semaphore(name))

        ident, x1, w, bl, b2r, eps = later.ident, later.x1, later.w, later.bl, later.b2r, later.eps
        last_panel = sb("last_panel", [P, AW], f32r)
        ring = [sb(f"ring{i}", [P, AW], f32r) for i in range(RING)]
        xb = [sb(f"xb{i}", [P, D]) for i in range(RING + 2)]
        xh = [sb(f"xh{i}", [P, D], f32r) for i in range(RING + 2)]
        xl = [sb(f"xl{i}", [P, D], f32r) for i in range(RING + 2)]
        xn = sb("xn2", [P, NB, D])
        zt = sb("zt", [P, AW])
        wz = sb("wz", [P, LAYERS, D])
        bz = sb("bz", [P, LAYERS])
        w2c = sb("w2c", [P, D])
        mean = sb("mean", [P, 2, NB])
        stat = sb("sstat", [P, 4, NB])
        sqr = sb("ssqr", [P, 2, 4 * D])
        bank = [ctx.enter_context(nc.psum_tensor(f"sbank{i}", [P, 512], fp32)) for i in range(8)]

        s_last = sem("l_last")
        s_ring = [sem(f"l_ring{i}") for i in range(RING)]
        s_xb = sem("l_xb")
        s_xl = sem("l_xl")
        s_use = sem("l_use")
        s_T = sem("l_T")
        s_tc = sem("l_tc")
        s_wz = sem("l_wz")
        s_z = sem("l_z")
        s_a = sem("l_a")
        s_h = sem("l_h")
        s_back = sem("l_back")
        s_zero = sem("l_zero")
        s_xn = sem("l_xn")
        s_res = sem("l_res")
        s_sqd = sem("l_sqd")
        s_ln = sem("l_ln")
        s_std = sem("l_std")
        s_norm = sem("l_norm")
        s_norm2 = sem("l_norm2")
        s_out = sem("l_out")
        CREDIT = RING + 1
        groups = block_groups()
        NGR = len(groups)
        NC = AW // CH
        adj = panels_of(adj_flat)

        def panels(eng, each):
            with eng.Fori(0, TURNS) as t:
                for i, j in enumerate((0, None) + tuple(range(1, RING))):
                    each(t * (RING + 1) + i, j, i, t)
            each(NB - 1, None, RING + 1, None)

        def centred(j):
            b, nb = groups[j]
            return xn[0:NP, b:b + nb, :]

        def squares(j):
            return sqr[:, j % 2, 0:groups[j][1] * D]

        block = ctx.enter_context(nc.Block())

        @block.sync
        def _(sp):
            def load(t, i):
                sp.dma_start(ring[i][:, :].bitcast(fp32).unsqueeze(1),
                             adj[:, bass.ds(t * (RING + 1) + (0 if i == 0 else i + 1), 1), :]).then_inc(s_ring[i], 16)

            for l in range(LAYERS):
                for i in range(RING):
                    if l:
                        sp.wait_ge(s_use, CREDIT + (l - 1) * NB + (TURNS - 1) * (RING + 1) + (0 if i == 0 else i + 1) + 1)
                    load(0, i)
                if l == 0:
                    sp.dma_start(last_panel[:, :].bitcast(fp32), adj[:, NB - 1, :]).then_inc(s_last, 16)
                with sp.Fori(1, TURNS) as t:
                    for i in range(RING):
                        sp.wait_ge(s_use, t * (RING + 1) + (CREDIT + l * NB - (RING + 1) + (0 if i == 0 else i + 1) + 1))
                        load(t, i)
            for (b0, b1), signal, n in (((0, 12), s_norm, 3), ((12, 20), s_norm, LN_HERE), ((20, NB), s_norm2, NGR - LN_HERE)):
                sp.wait_ge(signal, n)
                for p0, p1 in ((0, 112), (112, NP)):
                    sp.dma_start(rows_of(out, p0, p1)[:, b0:b1, :], xn[p0:p1, b0:b1, :]).then_inc(s_out, 16)
            sp.wait_ge(s_out, 6 * 16)

        @block.gpsimd
        def _(pool):
            nc.gpsimd.memset(xn[:, :, :], 0.0).then_inc(s_zero, 1)

        @block.scalar
        def _(act):
            for l in range(LAYERS):
                src = x1 if l == 0 else xn

                def block_of_x(nth, j, i, t):
                    if l:
                        act.wait_ge(s_xn, l * NGR)
                    act.wait_ge(s_use, nth + (l * NB + 1))
                    nc.scalar.copy(xb[i][:, :].unsqueeze(1), src[:, bass.ds(nth, 1), :]).then_inc(s_xb, 1)
                    nc.scalar.copy(xh[i][:, :].unsqueeze(1), src[:, bass.ds(nth, 1), :]).then_inc(s_xb, 1)

                panels(act, block_of_x)
                for n in range(NC):
                    act.wait_ge(s_a, l * NC + n + 1)
                    nc.scalar.activation(zt[:, n * CH:(n + 1) * CH], bank[n][:, 0:CH], ACT.Relu,
                                         bias=bl[:, l, 0:1]).then_inc(s_h, 1)
            norm_scalar(nc, act, centred, squares, stat, xn, s_xn, (LAYERS - 1) * NGR, s_sqd, s_ln, s_std, s_norm2)

        @block.vector
        def _(dve):
            steps = [0]

            def step(ins):
                steps[0] += 1
                ins.then_inc(s_wz, 1)
                dve.wait_ge(s_wz, steps[0])

            step(nc.vector.tensor_scalar(eps[:, :], eps[:, :], 1.0, None, ALU.add))
            step(nc.vector.tensor_scalar(wz[:, 0, :], ident[:, :], eps[:, 0:1], None, ALU.mult))
            nc.vector.memset(zt[:, N:AW], 0.0)
            for j, (b, nb) in enumerate(groups):
                dve.wait_ge(s_T, j + 1)
                nc.vector.tensor_copy(strided(zt, b, nb), bank[j][:, 0:nb * NP].rearrange("d (b p) -> d b p", b=nb)
                                      ).then_inc(s_tc, 1)
            for l in range(1, LAYERS):
                step(nc.vector.tensor_scalar(wz[:, l, :], w[:, l - 1, 1, :], eps[:, l:l + 1], None, ALU.mult))
                step(nc.vector.tensor_scalar(bz[:, l:l + 1], bl[:, l - 1, 1:2], eps[:, l:l + 1], None, ALU.mult))
            step(nc.vector.memset(bz[:, 0:1], 0.0))
            step(nc.vector.tensor_reduce(mean[:, 0, 0:1], w[:, LAYERS - 1, 1, :], axis=AX.X, op=ALU.add))
            step(nc.vector.tensor_scalar(mean[:, 0, 0:1], mean[:, 0, 0:1], -1.0 / D, None, ALU.mult))
            step(nc.vector.tensor_scalar(w2c[:, :], w[:, LAYERS - 1, 1, :], mean[:, 0, 0:1], None, ALU.add))
            for l in range(LAYERS):
                def lower_part(nth, j, i, t):
                    dve.wait_ge(s_xb, nth * 2 + (l * NB * 2 + 2))
                    nc.vector.tensor_tensor(xl[i][:, :], xb[i][:, :], xh[i][:, :].bitcast(fp32),
                                            ALU.subtract).then_inc(s_xl, 1)

                panels(dve, lower_part)
                if l == LAYERS - 1:
                    y = x1[0:NP, :, :]
                    wide = lambda v: v.unsqueeze(2).broadcast_to([NP, NB, D])
                    nc.vector.tensor_tensor(y, y, b2r[0:NP, l, :].unsqueeze(1).broadcast_to([NP, NB, D]),
                                            ALU.add).then_inc(s_res, 1)
                    dve.wait_ge(s_res, 1)
                    nc.vector.tensor_reduce(mean[0:NP, 0, :], y, axis=AX.X, op=ALU.add).then_inc(s_res, 1)
                    dve.wait_ge(s_res, 2)
                    nc.vector.tensor_scalar(mean[0:NP, 1, :], mean[0:NP, 0, :], 1.0 / D, None, ALU.mult).then_inc(s_res, 1)
                    dve.wait_ge(s_res, 3)
                    nc.vector.tensor_tensor(y, y, wide(mean[0:NP, 1, :]), ALU.subtract).then_inc(s_res, 1)
                    dve.wait_ge(s_res, 4)
                dve.wait_ge(s_use, CREDIT + (l + 1) * NB)
                for n in range(NC):
                    nc.vector.tensor_scalar(zt[:, n * CH:(n + 1) * CH], bank[n][:, 0:CH], bz[:, l:l + 1], None,
                                            ALU.add).then_inc(s_z, 1)
                if l == 0:
                    dve.wait_ge(s_zero, 1)
                for j, (b, nb) in enumerate(groups):
                    dve.wait_ge(s_back, l * NGR + j + 1)
                    got = bank[j][0:NP, 0:nb * D].rearrange("p (b d) -> p b d", b=nb)
                    more = (b2r[0:NP, l, :].unsqueeze(1).broadcast_to([NP, nb, D]) if l < LAYERS - 1
                            else x1[0:NP, b:b + nb, :])
                    nc.vector.tensor_tensor(xn[0:NP, b:b + nb, :], got, more, ALU.add).then_inc(s_xn, 1)
            norm_vector(nc, dve, centred, squares, stat, xn, s_sqd, s_ln, s_std, s_norm)

        @block.tensor
        def _(pe):
            for j, (b, nb) in enumerate(groups):
                for t in range(nb):
                    last = nc.tensor.transpose(bank[j][:, t * NP:(t + 1) * NP], x1[0:NP, b + t, :], ident[0:NP, 0:NP])
                last.then_inc(s_T, 1)
            pe.sem_inc(s_use, CREDIT)
            pe.wait_ge(s_tc, NGR)
            pe.wait_ge(s_wz, 2)

            def program(exact):
                for l in range(LAYERS):
                    def product(nth, j, i, t):
                        if t is None:
                            cut = lambda cols: last_panel[:, cols]
                            pe.wait_ge(s_last, 16)
                        elif j is None:
                            cut = lambda cols: stay[:, bass.ds(t, 1), cols].rearrange("p t c -> p (t c)")
                            if l == 0:
                                pe.wait_ge(s_stay, TURNS * 16)
                        else:
                            cut = lambda cols: ring[j][:, cols]
                            pe.wait_ge(s_ring[j], t * 16 + (l * TURNS * 16 + 16))
                        pe.wait_ge(s_xl, nth + (l * NB + 1))
                        parts = (xh[i], xl[i]) if exact else (xb[i],)
                        stop = isinstance(nth, int) and nth == NB - 1
                        for q, part in enumerate(parts):
                            for n in range(NC):
                                cols = cut(slice(n * CH, (n + 1) * CH))
                                last = nc.tensor.matmul(bank[n][:, 0:CH], part[:, :], cols if exact else cols.bitcast(fp32),
                                                        start=False, stop=stop and q == len(parts) - 1)
                        last.then_inc(s_use, 1)

                    for n in range(NC):
                        if l:
                            pe.wait_ge(s_xn, (l - 1) * NGR + n + 1)
                            if n == 0:
                                pe.wait_ge(s_wz, 2 + 2 * (LAYERS - 1))
                        nc.tensor.matmul(bank[n][:, 0:CH], wz[:, l, :], zt[:, n * CH:(n + 1) * CH],
                                         start=True, stop=False)
                    panels(pe, product)
                    for n in range(NC):
                        pe.wait_ge(s_z, l * NC + n + 1)
                        nc.tensor.matmul(bank[n][:, 0:CH], w[:, l, 0, :], zt[:, n * CH:(n + 1) * CH],
                                         start=True, stop=True).then_inc(s_a, 1)
                    pe.wait_ge(s_h, (l + 1) * NC)
                    if l == LAYERS - 1:
                        pe.wait_ge(s_wz, 6 + 2 * (LAYERS - 1))
                    w2 = w2c[:, :] if l == LAYERS - 1 else w[:, l, 1, :]
                    for j, (b, nb) in enumerate(groups):
                        for t in range(nb):
                            last = nc.tensor.matmul(bank[j][0:NP, t * D:(t + 1) * D],
                                                    strided(zt, b + t, 1).rearrange("d b p -> d (b p)"), w2,
                                                    start=True, stop=True)
                        last.then_inc(s_back, 1)

            flag = pe.value_load(few[0:1, 0:1], min_val=0, max_val=1)
            with pe.If(flag > 0):
                program(True)
            with pe.Else():
                program(False)


def gnn_kernel(nc, a, out):
    adj_flat = nc.dram_tensor("adj", (ASIZE, 1), fp32, kind="Internal").ap()
    along = nc.dram_tensor("along", (G * 3 * GE,), fp32, kind="Internal").ap()
    tables = [nc.dram_tensor(f"sums{k}", (AROWS, D), fp32, kind="Internal").ap() for k in range(K)]
    with (
        nc.sbuf_tensor("early_to", [P, EARLY, K], i32) as early_to,
        nc.sbuf_tensor("early_n", [P, EARLY, K], fp32) as early_n,
        nc.sbuf_tensor("npairs", [P, K], fp32) as npairs,
        nc.sbuf_tensor("few", [1, 1], i32) as few,
        nc.semaphore("s_adj") as s_adj,
        ExitStack() as ctx,
    ):
        later = Later(nc, ctx)
        s_stay = ctx.enter_context(nc.semaphore("s_stay"))
        edge_stage(nc, a, adj_flat, tables, along, early_to, early_n, npairs, s_adj, later)
        stay = ctx.enter_context(nc.sbuf_tensor("stay", [P, TURNS, NB * D], f32r))
        gru_stage(nc, a, tables, adj_flat, early_to, early_n, npairs, few, s_adj, later, stay, s_stay)
        sum_stage(nc, a, adj_flat, few, out, later, stay, s_stay)


_INS = (["x", "src", "dst", "edge_attr_128"] + [f"L0_gnn_{k}{i}" for i in (1, 2, 3) for k in "wb"]
        + [f"L0_gnn_g{i}_{k}" for i in range(3) for k in ("wih", "whh", "bih", "bhh")]
        + ["L1_gnn_eps", "L1_gnn_W1", "L1_gnn_b1", "L1_gnn_W2", "L1_gnn_b2"])


def kernel(**inputs):
    import numpy as _np
    import concourse.bacc as _bacc
    from concourse import mybir as _mybir
    from concourse.bass_utils import run_bass_kernel_spmd as _run

    nc = _bacc.Bacc("TRN2", target_bir_lowering=False, num_devices=1)
    arrays, aps = {}, {}
    for name in _INS:
        v = _np.ascontiguousarray(inputs[name])
        arrays[f"in_{name}"] = v
        aps[name] = nc.dram_tensor(f"in_{name}", v.shape, _mybir.dt.from_np(v.dtype), kind="ExternalInput").ap()
    out = nc.dram_tensor("out_0", (N, D), fp32, kind="ExternalOutput").ap()
    gnn_kernel(nc, aps, out)
    r = _run(nc, [arrays], core_ids=[0])
    return r.results[0]["out_0"]
```
